# Optimizing a Trainium2 kernel written in Bass

```python
import numpy as np
import jax
import jax.numpy as jnp

def _softmax(x, axis=-1):
    return jax.nn.softmax(x, axis=axis)

def _gelu(x):
    return jax.nn.gelu(x, approximate=True)

def _silu(x):
    return jax.nn.silu(x)

def _sigmoid(x):
    return jax.nn.sigmoid(x)

def _layernorm(x, axis=-1, eps=1e-05):
    m = jnp.mean(x, axis=axis, keepdims=True)
    v = jnp.var(x, axis=axis, keepdims=True)
    return (x - m) / jnp.sqrt(v + eps)

def _scatter_add(tgt, idx, src, axis=0):
    return tgt.at[idx].add(src)

def _segment_sum(src, seg, n):
    return jax.ops.segment_sum(src, seg, n)
kernel_name = 'mk_flamingo_gated_d2_seqx_r8_3073ac'

def setup_inputs(seed: int=0):
    np.random.seed(seed)
    _w = jnp.asarray

    def _rec_inputs():
        import jax
        import jax.numpy as jnp
        _rk = jax.random.key(seed)
        x = 4.136e-05 + 0.9999 * jax.random.normal(jax.random.fold_in(_rk, 1), (4, 256, 256), jnp.float32)
        _lenS = 256 - jax.random.randint(jax.random.fold_in(_rk, 7), (4,), 0, max(1, 256 // 4) + 1, jnp.int32)
        _lenS2 = 256 - jax.random.randint(jax.random.fold_in(_rk, 8), (4,), 0, max(1, 256 // 4) + 1, jnp.int32)
        _ctx_1024P = jax.random.normal(jax.random.fold_in(_rk, 11), (4, 16, 128), jnp.float32)
        _ctx_1024c = jax.random.dirichlet(jax.random.fold_in(_rk, 511), 0.3 * jnp.ones((16,), jnp.float32), (4, 256))
        _ctx_1024t = jnp.einsum('bsk,bkd->bsd', _ctx_1024c, _ctx_1024P)
        _ctx_1024t = _ctx_1024t * jax.lax.rsqrt(jnp.mean(jnp.square(_ctx_1024t)) + 1e-12) * 0.953939
        ctx_1024 = -0.000292821 + 1.00034 * (_ctx_1024t + 0.3 * jax.random.normal(jax.random.fold_in(_rk, 611), (4, 256, 128), jnp.float32))
        fside_BxSx2_0 = jax.random.uniform(jax.random.fold_in(_rk, 12), (4, 256, 2), jnp.float32, 0.0, 0.999707)
        _g = jax.random.normal(jax.random.fold_in(_rk, 9001), (2, 2), jnp.float32)
        _g = jnp.sign(_g) * jnp.maximum(jnp.abs(_g), 1.0) + (_g == 0) * 1.0
        g_xattn = _g[0]
        g_ffn = _g[1]
        return (x, ctx_1024, fside_BxSx2_0, g_xattn, g_ffn)
    x, ctx_1024, fside_BxSx2_0, g_xattn, g_ffn = _rec_inputs()

    def _L0_xattn_setup():
        import jax, jax.numpy as jnp
        import numpy as np
        import math
        B, L, DM = (2, 256, 128)
        DS, DC, EXP = (16, 4, 2)
        DI = EXP * DM
        DR = math.ceil(DM / 16)
        DT_MIN, DT_MAX, DT_FLOOR = (0.001, 0.1, 0.0001)

        def _ssm_forward(hidden_states, z, in_proj_w, conv_w, conv_b, x_proj_w, dt_proj_w, dt_proj_b, A_log, D):
            b = hidden_states.shape[0]
            x = jnp.einsum('ed,bld->bel', in_proj_w, hidden_states)
            xp = jnp.pad(x, ((0, 0), (0, 0), (DC - 1, 0)))
            xc = jax.lax.conv_general_dilated(xp, conv_w[:, None, :], window_strides=(1,), padding='VALID', dimension_numbers=('NCH', 'OIH', 'NCH'), feature_group_count=DI)
            u = jax.nn.silu(xc + conv_b[None, :, None])
            x_dbl = jnp.einsum('ke,bel->bkl', x_proj_w, u)
            dt_lo = x_dbl[:, :DR]
            Bm = x_dbl[:, DR:DR + DS]
            Cm = x_dbl[:, DR + DS:]
            delta = jax.nn.softplus(jnp.einsum('er,brl->bel', dt_proj_w, dt_lo) + dt_proj_b[None, :, None])
            A = -jnp.exp(A_log)

            def step(state, xs):
                d_t, B_t, C_t, u_t = xs
                dA = jnp.exp(d_t[..., None] * A)
                state = state * dA + (d_t * u_t)[..., None] * B_t[:, None, :]
                y_t = jnp.einsum('ben,bn->be', state, C_t)
                return (state, y_t)
            xs = (jnp.moveaxis(delta, -1, 0), jnp.moveaxis(Bm, -1, 0), jnp.moveaxis(Cm, -1, 0), jnp.moveaxis(u, -1, 0))
            state0 = jnp.zeros((b, DI, DS), delta.dtype)
            _, ys = jax.lax.scan(step, state0, xs)
            y = jnp.moveaxis(ys, 0, -1)
            y = y + D[None, :, None] * u
            y = y * jax.nn.silu(z)
            return jnp.swapaxes(y, 1, 2)
        key = jax.random.key(seed)
        ks = jax.random.split(key, 8)
        hidden_states = jax.random.normal(ks[0], (B, L, DM), jnp.float32)
        z = jax.random.normal(ks[1], (B, DI, L), jnp.float32)
        in_proj_w = jax.random.normal(ks[2], (DI, DM), jnp.float32) * DM ** (-0.5)
        conv_w = jax.random.normal(ks[3], (DI, DC), jnp.float32) * DC ** (-0.5)
        conv_b = jnp.zeros((DI,), jnp.float32)
        x_proj_w = jax.random.normal(ks[4], (DR + 2 * DS, DI), jnp.float32) * DI ** (-0.5)
        dt_std = DR ** (-0.5)
        dt_proj_w = jax.random.uniform(ks[5], (DI, DR), jnp.float32, -dt_std, dt_std)
        dt = jnp.exp(jax.random.uniform(ks[6], (DI,), jnp.float32) * (math.log(DT_MAX) - math.log(DT_MIN)) + math.log(DT_MIN))
        dt = jnp.clip(dt, DT_FLOOR)
        dt_proj_b = dt + jnp.log(-jnp.expm1(-dt))
        A_log = jnp.log(jnp.broadcast_to(jnp.arange(1, DS + 1, dtype=jnp.float32), (DI, DS)))
        D = jnp.ones((DI,), jnp.float32)
        return dict(hidden_states=hidden_states, z=z, in_proj_w=in_proj_w, conv_w=conv_w, conv_b=conv_b, x_proj_w=x_proj_w, dt_proj_w=dt_proj_w, dt_proj_b=dt_proj_b, A_log=A_log, D=D)
    _L0_xattn_all = _L0_xattn_setup()
    _L0_xattn_in = {k: v for k, v in _L0_xattn_all.items() if k in ('in_proj_w', 'conv_w', 'conv_b', 'x_proj_w', 'dt_proj_w', 'dt_proj_b', 'A_log', 'D')}
    del _L0_xattn_all

    def _L0_ffn_setup():
        import jax, jax.numpy as jnp
        import numpy as np
        E = 8
        TOP_K = 2
        H = 256
        I_MOE = 176
        I_SH = 704
        B, S = (2, 256)

        def _moe_forward(hidden_states, router_weight, gate_up_proj, down_proj, sh_gate_w, sh_up_w, sh_down_w, shared_gate_w):
            b, s, h = hidden_states.shape
            x = hidden_states.reshape(-1, h)
            shared = jnp.einsum('ti,hi->th', jax.nn.silu(x @ sh_gate_w.T) * (x @ sh_up_w.T), sh_down_w)
            logits = x @ router_weight.T
            probs = jax.nn.softmax(logits.astype(jnp.float32), axis=-1)
            top_v, top_i = jax.lax.top_k(probs, TOP_K)
            top_v = top_v / top_v.sum(axis=-1, keepdims=True)
            combine = (jax.nn.one_hot(top_i, E, dtype=top_v.dtype) * top_v[..., None]).sum(axis=1)
            out = jnp.zeros_like(x)
            for e in range(E):
                gu = x @ gate_up_proj[e].T
                gate, up = (gu[:, :I_MOE], gu[:, I_MOE:])
                cur = jax.nn.silu(gate) * up @ down_proj[e].T
                out = out + cur * combine[:, e:e + 1]
            out = out + jax.nn.sigmoid(x @ shared_gate_w.T) * shared
            return out.reshape(b, s, h)
        key = jax.random.key(seed)
        ks = jax.random.split(key, 8)
        scale = 0.02
        return {'hidden_states': jax.random.normal(ks[0], (B, S, H), dtype=jnp.float32), 'router_weight': jax.random.normal(ks[1], (E, H), dtype=jnp.float32) * scale, 'gate_up_proj': jax.random.normal(ks[2], (E, 2 * I_MOE, H), dtype=jnp.float32) * scale, 'down_proj': jax.random.normal(ks[3], (E, H, I_MOE), dtype=jnp.float32) * scale, 'sh_gate_w': jax.random.normal(ks[4], (I_SH, H), dtype=jnp.float32) * scale, 'sh_up_w': jax.random.normal(ks[5], (I_SH, H), dtype=jnp.float32) * scale, 'sh_down_w': jax.random.normal(ks[6], (H, I_SH), dtype=jnp.float32) * scale, 'shared_gate_w': jax.random.normal(ks[7], (1, H), dtype=jnp.float32) * scale}
    _L0_ffn_all = _L0_ffn_setup()
    _L0_ffn_in = {k: v for k, v in _L0_ffn_all.items() if k in ('router_weight', 'gate_up_proj', 'down_proj', 'sh_gate_w', 'sh_up_w', 'sh_down_w', 'shared_gate_w')}
    del _L0_ffn_all

    def _L1_xattn_setup():
        import jax, jax.numpy as jnp
        import numpy as np
        DIM = 256
        CTX_DIM = 128
        N_HEADS = 32
        HEAD_DIM = DIM // N_HEADS
        POS_DIM = 2
        B, N, CTXN = (2, 256, 256)
        ROPE_BASE = 10000.0

        def apply_axial_rope(x, pos):
            b, n, h, d = x.shape
            p = pos.shape[-1]
            dpa = d // p
            half = dpa // 2
            freqs = ROPE_BASE ** (-jnp.arange(half, dtype=x.dtype) / half)
            ang = pos[..., :, None] * freqs
            cos = jnp.cos(ang)[:, :, None, :, :]
            sin = jnp.sin(ang)[:, :, None, :, :]
            xr = x.reshape(b, n, h, p, half, 2)
            x1, x2 = (xr[..., 0], xr[..., 1])
            out = jnp.stack([x1 * cos - x2 * sin, x1 * sin + x2 * cos], axis=-1)
            return out.reshape(b, n, h, d)
        key = jax.random.key(seed)
        ks = jax.random.split(key, 8)
        x = jax.random.normal(ks[0], (B, N, DIM), jnp.float32)
        ctx = jax.random.normal(ks[1], (B, CTXN, CTX_DIM), jnp.float32)
        pos_map = jax.random.uniform(ks[2], (B, N, POS_DIM), jnp.float32)
        ctx_pos_map = jax.random.uniform(ks[3], (B, CTXN, POS_DIM), jnp.float32)
        Wq = jax.random.normal(ks[4], (DIM, DIM), jnp.float32) / np.sqrt(DIM)
        Wkv = jax.random.normal(ks[5], (CTX_DIM, 2 * DIM), jnp.float32) / np.sqrt(CTX_DIM)
        Wout = jax.random.normal(ks[6], (DIM, DIM), jnp.float32) / np.sqrt(DIM)
        bout = jnp.zeros((DIM,), jnp.float32)
        return {'x': x, 'ctx': ctx, 'pos_map': pos_map, 'ctx_pos_map': ctx_pos_map, 'Wq': Wq, 'Wkv': Wkv, 'Wout': Wout, 'bout': bout}
    _L1_xattn_all = _L1_xattn_setup()
    _L1_xattn_in = {k: v for k, v in _L1_xattn_all.items() if k in ('Wq', 'Wkv', 'Wout', 'bout')}
    del _L1_xattn_all

    def _L1_ffn_setup():
        import jax, jax.numpy as jnp
        import numpy as np
        B, T, D = (1, 128, 256)
        F_DIM = 176
        E = 8
        TOPK = 2
        key = jax.random.key(seed)
        ks = jax.random.split(key, 5)
        x = jax.random.normal(ks[0], (B, T, D), dtype=jnp.float32)
        gate_w = jax.random.normal(ks[1], (E, D), dtype=jnp.float32) * 0.02
        gate_proj = jax.random.normal(ks[2], (E, F_DIM, D), dtype=jnp.float32) * 0.02
        up_proj = jax.random.normal(ks[3], (E, F_DIM, D), dtype=jnp.float32) * 0.02
        down_proj = jax.random.normal(ks[4], (E, D, F_DIM), dtype=jnp.float32) * 0.02
        return {'x': x, 'gate_w': gate_w, 'gate_proj': gate_proj, 'up_proj': up_proj, 'down_proj': down_proj}
    _L1_ffn_all = _L1_ffn_setup()
    _L1_ffn_in = {k: v for k, v in _L1_ffn_all.items() if k in ('gate_w', 'gate_proj', 'up_proj', 'down_proj')}
    del _L1_ffn_all
    return {'x': x, 'ctx_1024': ctx_1024, 'fside_BxSx2_0': fside_BxSx2_0, 'g_xattn': g_xattn, 'g_ffn': g_ffn, 'L0_xattn_in_proj_w': _L0_xattn_in['in_proj_w'], 'L0_xattn_conv_w': _L0_xattn_in['conv_w'], 'L0_xattn_conv_b': _L0_xattn_in['conv_b'], 'L0_xattn_x_proj_w': _L0_xattn_in['x_proj_w'], 'L0_xattn_dt_proj_w': _L0_xattn_in['dt_proj_w'], 'L0_xattn_dt_proj_b': _L0_xattn_in['dt_proj_b'], 'L0_xattn_A_log': _L0_xattn_in['A_log'], 'L0_xattn_D': _L0_xattn_in['D'], 'L0_ffn_router_weight': _L0_ffn_in['router_weight'], 'L0_ffn_gate_up_proj': _L0_ffn_in['gate_up_proj'], 'L0_ffn_down_proj': _L0_ffn_in['down_proj'], 'L0_ffn_sh_gate_w': _L0_ffn_in['sh_gate_w'], 'L0_ffn_sh_up_w': _L0_ffn_in['sh_up_w'], 'L0_ffn_sh_down_w': _L0_ffn_in['sh_down_w'], 'L0_ffn_shared_gate_w': _L0_ffn_in['shared_gate_w'], 'L1_xattn_Wq': _L1_xattn_in['Wq'], 'L1_xattn_Wkv': _L1_xattn_in['Wkv'], 'L1_xattn_Wout': _L1_xattn_in['Wout'], 'L1_xattn_bout': _L1_xattn_in['bout'], 'L1_ffn_gate_w': _L1_ffn_in['gate_w'], 'L1_ffn_gate_proj': _L1_ffn_in['gate_proj'], 'L1_ffn_up_proj': _L1_ffn_in['up_proj'], 'L1_ffn_down_proj': _L1_ffn_in['down_proj']}

def reference(x, ctx_1024, fside_BxSx2_0, g_xattn, g_ffn, L0_xattn_in_proj_w, L0_xattn_conv_w, L0_xattn_conv_b, L0_xattn_x_proj_w, L0_xattn_dt_proj_w, L0_xattn_dt_proj_b, L0_xattn_A_log, L0_xattn_D, L0_ffn_router_weight, L0_ffn_gate_up_proj, L0_ffn_down_proj, L0_ffn_sh_gate_w, L0_ffn_sh_up_w, L0_ffn_sh_down_w, L0_ffn_shared_gate_w, L1_xattn_Wq, L1_xattn_Wkv, L1_xattn_Wout, L1_xattn_bout, L1_ffn_gate_w, L1_ffn_gate_proj, L1_ffn_up_proj, L1_ffn_down_proj):
    import jax
    import jax.numpy as jnp

    def _L0_xattn_ref(hidden_states, z, in_proj_w, conv_w, conv_b, x_proj_w, dt_proj_w, dt_proj_b, A_log, D):
        import jax, jax.numpy as jnp
        import numpy as np
        import math
        B, L, DM = (2, 256, 128)
        DS, DC, EXP = (16, 4, 2)
        DI = EXP * DM
        DR = math.ceil(DM / 16)
        DT_MIN, DT_MAX, DT_FLOOR = (0.001, 0.1, 0.0001)

        def _ssm_forward(hidden_states, z, in_proj_w, conv_w, conv_b, x_proj_w, dt_proj_w, dt_proj_b, A_log, D):
            b = hidden_states.shape[0]
            x = jnp.einsum('ed,bld->bel', in_proj_w, hidden_states)
            xp = jnp.pad(x, ((0, 0), (0, 0), (DC - 1, 0)))
            xc = jax.lax.conv_general_dilated(xp, conv_w[:, None, :], window_strides=(1,), padding='VALID', dimension_numbers=('NCH', 'OIH', 'NCH'), feature_group_count=DI)
            u = jax.nn.silu(xc + conv_b[None, :, None])
            x_dbl = jnp.einsum('ke,bel->bkl', x_proj_w, u)
            dt_lo = x_dbl[:, :DR]
            Bm = x_dbl[:, DR:DR + DS]
            Cm = x_dbl[:, DR + DS:]
            delta = jax.nn.softplus(jnp.einsum('er,brl->bel', dt_proj_w, dt_lo) + dt_proj_b[None, :, None])
            A = -jnp.exp(A_log)

            def step(state, xs):
                d_t, B_t, C_t, u_t = xs
                dA = jnp.exp(d_t[..., None] * A)
                state = state * dA + (d_t * u_t)[..., None] * B_t[:, None, :]
                y_t = jnp.einsum('ben,bn->be', state, C_t)
                return (state, y_t)
            xs = (jnp.moveaxis(delta, -1, 0), jnp.moveaxis(Bm, -1, 0), jnp.moveaxis(Cm, -1, 0), jnp.moveaxis(u, -1, 0))
            state0 = jnp.zeros((b, DI, DS), delta.dtype)
            _, ys = jax.lax.scan(step, state0, xs)
            y = jnp.moveaxis(ys, 0, -1)
            y = y + D[None, :, None] * u
            y = y * jax.nn.silu(z)
            return jnp.swapaxes(y, 1, 2)
        return _ssm_forward(hidden_states, z, in_proj_w, conv_w, conv_b, x_proj_w, dt_proj_w, dt_proj_b, A_log, D)

    def _L0_ffn_ref(hidden_states, router_weight, gate_up_proj, down_proj, sh_gate_w, sh_up_w, sh_down_w, shared_gate_w):
        import jax, jax.numpy as jnp
        import numpy as np
        E = 8
        TOP_K = 2
        H = 256
        I_MOE = 176
        I_SH = 704
        B, S = (2, 256)

        def _moe_forward(hidden_states, router_weight, gate_up_proj, down_proj, sh_gate_w, sh_up_w, sh_down_w, shared_gate_w):
            b, s, h = hidden_states.shape
            x = hidden_states.reshape(-1, h)
            shared = jnp.einsum('ti,hi->th', jax.nn.silu(x @ sh_gate_w.T) * (x @ sh_up_w.T), sh_down_w)
            logits = x @ router_weight.T
            probs = jax.nn.softmax(logits.astype(jnp.float32), axis=-1)
            top_v, top_i = jax.lax.top_k(probs, TOP_K)
            top_v = top_v / top_v.sum(axis=-1, keepdims=True)
            combine = (jax.nn.one_hot(top_i, E, dtype=top_v.dtype) * top_v[..., None]).sum(axis=1)
            out = jnp.zeros_like(x)
            for e in range(E):
                gu = x @ gate_up_proj[e].T
                gate, up = (gu[:, :I_MOE], gu[:, I_MOE:])
                cur = jax.nn.silu(gate) * up @ down_proj[e].T
                out = out + cur * combine[:, e:e + 1]
            out = out + jax.nn.sigmoid(x @ shared_gate_w.T) * shared
            return out.reshape(b, s, h)
        return _moe_forward(hidden_states, router_weight, gate_up_proj, down_proj, sh_gate_w, sh_up_w, sh_down_w, shared_gate_w)

    def _L1_xattn_ref(x, ctx, pos_map, ctx_pos_map, Wq, Wkv, Wout, bout):
        import jax, jax.numpy as jnp
        import numpy as np
        DIM = 256
        CTX_DIM = 128
        N_HEADS = 32
        HEAD_DIM = DIM // N_HEADS
        POS_DIM = 2
        B, N, CTXN = (2, 256, 256)
        ROPE_BASE = 10000.0

        def apply_axial_rope(x, pos):
            b, n, h, d = x.shape
            p = pos.shape[-1]
            dpa = d // p
            half = dpa // 2
            freqs = ROPE_BASE ** (-jnp.arange(half, dtype=x.dtype) / half)
            ang = pos[..., :, None] * freqs
            cos = jnp.cos(ang)[:, :, None, :, :]
            sin = jnp.sin(ang)[:, :, None, :, :]
            xr = x.reshape(b, n, h, p, half, 2)
            x1, x2 = (xr[..., 0], xr[..., 1])
            out = jnp.stack([x1 * cos - x2 * sin, x1 * sin + x2 * cos], axis=-1)
            return out.reshape(b, n, h, d)
        b, n, _ = x.shape
        ctx_n = ctx.shape[1]
        q = (x @ Wq).reshape(b, n, N_HEADS, HEAD_DIM)
        k, v = jnp.split(ctx @ Wkv, 2, axis=-1)
        k = k.reshape(b, ctx_n, N_HEADS, HEAD_DIM)
        v = v.reshape(b, ctx_n, N_HEADS, HEAD_DIM)
        q = apply_axial_rope(q, pos_map)
        k = apply_axial_rope(k, ctx_pos_map)
        scale = 1.0 / np.sqrt(HEAD_DIM).astype(np.float32)
        logits = jnp.einsum('bqhd,bkhd->bhqk', q, k) * scale
        w = jax.nn.softmax(logits, axis=-1)
        attn = jnp.einsum('bhqk,bkhd->bqhd', w, v)
        attn = attn.reshape(b, n, N_HEADS * HEAD_DIM)
        return attn @ Wout + bout

    def _L1_ffn_ref(x, gate_w, gate_proj, up_proj, down_proj):
        import jax, jax.numpy as jnp
        import numpy as np
        B, T, D = (1, 128, 256)
        F_DIM = 176
        E = 8
        TOPK = 2
        b, t, d = x.shape
        x_flat = x.reshape(-1, d)
        n = x_flat.shape[0]
        router_logits = x_flat @ gate_w.T
        top_w, sel = jax.lax.top_k(router_logits, TOPK)
        top_w = jax.nn.softmax(top_w, axis=-1)
        tok_ids = jnp.arange(n)[:, None]
        tw = jnp.zeros((n, E), dtype=x.dtype).at[tok_ids, sel].add(top_w)
        g = jnp.einsum('nd,efd->enf', x_flat, gate_proj)
        u = jnp.einsum('nd,efd->enf', x_flat, up_proj)
        h = jax.nn.silu(g) * u
        eo = jnp.einsum('enf,edf->end', h, down_proj)
        out = jnp.einsum('end,ne->nd', eo, tw)
        return out.reshape(b, t, d)
    x = x + jnp.tanh(g_xattn[0]) * _L0_xattn_ref(ctx_1024, _layernorm(x, axis=-1), L0_xattn_in_proj_w, L0_xattn_conv_w, L0_xattn_conv_b, L0_xattn_x_proj_w, L0_xattn_dt_proj_w, L0_xattn_dt_proj_b, L0_xattn_A_log, L0_xattn_D)
    x = x + jnp.tanh(g_ffn[0]) * _L0_ffn_ref(_layernorm(x, axis=-1), L0_ffn_router_weight, L0_ffn_gate_up_proj, L0_ffn_down_proj, L0_ffn_sh_gate_w, L0_ffn_sh_up_w, L0_ffn_sh_down_w, L0_ffn_shared_gate_w)
    x = x + jnp.tanh(g_xattn[1]) * _L1_xattn_ref(_layernorm(x, axis=-1), ctx_1024, fside_BxSx2_0, fside_BxSx2_0, L1_xattn_Wq, L1_xattn_Wkv, L1_xattn_Wout, L1_xattn_bout)
    x = x + jnp.tanh(g_ffn[1]) * _L1_ffn_ref(_layernorm(x, axis=-1), L1_ffn_gate_w, L1_ffn_gate_proj, L1_ffn_up_proj, L1_ffn_down_proj)
    return x

_drawn_inputs = setup_inputs


def setup_inputs(seed=0):
    import zlib

    import numpy as np

    out = dict(_drawn_inputs(seed))
    spreads = {'g_ffn': (-1.0, 0.6),
     'L0_xattn_conv_b': (0.0, 0.286),
     'L0_xattn_D': (1.0, 0.2),
     'L1_xattn_bout': (0.0, 0.1)}
    factors = {'L0_xattn_dt_proj_w': 8.0,
     'L0_xattn_dt_proj_b': 3.643,
     'L0_xattn_A_log': 3.199,
     'L0_ffn_router_weight': 8.0,
     'L0_ffn_gate_up_proj': 8.0,
     'L0_ffn_down_proj': 8.0,
     'L0_ffn_sh_gate_w': 6.11,
     'L0_ffn_sh_up_w': 6.02,
     'L0_ffn_sh_down_w': 6.038,
     'L0_ffn_shared_gate_w': 8.0,
     'L1_ffn_gate_w': 8.0,
     'L1_ffn_gate_proj': 8.0,
     'L1_ffn_up_proj': 7.987,
     'L1_ffn_down_proj': 7.965}
    for name, (base, spread) in spreads.items():
        noise = np.random.default_rng([zlib.crc32(name.encode()), seed]).standard_normal(out[name].shape)
        drawn = base * np.exp(spread * noise) if base else spread * noise
        out[name] = jnp.asarray(drawn.astype(out[name].dtype))
    for name, factor in factors.items():
        out[name] = (out[name] * factor).astype(out[name].dtype)
    return out
```

```python
from contextlib import ExitStack

import concourse.bass as bass
from concourse import mybir

F32 = mybir.dt.float32
BF16 = mybir.dt.bfloat16
U32 = mybir.dt.uint32
ACT = mybir.ActivationFunctionType
ALU = mybir.AluOpType
AX = mybir.AxisListType

P = 128
NB = 4
L = 256
D = 256
HALVES = D // P
NS = 16
GROUPS = NS // 2
DR = 8
TAPS = 4
E = 8
FE = 176
FS = 704
T0 = -(-(E * FE + FS) // P)
T1 = E * FE // P
NH = 32
HD = D // NH
STACK = 9 * HD
SCALE = 1.0 / float(HD) ** 0.5
EPS = 1e-5
TWO_PI_HI = 6.28125
TWO_PI_LO = 0.0019353071795864769
ROUND = 12582912.0
CHAIN = dict(DVE_A=28, ACT_A=26, POOL_A=7, DVE_B=37, ACT_B=9, POOL_B=0)


def program(nc, x_t, x_rows, ctx_t, pos, gates, in_proj, conv_w, conv_b, bc_proj, dt_lo_proj, dt_proj,
            dt_b, a_log, d_skip, gu0, down0, route0, gu1, down1, route1, wq, wq_swap, wk, wk_swap, wv,
            wout, bout, sel_state, sel0, sel1, ident, columns, iota8, out):
    ctx = ExitStack()
    with ctx:
        def sb(name, shape, dt=F32):
            return ctx.enter_context(nc.sbuf_tensor(name, shape, dt))

        def sem(name):
            return ctx.enter_context(nc.semaphore(name))

        bank = [ctx.enter_context(nc.psum_tensor(f"bank{i}", [P, 512], F32)) for i in range(8)]

        w_in = sb("w_in", [P, D])
        w_conv = sb("w_conv", [P, HALVES, TAPS])
        b_conv = sb("b_conv", [P, HALVES])
        w_bc = sb("w_bc", [P, HALVES, 96])
        w_dtlo = sb("w_dtlo", [P, HALVES, DR])
        w_dt = sb("w_dt", [DR, D])
        b_dt = sb("b_dt", [P, HALVES])
        a_col = sb("a_col", [P, HALVES, NS])
        d_col = sb("d_col", [P, HALVES])
        gate_raw = sb("gate_raw", [P, 4])
        gate = sb("gate", [P, 4])
        half_gate = sb("half_gate", [P, 4])
        w_gu0 = sb("w_gu0", [P, T0, 2, 2, P])
        w_down0 = sb("w_down0", [P, T0, D])
        w_gu1 = w_gu0[:, 0:T1, :, :, :]
        w_down1 = w_down0[:, 0:T1, :]
        w_route0 = sb("w_route0", [P, HALVES, E + 1])
        w_route1 = sb("w_route1", [P, HALVES, E])
        w_q = sb("w_q", [P, HALVES, D])
        w_qs = sb("w_qs", [P, HALVES, D])
        w_k = sb("w_k", [P, D])
        w_ks = sb("w_ks", [P, D])
        w_v = sb("w_v", [P, D])
        w_out = sb("w_out", [P, HALVES, D])
        b_out = sb("b_out", [P, HALVES])
        pick_state = sb("pick_state", [96, 2 * NS, P], BF16)
        pick0 = sb("pick0", [96, T0, P], BF16)
        pick1 = sb("pick1", [96, T1, P], BF16)
        ident_b = sb("ident_b", [P, P], BF16)
        col = sb("col", [P, 8])
        iota = sb("iota", [P, E])
        mean_w = sb("mean_w", [P, P])
        ones_pad = sb("ones_pad", [P, 4, 32])

        xres = sb("xres", [P, NB, 2 * L])
        ctx_all = sb("ctx_all", [P, NB, L])
        region3 = sb("region3", [P, 6144])
        delta = region3[:, 0:2048].rearrange("p (b e l) -> p b e l", b=NB, e=2)
        du = region3[:, 2048:4096].rearrange("p (b n) -> p b n", b=NB)
        ygate = region3[:, 4096:6144].rearrange("p (b n) -> p b n", b=NB)
        p_exp = region3[:, 0:4096].rearrange("p (r j k l) -> p r j k l", r=2, j=4, k=2)
        v_pad = region3[:, 4096:6144].rearrange("p (k h c) -> p k h c", k=2, h=NH)
        bc3 = sb("bc3", [96, NB * L], BF16)
        cos_t = sb("cos_t", [P, NB, L])
        sin_t = sb("sin_t", [P, NB, L])

        region = sb("region", [P, 9248])
        xpad = region[:, 0:HALVES * NB * (L + 3)].rearrange("p (e b l) -> p e b l", e=HALVES, b=NB)
        tmp = region[:, 2080:4128].rearrange("p (b n) -> p b n", b=NB)
        tmp2 = region[:, 4128:6176].rearrange("p (b n) -> p b n", b=NB)
        u_all = region[:, 6176:8224].rearrange("p (b n) -> p b n", b=NB)
        bc_rest = region[0:96, 8224:9248]
        q_stack = region[0:96, 0:NH * L // 2].bitcast(BF16).rearrange("p (h l) -> p h l", h=NH)
        k_stack = region[0:96, NH * L // 2:NH * L].bitcast(BF16).rearrange("p (h l) -> p h l", h=NH)
        da = region[:, 0:2048].rearrange("p (r j e l) -> p r j e l", r=2, j=2, e=2)
        dbu = region[:, 4128:5152]
        states = region[:, 5152:6176]
        rt1, rt2 = region[:, 8192:8704], region[:, 8704:9216]
        region2 = sb("region2", [P, 3072])
        x_nat = region2[:, 0:2048].rearrange("p (b e l) -> p b e l", b=NB, e=2)
        dt_lo = region2[0:DR, 2048:3072]
        hc = region2[:, 0:2048].rearrange("p (r j n) -> p r j n", r=2, j=2)
        acc = region2[:, 2048:2560]
        qk = region2[:, 0:1024]
        parts = region2[:, 1024:2560].bitcast(BF16).rearrange("p (i n) -> p i n", i=3)
        step = sb("step", [P, 2, L])
        stats = sb("stats", [P, 8, 6])
        mv = sb("mv", [P, 8, 2])
        z_scale = sb("z_scale", [P, 8])
        z_bias = sb("z_bias", [P, 8])

        dev = sb("dev", [P, 512])
        sq = sb("sq", [P, 512])
        rstd = sb("rstd", [P, L])
        xn = sb("xn", [P, HALVES, L])
        logit = sb("logit", [P, 2, 16])
        top = sb("top", [P, 2, E])
        top_i = sb("top_i", [P, 2, E], U32)
        top_f = sb("top_f", [P, 2, E])
        filler = sb("filler", [P, 1])
        gap = sb("gap", [P, 2, 1])
        egap = sb("egap", [P, 2, 1])
        sg = sb("sg", [P, 2, 1])
        w12 = sb("w12", [P, 2, 2])
        cm = sb("cm", [P, 2, 32])
        cm_b = sb("cm_b", [P, 2, E])
        cm3 = sb("cm3", [P, 2, 3, 32], BF16)
        cmt = sb("cmt", [96, L], BF16)
        th = sb("th", [P, 2, 512])
        h1 = sb("h1", [P, 3, 512])
        cbs = sb("cbs", [P, 2, 512])
        hh = sb("hh", [P, 3, 2, L])
        ctx_b = sb("ctx_b", [P, L])
        mx = sb("mx", [P, 2, NH])
        mrest = sb("mrest", [P, 2, NH])
        mp = sb("mp", [P, 2, 3, NH], BF16)
        mt = sb("mt", [96, L], BF16)
        attn = step
        scratch = nc.dram_tensor("scratch", (3, 2, D, L), BF16, kind="Internal").ap()

        ld_const, ld_front, ld_x, ld_m0, ld_m1, ld_at = (
            sem(n) for n in ("ld_const", "ld_front", "ld_x", "ld_m0", "ld_m1", "ld_at"))
        dve_front, act_front, pool_front = sem("dve_front"), sem("act_front"), sem("pool_front")
        dve_0, act_0, pool_0 = sem("dve_0"), sem("act_0"), sem("pool_0")
        dve_a, act_a, pool_a = sem("dve_a"), sem("act_a"), sem("pool_a")
        dve_z, act_z, pool_z = sem("dve_z"), sem("act_z"), sem("pool_z")
        dve_b, act_b, pool_b = sem("dve_b"), sem("act_b"), sem("pool_b")
        memset_done, xin_ready, xin_copied, conv_ready, u_ready = (
            sem(n) for n in ("memset_done", "xin_ready", "xin_copied", "conv_ready", "u_ready"))
        bc_proj_ready, dtlo_ready, dtlo_copied, dt_ready = (
            sem(n) for n in ("bc_proj_ready", "dtlo_ready", "dtlo_copied", "dt_ready"))
        soft_in, w_ready, ln_ready, zstat_ready, zrstd_ready, zbias_ready, ygate_raw = (
            sem(n) for n in ("soft_in", "w_ready", "ln_ready", "zstat_ready", "zrstd_ready", "zbias_ready",
                             "ygate_raw"))
        a_exp, front_dve, front_pool, ang_ready, gate_ready, bc3_ready = (
            sem(n) for n in ("a_exp", "front_dve", "front_pool", "ang_ready", "gate_ready",
                             "bc3_ready"))
        step_ready, da_ready, bc_ready, dbu_done, scan_done, hc_ready, hc_used, acc_used = (
            sem(n) for n in ("step_ready", "da_ready", "bc_ready", "dbu_done", "scan_done", "hc_ready", "hc_used",
                             "acc_used"))
        x_ready = {k: sem(f"x_ready_{k}") for k in ("m0", "at", "m1", "out")}
        norm = {k: {n: sem(f"{n}_{k}") for n in ("mean_ready", "dev_ready", "sq_ready", "var_ready",
                                                 "rstd_ready", "xn_ready")} for k in ("m0", "at", "m1")}
        moe = {k: {n: sem(f"{n}_{k}") for n in (
            "logits_ready", "gap_ready", "egap_ready", "cm_ready", "cmt_ready", "cmt_copied", "gu_ready",
            "tanh_ready", "h1_ready", "cb_ready", "cb_copied", "h_ready", "h_used")}
            for k in ("m0", "m1")}
        (ctx_copied, qk_ready, v_ready, v_copied, rope_read, parts_ready, parts_stored, stacks_ready,
         s1_ready, max_done, mp_ready, mt_ready, mt_copied, rows_ready, s2_ready, exp_done, pv_done,
         attn_ready, o_ready, vpad_zero) = (sem(n) for n in (
            "ctx_copied", "qk_ready", "v_ready", "v_copied", "rope_read", "parts_ready", "parts_stored",
            "stacks_ready", "s1_ready", "max_done", "mp_ready", "mt_ready", "mt_copied", "rows_ready",
            "s2_ready", "exp_done", "pv_done", "attn_ready", "o_ready", "vpad_zero"))
        stored = sem("stored")
        block = ctx.enter_context(nc.Block())

        N_CONST = 2

        def wait(e, s, value):
            if isinstance(value, int):
                if value > 0:
                    e.wait_ge(s, value)
                return
            e.wait_ge(s, value)
            e.wait_ge(ld_const, 16 * N_CONST)

        class Chain:

            def __init__(self, e, s, base=0):
                self.e, self.s, self.base, self.n, self.marks = e, s, base, 0, []

            def then(self, ins, s=None, value=None):
                if s is None:
                    self.n += 1
                    s, value = self.s, self.base + self.n
                self.marks.append((s, value))
                ins.then_inc(s, 1)

            def behind(self, lag=0):
                if len(self.marks) > lag:
                    wait(self.e, *self.marks[-1 - lag])

            def close(self, per=None):
                assert per is None or self.n == per, (self.n, per)
                self.behind()

        MOE = {
            "m0": dict(T=T0, gu=w_gu0, down=w_down0, route=w_route0, nr=E + 1, pick=pick0, gate=2,
                       banks=[(2, 3), (4, 5)], ld=ld_m0, nxt="at"),
            "m1": dict(T=T1, gu=w_gu1, down=w_down1, route=w_route1, nr=E, pick=pick1, gate=3,
                       banks=[(4, 5)], ld=ld_m1, nxt="out"),
        }
        for m in MOE.values():
            m["NP"] = -(-m["T"] // 2)
        CB, Y = bank[6], bank[7]

        @block.sync
        def _(sp):
            sp.dma_start(w_in[:, :], in_proj).then_inc(ld_front, 16)
            sp.dma_start(ctx_all[:, :, :], ctx_t).then_inc(ld_front, 16)
            sp.dma_start(w_conv[:, :, :], conv_w).then_inc(ld_front, 16)
            sp.dma_start(b_conv[:, :], conv_b).then_inc(ld_front, 16)
            sp.dma_start(w_bc[:, :, :], bc_proj).then_inc(ld_front, 16)
            sp.dma_start(w_dtlo[:, :, :], dt_lo_proj).then_inc(ld_front, 16)
            sp.dma_start(w_dt[:, :], dt_proj).then_inc(ld_front, 16)
            sp.dma_start(b_dt[:, :], dt_b).then_inc(ld_front, 16)
            sp.dma_start(a_col[:, :, :], a_log).then_inc(ld_front, 16)
            sp.dma_start(d_col[:, :], d_skip).then_inc(ld_front, 16)
            sp.dma_start(xres[:, :, :], x_t).then_inc(ld_x, 16)
            sp.dma_start(pick_state[:, :, :], sel_state).then_inc(ld_x, 16)
            sp.dma_start(ident_b[:, :], ident).then_inc(ld_m0, 16)
            sp.dma_start(w_gu0[:, :, :, :, :], gu0).then_inc(ld_m0, 16)
            sp.dma_start(w_route0[:, :, :], route0).then_inc(ld_m0, 16)
            sp.dma_start(pick0[:, :, :], sel0).then_inc(ld_m0, 16)
            sp.dma_start(w_down0[:, :, :], down0).then_inc(ld_m0, 16)
            sp.dma_start(iota[:, :], iota8).then_inc(ld_m0, 16)
            for to, of in ((w_q[:, :, :], wq), (w_qs[:, :, :], wq_swap), (w_k[:, :], wk),
                           (w_ks[:, :], wk_swap), (w_v[:, :], wv), (w_out[:, :, :], wout),
                           (b_out[:, :], bout)):
                sp.dma_start(to, of).then_inc(ld_at, 16)
            sp.wait_ge(x_ready["at"], NB)
            for to, of in ((w_gu1, gu1), (w_down1, down1),
                           (w_route1[:, :, :], route1), (pick1[:, :, :], sel1)):
                sp.dma_start(to, of).then_inc(ld_m1, 16)
            sp.wait_ge(vpad_zero, 2)
            with sp.Fori(0, NB) as b:
                wait(sp, parts_ready, b + 1)
                sp.dma_start(scratch.rearrange("i s (t p) l -> p i s t l", p=P),
                             parts[:, :, :].rearrange("p i (s t l) -> p i s t l", s=2, t=2)
                             ).then_inc(parts_stored, 16)
                wait(sp, parts_stored, 16 * b + 16)
                for j in range(3):
                    for i in range(3):
                        r = j * 24 + i * 8
                        sp.dma_start(q_stack[r:r + 8, :, :],
                                     scratch[i, 0].rearrange("(h d) l -> d h l", d=HD)
                                     ).then_inc(stacks_ready, 16)
                        sp.dma_start(k_stack[r:r + 8, :, :],
                                     scratch[j, 1].rearrange("(h d) l -> d h l", d=HD)
                                     ).then_inc(stacks_ready, 16)
                wait(sp, mt_copied, b + 1)
                for s in range(3):
                    sp.dma_start(q_stack[STACK + s:STACK + s + 1, :, :], mt[32 * s:32 * s + 32, :]
                                 ).then_inc(rows_ready, 16)
                wait(sp, x_ready["out"], b + 1)
                sp.dma_start(out[:, b, :], xres[:, b, :]).then_inc(stored, 16)
            sp.wait_ge(stored, 16 * NB)

        @block.gpsimd
        def _(pool):
            pool.memset(region[:, 0:HALVES * NB * (L + 3)].rearrange("p (g l) -> p g l", l=L + 3)[:, :, 0:3],
                        0.0).then_inc(memset_done, 1)
            pool.memset(mean_w[:, :], 1.0 / D).then_inc(memset_done, 1)
            pool.memset(ones_pad[:, :, :], 0.0).then_inc(memset_done, 1)
            pool.memset(cm[:, :, :], 0.0).then_inc(memset_done, 1)
            pool.wait_ge(memset_done, 4)
            for r in range(4):
                pool.memset(ones_pad[:, r, r * HD:(r + 1) * HD], 1.0).then_inc(memset_done, 1)
            ch = Chain(pool, pool_front)
            pool.wait_ge(ld_const, 16 * N_CONST)
            ang, turns = cos_t[:, :, :], sin_t[:, :, :]
            ch.then(pool.tensor_scalar(ang, ang, col[:, 2:3], None, ALU.mult))
            ch.behind()
            ch.then(pool.tensor_scalar(turns, ang, 1.0 / (TWO_PI_HI + TWO_PI_LO), ROUND, ALU.mult, ALU.add))
            ch.behind()
            ch.then(pool.tensor_scalar(turns, turns, ROUND, None, ALU.subtract))
            t3 = h1[:, 0:2, :].rearrange("p a n -> p (a n)").rearrange("p (b l) -> p b l", b=NB)
            for part in (TWO_PI_HI, TWO_PI_LO):
                ch.behind()
                ch.then(pool.tensor_scalar(t3, turns, part, None, ALU.mult))
                ch.behind()
                ch.then(pool.tensor_tensor(ang, ang, t3, ALU.subtract))
            ch.behind()
            ch.then(pool.tensor_copy(t3, ang), ang_ready, 1)
            pool.wait_ge(ygate_raw, 8)
            pool.wait_ge(gate_ready, 1)
            ch.behind()
            ch.then(pool.tensor_scalar(ygate[:, :, :], ygate[:, :, :], gate[:, 0:1], None, ALU.mult))
            pool.wait_ge(u_ready, 2)
            pool.wait_ge(ld_x, 32)
            pool.wait_ge(front_dve, 1)
            for e in range(2):
                ch.behind()
                ch.then(pool.tensor_scalar(tmp[:, :, e * L:(e + 1) * L], u_all[:, :, e * L:(e + 1) * L],
                                           d_col[:, e:e + 1], None, ALU.mult))
            ch.behind()
            ch.then(pool.tensor_tensor(tmp, tmp, ygate[:, :, :], ALU.mult))
            ch.behind()
            ch.then(pool.tensor_tensor(xres[:, :, :], xres[:, :, :], tmp, ALU.add), front_pool, 1)

            def mixer_group(ch, b, g):
                if g == 0:
                    wait(pool, acc_used, b)
                wait(pool, hc_ready, GROUPS * b + g + 1)
                ch.behind()
                if g == 0:
                    ch.then(pool.tensor_tensor(acc, hc[:, g % 2, 0, :], hc[:, g % 2, 1, :], ALU.add)
                            , hc_used, GROUPS * b + g + 1)
                else:
                    ch.then(pool.tensor_tensor(acc, acc, hc[:, g % 2, 0, :], ALU.add))
                    ch.behind()
                    ch.then(pool.tensor_tensor(acc, acc, hc[:, g % 2, 1, :], ALU.add), hc_used, GROUPS * b + g + 1)

            def expert_pair(ch, k, b, p):
                m, s = MOE[k], moe[k]
                n = min(2, m["T"] - 2 * p) * L
                wait(pool, s["h1_ready"], m["NP"] * b + p + 1)
                wait(pool, s["cb_copied"], m["NP"] * b + p + 1)
                if p >= 3:
                    wait(pool, s["h_used"], m["NP"] * b + p - 2)
                ch.behind(2)
                ch.then(pool.tensor_tensor(hh[:, p % 3, 0:n // L, :].rearrange("p a l -> p (a l)"),
                                           h1[:, p % 3, 0:n], cbs[:, p % 2, 0:n], ALU.mult)
                        , s["h_ready"], m["NP"] * b + p + 1)

            ch.close()
            ch = Chain(pool, pool_0)
            for g in range(GROUPS):
                mixer_group(ch, 0, g)
            ch.close()
            with pool.Fori(0, NB - 1) as i:
                ch = Chain(pool, pool_a, i * CHAIN["POOL_A"])
                for slot in range(12):
                    if slot < GROUPS:
                        mixer_group(ch, i + 1, slot)
                    if slot >= 3:
                        expert_pair(ch, "m0", i, slot - 3)
                ch.close(CHAIN["POOL_A"])
            ch = Chain(pool, pool_z)
            for p in range(MOE["m0"]["NP"]):
                expert_pair(ch, "m0", NB - 1, p)
            ch.close()
            pool.wait_ge(x_ready["at"], NB)
            pool.memset(v_pad, 0.0).then_inc(vpad_zero, 1)
            pool.wait_ge(vpad_zero, 1)
            pool.memset(k_stack[64:96, :, :], 1.0).then_inc(vpad_zero, 1)
            with pool.Fori(0, NB) as b:
                ch = Chain(pool, pool_b, b * CHAIN["POOL_B"])
                for p in range(MOE["m1"]["NP"]):
                    expert_pair(ch, "m1", b, p)
                ch.close(CHAIN["POOL_B"])

        @block.scalar
        def _(act):
            act.dma_start(col[:, :], columns).then_inc(ld_const, 16)
            act.dma_start(cos_t[:, :, :], pos).then_inc(ld_const, 16)
            act.dma_start(x_nat, x_rows).then_inc(ld_front, 16)
            act.dma_start(gate_raw[:, :], gates).then_inc(ld_front, 16)
            ch = Chain(act, act_front)
            act.wait_ge(ld_const, 32)
            for e in range(2):
                for q in range(2):
                    n = 2 * e + q
                    act.wait_ge(xin_ready, n + 1)
                    ch.then(act.activation(xpad[:, e, 2 * q:2 * q + 2, 3:3 + L],
                                           bank[n][:, :].rearrange("p (b l) -> p b l", b=2),
                                           ACT.Copy), xin_copied, n + 1)
            act.wait_ge(zstat_ready, 1)
            act.wait_ge(ld_front, 16 * 12)
            ch.then(act.activation(z_scale[:, :], mv[:, :, 1], ACT.Ln, bias=col[:, 0:1]))
            ch.behind()
            ch.then(act.activation(z_scale[:, :], z_scale[:, :], ACT.Exp, scale=-0.5), zrstd_ready, 1)
            ch.then(act.activation(a_col[:, :, :], a_col[:, :, :], ACT.Exp), a_exp, 1)
            for e in range(2):
                act.wait_ge(conv_ready, e + 1)
                ch.then(act.activation(u_all[:, :, e * L:(e + 1) * L], tmp[:, :, e * L:(e + 1) * L], ACT.Silu,
                                       bias=b_conv[:, e:e + 1]), u_ready, e + 1)
            act.wait_ge(zbias_ready, 1)
            for n in range(8):
                b, e = n // 2, n % 2
                ch.then(act.activation(ygate[:, b, e * L:(e + 1) * L], x_nat[:, b, e, :], ACT.Silu,
                                       bias=z_bias[:, n:n + 1], scale=z_scale[:, n:n + 1])
                        , ygate_raw, n + 1)
            ch.then(act.activation(gate[:, :], gate_raw[:, :], ACT.Tanh), gate_ready, 1)
            act.wait_ge(ang_ready, 1)
            t3 = h1[:, 0:2, :].rearrange("p a n -> p (a n)").rearrange("p (b l) -> p b l", b=NB)
            ch.then(act.activation(sin_t[:, :, :], t3, ACT.Sin, scale=col[:, 3:4]))
            ch.then(act.activation(cos_t[:, :, :], t3, ACT.Abs))
            ch.behind()
            ch.then(act.activation(cos_t[:, :, :], cos_t[:, :, :], ACT.Sin, bias=col[:, 1:2], scale=-1.0))
            act.wait_ge(dtlo_ready, 1)
            for q in range(2):
                ch.then(act.activation(dt_lo[:, 512 * q:512 * q + 512], bank[4 + q][0:DR, :], ACT.Copy)
                        , dtlo_copied, q + 1)
            for e in range(2):
                for q in range(2):
                    n = 2 * e + q
                    act.wait_ge(dt_ready, n + 1)
                    ch.behind()
                    ch.then(act.activation(delta[:, 2 * q:2 * q + 2, e, :],
                                           bank[n][:, :].rearrange("p (b l) -> p b l", b=2), ACT.Identity,
                                           bias=b_dt[:, e:e + 1]))
            dl = delta[:, :, :, :].rearrange("p b e l -> p (b e l)")
            t1 = tmp.rearrange("p b n -> p (b n)")
            t2 = tmp2.rearrange("p b n -> p (b n)")
            ch.behind()
            ch.then(act.activation(t2, dl, ACT.Abs))
            ch.behind()
            ch.then(act.activation(t2, t2, ACT.Exp, scale=-1.0), soft_in, 1)
            act.wait_ge(w_ready, 1)
            ch.then(act.activation(t1, xpad_flat(region), ACT.Ln), ln_ready, 1)

            def mixer_decay(ch, b, g):
                wait(act, scan_done, GROUPS * b + g - 1)
                if g == 0:
                    wait(act, step_ready, b + 1)
                for j in range(2):
                    for e in range(2):
                        n = 2 * g + j
                        ins = act.activation(da[:, g % 2, j, e, 1:L], step[:, e, 1:L], ACT.Exp,
                                             scale=a_col[:, e, n:n + 1])
                        ch.then(ins, *((da_ready, GROUPS * b + g + 1) if j and e else ()))

            def norm_square(ch, k, b):
                wait(act, norm[k]["dev_ready"], b + 1)
                ch.behind()
                ch.then(act.activation(sq[:, :], dev[:, :], ACT.Square), norm[k]["sq_ready"], b + 1)

            def norm_rstd(ch, k, b, at):
                wait(act, norm[k]["var_ready"], b + 1)
                ch.then(act.activation(rstd[:, :], at[:, L:2 * L], ACT.Ln, bias=col[:, 0:1]))
                ch.behind()
                ch.then(act.activation(rstd[:, :], rstd[:, :], ACT.Exp, scale=-0.5)
                        , norm[k]["rstd_ready"], b + 1)

            def route_exp(ch, k, b):
                wait(act, moe[k]["gap_ready"], b + 1)
                if k == "m0":
                    ch.then(act.activation(sg[:, :, :], logit[:, :, E:E + 1], ACT.Tanh, scale=0.5))
                ch.then(act.activation(egap[:, :, :], gap[:, :, :], ACT.Exp)
                        , moe[k]["egap_ready"], b + 1)

            def route_copy(ch, k, b):
                wait(act, moe[k]["cmt_ready"], b + 1)
                ch.then(act.activation(cmt[:, :], CB[0:96, L:2 * L], ACT.Copy)
                        , moe[k]["cmt_copied"], b + 1)

            def expert_tanh(ch, k, b, p):
                m, s = MOE[k], moe[k]
                n = min(2, m["T"] - 2 * p) * L
                wait(act, s["gu_ready"], m["NP"] * b + p + 1)
                if p >= 2:
                    wait(act, s["h1_ready"], m["NP"] * b + p - 1)
                ch.behind(1)
                ch.then(act.activation(th[:, p % 2, 0:n], bank[m["banks"][p % len(m["banks"])][0]][:, 0:n],
                                       ACT.Tanh, scale=0.5), s["tanh_ready"], m["NP"] * b + p + 1)

            def expert_weight(ch, k, b, p):
                m, s = MOE[k], moe[k]
                n = min(2, m["T"] - 2 * p) * L
                wait(act, s["cb_ready"], m["NP"] * b + p + 1)
                if p >= 2:
                    wait(act, s["h_ready"], m["NP"] * b + p - 1)
                ch.behind(1)
                ch.then(act.activation(cbs[:, p % 2, 0:n], CB[:, 0:n], ACT.Copy), s["cb_copied"], m["NP"] * b + p + 1)

            act.wait_ge(front_dve, 1)
            ch.close()
            ch = Chain(act, act_0)
            for g in range(GROUPS):
                mixer_decay(ch, 0, g)

            def turn_a(ch, i, mixer):
                for slot in range(12):
                    if mixer and slot == 0:
                        mixer_decay(ch, i + 1, 0)
                    if mixer and slot + 1 < GROUPS:
                        mixer_decay(ch, i + 1, slot + 1)
                    if slot == 0:
                        norm_square(ch, "m0", i)
                    elif slot == 1:
                        norm_rstd(ch, "m0", i, CB)
                    elif slot == 2:
                        route_exp(ch, "m0", i)
                    elif slot == 3:
                        route_copy(ch, "m0", i)
                    if 2 <= slot < 11:
                        expert_tanh(ch, "m0", i, slot - 2)
                    if slot >= 3:
                        expert_weight(ch, "m0", i, slot - 3)

            ch.close()
            with act.Fori(0, NB - 1) as i:
                ch = Chain(act, act_a, i * CHAIN["ACT_A"])
                turn_a(ch, i, True)
                ch.close(CHAIN["ACT_A"])
            ch = Chain(act, act_z)
            turn_a(ch, NB - 1, False)

            ch.close()
            with act.Fori(0, NB) as b:
                ch = Chain(act, act_b, b * CHAIN["ACT_B"])
                norm_square(ch, "at", b)
                ch.then(act.activation(ctx_b[:, :], ctx_all[:, b, :], ACT.Copy), ctx_copied, b + 1)
                norm_rstd(ch, "at", b, bank[2])
                wait(act, vpad_zero, 2)
                wait(act, v_ready, b + 1)
                for r in range(4):
                    for t in range(2):
                        ins = act.activation(
                            v_pad[:, t, :, :].rearrange("p (g r) c -> p g r c", r=4)[:, :, r, r * HD:(r + 1) * HD],
                            bank[0][:, t * L:(t + 1) * L].rearrange("p (g r d) -> p g r d", g=NH // 4,
                                                                    r=4)[:, :, r, :], ACT.Copy)
                        ch.then(ins, *((v_copied, b + 1) if r == 3 and t == 1 else ()))
                wait(act, mt_ready, b + 1)
                ch.then(act.activation(mt[:, :], bank[2][0:96, 0:L], ACT.Copy), mt_copied, b + 1)
                for n in range(NH):
                    wait(act, s2_ready, NH * b + n + 1)
                    if n % 4 == 0 and n >= 8:
                        wait(act, pv_done, 8 * b + n // 4 - 1)
                    ch.behind(2)
                    ch.then(act.activation(p_exp[:, n // 4 % 2, n % 4, :, :],
                                           bank[n % 2][:, :].rearrange("p (k l) -> p k l", k=2), ACT.Exp,
                                           scale=SCALE), exp_done, NH * b + n + 1)
                norm_square(ch, "m1", b)
                norm_rstd(ch, "m1", b, CB)
                route_exp(ch, "m1", b)
                expert_tanh(ch, "m1", b, 0)
                route_copy(ch, "m1", b)
                expert_weight(ch, "m1", b, 0)
                for p in range(1, MOE["m1"]["NP"]):
                    expert_tanh(ch, "m1", b, p)
                    expert_weight(ch, "m1", b, p)
                ch.close(CHAIN["ACT_B"])

        @block.vector
        def _(dve):
            ch = Chain(dve, dve_front)
            dve.wait_ge(ld_front, 16 * 12)
            for n in range(8):
                ch.then(dve.bn_stats(stats[:, n, :], x_nat[:, n // 2, n % 2, :]))
            ch.behind()
            for n in range(8):
                ch.then(dve.bn_aggr(mv[:, n, :], stats[:, n, :]), *((zstat_ready, 1) if n == 7 else ()))
            for e in range(2):
                dve.wait_ge(xin_copied, 2 * e + 2)
                dve.wait_ge(memset_done, 8)
                dst = tmp[:, :, e * L:(e + 1) * L]
                for k in range(TAPS):
                    src = xpad[:, e, :, k:k + L]
                    ch.behind()
                    if k == 0:
                        ch.then(dve.tensor_scalar(dst, src, w_conv[:, e, k:k + 1], None, ALU.mult))
                    else:
                        ins = dve.scalar_tensor_tensor(dst, src, w_conv[:, e, k:k + 1], dst, ALU.mult, ALU.add)
                        ch.then(ins, *((conv_ready, e + 1) if k == TAPS - 1 else ()))
            dve.wait_ge(zrstd_ready, 1)
            ch.behind()
            ch.then(dve.scalar_tensor_tensor(z_bias[:, :], mv[:, :, 0], -1.0, z_scale[:, :],
                                             ALU.mult, ALU.mult), zbias_ready, 1)
            dve.wait_ge(a_exp, 1)
            ch.then(dve.tensor_scalar(a_col[:, :, :], a_col[:, :, :], -1.0, None, ALU.mult))
            dve.wait_ge(bc_proj_ready, 1)
            for q in range(2):
                cols = slice(512 * q, 512 * q + 512)
                src, rest, to = bank[6 + q], bc_rest[:, cols], bc3[:, cols]
                ch.behind()
                ch.then(dve.tensor_copy(to, src[0:96, :]))
                ch.behind()
                ch.then(dve.tensor_tensor(rest, src[0:96, :], to, ALU.subtract))
                ch.behind()
                for strip in ((32, 64), (64, 96)):
                    ch.then(dve.tensor_copy(bc3[strip[0]:strip[1], cols], bc_rest[strip[0]:strip[1], cols]))
                ch.behind()
                ch.then(dve.tensor_tensor(bc_rest[64:96, cols], bc_rest[64:96, cols], bc3[64:96, cols],
                                          ALU.subtract))
                ch.behind()
                ch.then(dve.tensor_copy(bc3[64:96, cols], bc_rest[64:96, cols]), bc3_ready, q + 1)
            dve.wait_ge(gate_ready, 1)
            ch.then(dve.tensor_scalar(half_gate[:, :], gate[:, :], 0.5, None, ALU.mult))
            dl = delta[:, :, :, :].rearrange("p b e l -> p (b e l)")
            t1 = tmp.rearrange("p b n -> p (b n)")
            t2 = tmp2.rearrange("p b n -> p (b n)")
            w1 = xpad_flat(region)
            dve.wait_ge(soft_in, 1)
            dve.wait_ge(u_ready, 2)
            ch.behind()
            ch.then(dve.tensor_scalar(w1, t2, 1.0, None, ALU.add), w_ready, 1)
            ch.behind()
            ch.then(dve.scalar_tensor_tensor(t2, w1, 1.0, t2, ALU.subtract, ALU.subtract))
            dve.wait_ge(ln_ready, 1)
            ch.behind()
            ch.then(dve.scalar_tensor_tensor(dl, dl, 0.0, t1, ALU.max, ALU.add))
            ch.behind()
            ch.then(dve.tensor_tensor(dl, dl, t2, ALU.subtract))
            ch.behind()
            ch.then(dve.tensor_tensor(du[:, :, :], delta[:, :, :, :].rearrange("p b e l -> p b (e l)"),
                                      u_all, ALU.mult))
            dve.wait_ge(ygate_raw, 8)
            dve.wait_ge(dt_ready, 4)
            ch.then(dve.memset(da[:, :, :, :, 0:1].rearrange("p r j e l -> p (r j e) l"), 0.0)
                    , front_dve, 1)

            def mixer_step(ch, b):
                ch.behind()
                ch.then(dve.tensor_scalar(step[:, :, :].rearrange("p e l -> p (e l)"),
                                          delta[:, b, :, :].rearrange("p e l -> p (e l)"), 1.0, None,
                                          ALU.mult), step_ready, b + 1)

            def mixer_group(ch, b, g):
                wait(dve, bc_ready, GROUPS * b + g + 1)
                ch.behind(1)
                ch.then(dve.tensor_tensor(
                    dbu.rearrange("p (j e l) -> p j e l", j=2, e=2),
                    du[:, b, :].rearrange("p (e l) -> p e l", e=2).unsqueeze(1).broadcast_to([P, 2, 2, L]),
                    bank[0][:, :].rearrange("p (j l) -> p j l", j=2).unsqueeze(2).broadcast_to([P, 2, 2, L]),
                    ALU.mult), dbu_done, GROUPS * b + g + 1)
                wait(dve, da_ready, GROUPS * b + g + 1)
                ch.behind()
                ch.then(dve.tensor_tensor_scan(
                    states, da[:, g % 2, :, :, :].rearrange("p j e l -> p (j e l)"), dbu, 0.0,
                    ALU.mult, ALU.add), scan_done, GROUPS * b + g + 1)
                wait(dve, hc_used, GROUPS * b + g - 1)
                ch.behind()
                ch.then(dve.tensor_tensor(
                    hc[:, g % 2, :, :].rearrange("p j (e l) -> p j e l", e=2),
                    states.rearrange("p (j e l) -> p j e l", j=2, e=2),
                    bank[1][:, :].rearrange("p (j l) -> p j l", j=2).unsqueeze(2).broadcast_to([P, 2, 2, L]),
                    ALU.mult), hc_ready, GROUPS * b + g + 1)

            def mixer_end(ch, b):
                wait(dve, hc_used, GROUPS * b + GROUPS)
                ch.behind()
                ch.then(dve.tensor_tensor(dev[:, :], acc, ygate[:, b, :], ALU.mult), acc_used, b + 1)
                ch.behind()
                ch.then(dve.tensor_tensor(xres[:, b, :], xres[:, b, :], dev[:, :], ALU.add)
                        , x_ready["m0"], b + 1)

            def norm_dev(ch, k, b, at):
                wait(dve, norm[k]["mean_ready"], b + 1)
                ch.behind()
                ch.then(dve.tensor_tensor(
                    dev[:, :].rearrange("p (e l) -> p e l", e=2),
                    xres[:, b, :].rearrange("p (e l) -> p e l", e=2),
                    at[:, 0:L].unsqueeze(1).broadcast_to([P, 2, L]), ALU.subtract)
                , norm[k]["dev_ready"], b + 1)

            def norm_scale(ch, k, b):
                wait(dve, norm[k]["rstd_ready"], b + 1)
                ch.behind()
                ch.then(dve.tensor_tensor(
                    xn[:, :, :], dev[:, :].rearrange("p (e l) -> p e l", e=2),
                    rstd[:, :].unsqueeze(1).broadcast_to([P, 2, L]), ALU.mult)
                , norm[k]["xn_ready"], b + 1)

            def route_top(ch, k, b):
                nr = MOE[k]["nr"]
                wait(dve, moe[k]["logits_ready"], b + 1)
                ch.behind()
                ch.then(dve.tensor_copy(logit[:, :, 0:nr],
                                        CB[:, 0:32].rearrange("p (t n) -> p t n", t=2)[:, :, 0:nr]))
                ch.behind()
                ch.then(dve.memset(filler[:, :], 0.0))
                for t in range(2):
                    ch.then(dve.max(top[:, t, :], logit[:, t, 0:E]))
                ch.behind()
                ch.then(dve.tensor_tensor(gap[:, :, :], top[:, :, 1:2], top[:, :, 0:1], ALU.subtract)
                        , moe[k]["gap_ready"], b + 1)
                for t in range(2):
                    ch.then(dve.max_index(top_i[:, t, :], top[:, t, :], logit[:, t, 0:E]))
                ch.behind()
                ch.then(dve.tensor_copy(top_f[:, :, :], top_i[:, :, :]))

            def route_weights(ch, k, b):
                wait(dve, moe[k]["egap_ready"], b + 1)
                ch.behind()
                ch.then(dve.tensor_scalar(w12[:, :, 0:1], egap[:, :, :], 1.0, None, ALU.add))
                ch.behind()
                ch.then(dve.reciprocal(w12[:, :, 0:1], w12[:, :, 0:1]))
                ch.behind()
                ch.then(dve.tensor_tensor(w12[:, :, 1:2], egap[:, :, :], w12[:, :, 0:1], ALU.mult))
                ch.behind()
                for t in range(2):
                    ch.then(dve.tensor_scalar(cm[:, t, 0:E], iota[:, :], top_f[:, t, 0:1], w12[:, t, 0:1],
                                              ALU.is_equal, ALU.mult))
                for t in range(2):
                    ch.then(dve.tensor_scalar(cm_b[:, t, :], iota[:, :], top_f[:, t, 1:2], w12[:, t, 1:2],
                                              ALU.is_equal, ALU.mult))
                ch.behind()
                ch.then(dve.tensor_tensor(cm[:, :, 0:E], cm[:, :, 0:E], cm_b[:, :, :], ALU.add))
                if k == "m0":
                    ch.then(dve.tensor_scalar(cm[:, :, E:E + 1], sg[:, :, :], 0.5, 0.5, ALU.mult, ALU.add))
                ch.behind()
                ch.then(dve.tensor_copy(cm3[:, :, 0, :], cm[:, :, :]))
                ch.behind()
                ch.then(dve.tensor_tensor(cm[:, :, :], cm[:, :, :], cm3[:, :, 0, :], ALU.subtract))
                ch.behind()
                ch.then(dve.tensor_copy(cm3[:, :, 1, :], cm[:, :, :]))
                ch.behind()
                ch.then(dve.tensor_tensor(cm3[:, :, 2, :], cm[:, :, :], cm3[:, :, 1, :], ALU.subtract)
                        , moe[k]["cm_ready"], b + 1)

            def expert_pair(ch, k, b, p):
                m, s = MOE[k], moe[k]
                n = min(2, m["T"] - 2 * p) * L
                gb, ub = m["banks"][p % len(m["banks"])]
                wait(dve, s["tanh_ready"], m["NP"] * b + p + 1)
                ch.behind(1)
                ch.then(dve.scalar_tensor_tensor(th[:, p % 2, 0:n], th[:, p % 2, 0:n], 1.0,
                                                 bank[gb][:, 0:n], ALU.add, ALU.mult))
                if p >= 3:
                    wait(dve, s["h_ready"], m["NP"] * b + p - 2)
                ch.behind()
                ch.then(dve.tensor_tensor(h1[:, p % 3, 0:n], th[:, p % 2, 0:n], bank[ub][:, 0:n], ALU.mult)
                        , s["h1_ready"], m["NP"] * b + p + 1)

            def expert_end(ch, k, b):
                m = MOE[k]
                wait(dve, moe[k]["h_used"], m["NP"] * b + m["NP"])
                ch.behind()
                ch.then(dve.scalar_tensor_tensor(xres[:, b, :], Y[:, :], half_gate[:, m["gate"]:m["gate"] + 1],
                                                 xres[:, b, :], ALU.mult, ALU.add)
                        , x_ready[m["nxt"]], b + 1)

            ch.close()
            ch = Chain(dve, dve_0)
            mixer_step(ch, 0)
            for g in range(GROUPS):
                mixer_group(ch, 0, g)
            dve.wait_ge(front_pool, 1)
            mixer_end(ch, 0)
            dve.wait_ge(ld_m0, 16 * 6)

            def turn_a(ch, i, mixer):
                if mixer:
                    mixer_step(ch, i + 1)
                for slot in range(12):
                    if mixer and slot < GROUPS:
                        mixer_group(ch, i + 1, slot)
                    if slot == 0:
                        norm_dev(ch, "m0", i, CB)
                    elif slot == 1:
                        norm_scale(ch, "m0", i)
                    elif slot == 2:
                        route_top(ch, "m0", i)
                    elif slot == 3:
                        route_weights(ch, "m0", i)
                    if 2 <= slot < 11:
                        expert_pair(ch, "m0", i, slot - 2)
                if mixer:
                    mixer_end(ch, i + 1)
                expert_end(ch, "m0", i)

            ch.close()
            with dve.Fori(0, NB - 1) as i:
                ch = Chain(dve, dve_a, i * CHAIN["DVE_A"])
                turn_a(ch, i, True)
                ch.close(CHAIN["DVE_A"])
            ch = Chain(dve, dve_z)
            turn_a(ch, NB - 1, False)

            ch.close()
            with dve.Fori(0, NB) as b:
                ch = Chain(dve, dve_b, b * CHAIN["DVE_B"])
                norm_dev(ch, "at", b, bank[2])
                norm_scale(ch, "at", b)
                for s in range(2):
                    wait(dve, qk_ready, 2 * b + s + 1)
                    for t, (src, table) in enumerate(((2 * s, cos_t), (2 * s + 1, sin_t))):
                        ch.behind()
                        ins = dve.tensor_tensor(
                            (rt1, rt2)[t][:, :].rearrange("p (m l) -> p m l", m=2),
                            bank[src][:, :].rearrange("p (m l) -> p m l", m=2),
                            table[:, b, :].unsqueeze(1).broadcast_to([P, 2, L]), ALU.mult)
                        ch.then(ins, *((rope_read, 2 * b + s + 1) if t else ()))
                    ch.behind()
                    if s == 0:
                        ch.then(dve.tensor_tensor(qk[:, 0:512], rt1[:, :], rt2[:, :], ALU.add))
                    else:
                        ch.then(dve.tensor_tensor(qk[:, 512:1024], rt1[:, :], rt2[:, :], ALU.add))
                ch.behind()
                ch.then(dve.tensor_copy(parts[:, 0, :], qk))
                ch.behind()
                ch.then(dve.tensor_tensor(qk, qk, parts[:, 0, :], ALU.subtract))
                ch.behind()
                ch.then(dve.tensor_copy(parts[:, 1, :], qk))
                ch.behind()
                ch.then(dve.tensor_tensor(parts[:, 2, :], qk, parts[:, 1, :], ALU.subtract)
                        , parts_ready, b + 1)
                for h in range(NH):
                    wait(dve, s1_ready, NH * b + h + 1)
                    ch.behind(1)
                    ch.then(dve.tensor_reduce(mx[:, :, h], bank[h % 2][:, :].rearrange("p (t k) -> p t k", t=2),
                                              AX.X, ALU.max), max_done, NH * b + h + 1)
                ch.behind()
                ch.then(dve.tensor_scalar(mp[:, :, 0, :], mx[:, :, :], -1.0, None, ALU.mult))
                ch.behind()
                ch.then(dve.scalar_tensor_tensor(mrest[:, :, :], mx[:, :, :], -1.0, mp[:, :, 0, :],
                                                 ALU.mult, ALU.subtract))
                ch.behind()
                ch.then(dve.tensor_copy(mp[:, :, 1, :], mrest[:, :, :]))
                ch.behind()
                ch.then(dve.tensor_tensor(mp[:, :, 2, :], mrest[:, :, :], mp[:, :, 1, :], ALU.subtract)
                        , mp_ready, b + 1)
                wait(dve, pv_done, 8 * b + 8)
                ch.behind()
                ch.then(dve.reciprocal(rt1[:, :], bank[3][:, :]))
                ch.behind()
                ch.then(dve.tensor_tensor(attn[:, :, :], bank[2][:, :].rearrange("p (e l) -> p e l", e=2),
                                          rt1[:, :].rearrange("p (e l) -> p e l", e=2), ALU.mult)
                        , attn_ready, b + 1)
                wait(dve, o_ready, b + 1)
                ch.behind()
                for e in range(2):
                    ch.then(dve.tensor_scalar(rt2[:, e * L:(e + 1) * L], bank[0][:, e * L:(e + 1) * L],
                                              b_out[:, e:e + 1], gate[:, 1:2], ALU.add, ALU.mult))
                ch.behind()
                ch.then(dve.tensor_tensor(xres[:, b, :], xres[:, b, :], rt2[:, :], ALU.add)
                        , x_ready["m1"], b + 1)
                norm_dev(ch, "m1", b, CB)
                norm_scale(ch, "m1", b)
                route_top(ch, "m1", b)
                expert_pair(ch, "m1", b, 0)
                route_weights(ch, "m1", b)
                for p in range(1, MOE["m1"]["NP"]):
                    expert_pair(ch, "m1", b, p)
                expert_end(ch, "m1", b)
                ch.close(CHAIN["DVE_B"])

        @block.tensor
        def _(pe):
            pe.wait_ge(ld_front, 16 * 12)
            for e in range(2):
                for q in range(2):
                    pe.matmul(bank[2 * e + q][:, :], w_in[:, e * P:(e + 1) * P], ctx_all[:, 2 * q:2 * q + 2, :],
                              start=True, stop=True).then_inc(xin_ready, 1)
            pe.wait_ge(u_ready, 2)
            for q in range(2):
                for e in range(2):
                    last = pe.matmul(bank[4 + q][0:DR, :], w_dtlo[:, e, :],
                                     u_all[:, 2 * q:2 * q + 2, e * L:(e + 1) * L], start=(e == 0), stop=(e == 1))
            last.then_inc(dtlo_ready, 1)
            for q in range(2):
                for e in range(2):
                    last = pe.matmul(bank[6 + q][0:96, :], w_bc[:, e, :],
                                     u_all[:, 2 * q:2 * q + 2, e * L:(e + 1) * L], start=(e == 0), stop=(e == 1))
            last.then_inc(bc_proj_ready, 1)
            pe.wait_ge(dtlo_copied, 2)
            for e in range(2):
                for q in range(2):
                    pe.matmul(bank[2 * e + q][:, :], w_dt[:, e * P:(e + 1) * P], dt_lo[:, 512 * q:512 * q + 512],
                              start=True, stop=True).then_inc(dt_ready, 1)

            def mixer_spread(b, g):
                for which, (to, free) in enumerate(((bank[0], dbu_done), (bank[1], hc_ready))):
                    wait(pe, free, GROUPS * b + g)
                    for j in range(2):
                        last = pe.matmul(to[:, j * L:(j + 1) * L], pick_state[:, which * NS + 2 * g + j, :],
                                         bc3[:, bass.ds(b * L, L)], start=True, stop=True)
                last.then_inc(bc_ready, 1)

            def norm_mean(k, b, to):
                wait(pe, x_ready[k], b + 1)
                for e in range(2):
                    last = pe.matmul(to[:, 0:L], mean_w[:, :], xres[:, b, e * L:(e + 1) * L],
                                     start=(e == 0), stop=(e == 1))
                last.then_inc(norm[k]["mean_ready"], 1)

            def norm_var(k, b, to):
                wait(pe, norm[k]["sq_ready"], b + 1)
                for e in range(2):
                    last = pe.matmul(to[:, L:2 * L], mean_w[:, :], sq[:, e * L:(e + 1) * L],
                                     start=(e == 0), stop=(e == 1))
                last.then_inc(norm[k]["var_ready"], 1)

            def route(k, b):
                m = MOE[k]
                wait(pe, norm[k]["xn_ready"], b + 1)
                for t in range(2):
                    for e in range(2):
                        last = pe.matmul(CB[:, 16 * t:16 * t + m["nr"]], xn[:, e, t * P:(t + 1) * P],
                                         m["route"][:, e, 0:m["nr"]], start=(e == 0), stop=(e == 1))
                last.then_inc(moe[k]["logits_ready"], 1)

            def route_turn(k, b):
                wait(pe, moe[k]["cm_ready"], b + 1)
                for t in range(2):
                    last = pe.matmul(CB[0:96, L + t * P:L + (t + 1) * P],
                                     cm3[:, t, :, :].rearrange("p s c -> p (s c)"), ident_b[:, :],
                                     start=True, stop=True)
                last.then_inc(moe[k]["cmt_ready"], 1)

            def expert_up(k, b, p):
                m, s = MOE[k], moe[k]
                banks = m["banks"][p % len(m["banks"])]
                if p >= len(m["banks"]):
                    wait(pe, s["h1_ready"], m["NP"] * b + p - len(m["banks"]) + 1)
                for j in range(min(2, m["T"] - 2 * p)):
                    for which in range(2):
                        for e in range(2):
                            last = pe.matmul(bank[banks[which]][:, j * L:(j + 1) * L],
                                             m["gu"][:, 2 * p + j, e, which, :], xn[:, e, :],
                                             start=(e == 0), stop=(e == 1))
                last.then_inc(s["gu_ready"], 1)

            def expert_weight(k, b, p):
                m, s = MOE[k], moe[k]
                if p == 0:
                    wait(pe, s["cmt_copied"], b + 1)
                else:
                    wait(pe, s["cb_copied"], m["NP"] * b + p)
                for j in range(min(2, m["T"] - 2 * p)):
                    last = pe.matmul(CB[:, j * L:(j + 1) * L], m["pick"][:, 2 * p + j, :], cmt[:, :],
                                     start=True, stop=True)
                last.then_inc(s["cb_ready"], 1)

            def expert_down(k, b, p):
                m, s = MOE[k], moe[k]
                wait(pe, s["h_ready"], m["NP"] * b + p + 1)
                for j in range(min(2, m["T"] - 2 * p)):
                    t = 2 * p + j
                    for e in range(2):
                        last = pe.matmul(Y[:, e * L:(e + 1) * L], m["down"][:, t, e * P:(e + 1) * P],
                                         hh[:, p % 3, j, :], start=(t == 0 and e == 0),
                                         stop=(t == m["T"] - 1), skip_group_check=True)
                last.then_inc(s["h_used"], 1)

            def turn_a(i, mixer):
                for slot in range(13):
                    if mixer and slot < GROUPS:
                        mixer_spread(i + 1, slot)
                    if slot == 0:
                        norm_mean("m0", i, CB)
                    elif slot == 1:
                        norm_var("m0", i, CB)
                    elif slot == 2:
                        route("m0", i)
                    elif slot == 3:
                        route_turn("m0", i)
                    if 2 <= slot < 11:
                        expert_up("m0", i, slot - 2)
                    if 3 <= slot < 12:
                        expert_weight("m0", i, slot - 3)
                    if slot >= 4:
                        expert_down("m0", i, slot - 4)

            pe.wait_ge(bc3_ready, 2)
            pe.wait_ge(ld_x, 32)
            pe.wait_ge(front_dve, 1)
            for g in range(GROUPS):
                mixer_spread(0, g)
            pe.wait_ge(memset_done, 8)
            pe.wait_ge(ld_m0, 16 * 6)
            with pe.Fori(0, NB - 1) as i:
                turn_a(i, True)
            turn_a(NB - 1, False)

            pe.wait_ge(ld_at, 16 * 7)
            pe.wait_ge(ld_m1, 16 * 4)
            with pe.Fori(0, NB) as b:
                norm_mean("at", b, bank[2])
                norm_var("at", b, bank[2])
                wait(pe, norm["at"]["xn_ready"], b + 1)
                for to, w in ((bank[0], w_q), (bank[1], w_qs)):
                    for m in range(2):
                        for e in range(2):
                            last = pe.matmul(to[:, m * L:(m + 1) * L], w[:, e, m * P:(m + 1) * P], xn[:, e, :],
                                             start=(e == 0), stop=(e == 1))
                last.then_inc(qk_ready, 1)
                wait(pe, ctx_copied, b + 1)
                for to, w in ((bank[2], w_k), (bank[3], w_ks)):
                    for m in range(2):
                        last = pe.matmul(to[:, m * L:(m + 1) * L], w[:, m * P:(m + 1) * P], ctx_b[:, :],
                                         start=True, stop=True)
                last.then_inc(qk_ready, 1)
                wait(pe, rope_read, 2 * b + 1)
                for t in range(2):
                    last = pe.matmul(bank[0][:, t * L:(t + 1) * L], ctx_b[:, t * P:(t + 1) * P], w_v[:, :],
                                     start=True, stop=True)
                last.then_inc(v_ready, 1)
                wait(pe, stacks_ready, 16 * 18 * (b + 1))
                wait(pe, v_copied, b + 1)
                for h in range(NH):
                    if h >= 2:
                        wait(pe, max_done, NH * b + h - 1)
                    for t in range(2):
                        last = pe.matmul(bank[h % 2][:, t * L:(t + 1) * L], q_stack[0:STACK, h, t * P:(t + 1) * P],
                                         k_stack[0:STACK, h, :], start=True, stop=True)
                    last.then_inc(s1_ready, 1)
                wait(pe, mp_ready, b + 1)
                for t in range(2):
                    last = pe.matmul(bank[2][0:96, t * P:(t + 1) * P], mp[:, t, :, :].rearrange("p s h -> p (s h)"),
                                     ident_b[:, :], start=True, stop=True)
                last.then_inc(mt_ready, 1)
                wait(pe, rows_ready, 48 * (b + 1))

                def values(g):
                    half, r = g // 4, g % 4
                    wait(pe, exp_done, NH * b + 4 * g + 4)
                    for k in range(2):
                        for to, w in ((bank[2], None), (bank[3], ones_pad[:, r, :])):
                            for s in range(4):
                                h = 16 * half + 4 * s + r
                                last = pe.matmul(to[32 * s:32 * s + 32, half * L:(half + 1) * L],
                                                 v_pad[:, k, h, :] if w is None else w,
                                                 p_exp[:, g % 2, s, k, :],
                                                 start=(r == 0 and k == 0), stop=(r == 3 and k == 1))
                    last.then_inc(pv_done, 1)

                for g in range(8):
                    half, r = g // 4, g % 4
                    for s in range(4):
                        n, h = 4 * g + s, 16 * half + 4 * s + r
                        if n >= 2:
                            wait(pe, exp_done, NH * b + n - 1)
                        for k in range(2):
                            last = pe.matmul(bank[n % 2][:, k * L:(k + 1) * L],
                                             k_stack[0:STACK + 3, h, k * P:(k + 1) * P],
                                             q_stack[0:STACK + 3, h, :], start=True, stop=True)
                        last.then_inc(s2_ready, 1)
                    if g >= 1:
                        values(g - 1)
                values(7)
                wait(pe, attn_ready, b + 1)
                for m in range(2):
                    for e in range(2):
                        last = pe.matmul(bank[0][:, m * L:(m + 1) * L], w_out[:, e, m * P:(m + 1) * P],
                                         attn[:, e, :], start=(e == 0), stop=(e == 1))
                last.then_inc(o_ready, 1)
                norm_mean("m1", b, CB)
                norm_var("m1", b, CB)
                route("m1", b)
                expert_up("m1", b, 0)
                route_turn("m1", b)
                expert_weight("m1", b, 0)
                for p in range(1, MOE["m1"]["NP"]):
                    expert_up("m1", b, p)
                    expert_weight("m1", b, p)
                    expert_down("m1", b, p - 1)
                expert_down("m1", b, MOE["m1"]["NP"] - 1)


def xpad_flat(region):
    return region[:, 0:2048]




def _lay_out(np, i):
    bf = np.dtype("bfloat16")

    def halves(a):
        return a.reshape(2, P, -1).transpose(1, 0, 2)

    def feature_rows(blocks, tiles):
        rows = np.concatenate(blocks, 0)
        full = np.zeros((tiles * P, rows.shape[1]), rows.dtype)
        full[:rows.shape[0]] = rows
        return full

    def gate_up(gate, up, tiles):
        both = np.stack([feature_rows(gate, tiles), feature_rows(up, tiles)])
        return both.reshape(2, tiles, P, 2, P).transpose(4, 1, 3, 0, 2)

    def down(blocks, tiles):
        return feature_rows(blocks, tiles).reshape(tiles, P, D).transpose(1, 0, 2)

    def expert_pick(tiles, shared):
        pick = np.zeros((96, tiles, P), bf)
        for f in range(tiles * P):
            j = f // FE if f < E * FE else E
            for s in range(3):
                pick[32 * s + j, f // P, f % P] = 1
        return pick

    x, c = i["x"], i["ctx_1024"]
    w_x = i["L0_xattn_x_proj_w"]
    gu = i["L0_ffn_gate_up_proj"]
    g1, u1 = i["L1_ffn_gate_proj"], i["L1_ffn_up_proj"]
    swap = np.arange(D) ^ 1
    wkv = i["L1_xattn_Wkv"]
    sel_state = np.zeros((96, 2 * NS, P), bf)
    for j in range(2 * NS):
        sel_state[[j, 32 + j, 64 + j], j, :] = 1
    row = np.arange(P)
    columns = np.zeros((P, 8), np.float32)
    columns[:, 0] = EPS
    columns[:, 1] = np.pi / 2
    columns[:, 2] = np.where(row // 2 % 2 == 0, 1.0, 0.01)
    columns[:, 3] = np.where(row % 2 == 0, -1.0, 1.0)
    return dict(
        x_t=x.transpose(2, 0, 1).reshape(2, P, NB, L).transpose(1, 2, 0, 3).reshape(P, NB, 2 * L),
        x_rows=x.reshape(NB, 2, P, D).transpose(2, 0, 1, 3),
        ctx_t=c.transpose(2, 0, 1),
        pos=i["fside_BxSx2_0"].transpose(2, 0, 1)[row % HD // 4],
        gates=np.broadcast_to(np.concatenate([i["g_xattn"], i["g_ffn"]]), (P, 4)),
        in_proj=i["L0_xattn_in_proj_w"].T,
        conv_w=halves(i["L0_xattn_conv_w"]),
        conv_b=i["L0_xattn_conv_b"].reshape(2, P).T,
        bc_proj=halves(np.tile(w_x[DR:].T, (1, 3))),
        dt_lo_proj=halves(w_x[:DR].T),
        dt_proj=i["L0_xattn_dt_proj_w"].T,
        dt_b=i["L0_xattn_dt_proj_b"].reshape(2, P).T,
        a_log=halves(i["L0_xattn_A_log"]),
        d_skip=i["L0_xattn_D"].reshape(2, P).T,
        gu0=gate_up([gu[:, :FE].reshape(-1, D), i["L0_ffn_sh_gate_w"]],
                    [gu[:, FE:].reshape(-1, D), i["L0_ffn_sh_up_w"]], T0),
        down0=down([i["L0_ffn_down_proj"].transpose(0, 2, 1).reshape(-1, D), i["L0_ffn_sh_down_w"].T], T0),
        route0=halves(np.concatenate([i["L0_ffn_router_weight"], i["L0_ffn_shared_gate_w"]]).T),
        gu1=gate_up([g1.reshape(-1, D)], [u1.reshape(-1, D)], T1),
        down1=down([i["L1_ffn_down_proj"].transpose(0, 2, 1).reshape(-1, D)], T1),
        route1=halves(i["L1_ffn_gate_w"].T),
        wq=halves(i["L1_xattn_Wq"]),
        wq_swap=halves(i["L1_xattn_Wq"][:, swap]),
        wk=wkv[:, :D],
        wk_swap=wkv[:, swap],
        wv=wkv[:, D:],
        wout=halves(i["L1_xattn_Wout"]),
        bout=i["L1_xattn_bout"].reshape(2, P).T,
        sel_state=sel_state,
        sel0=expert_pick(T0, True),
        sel1=expert_pick(T1, False),
        ident=np.eye(P, dtype=bf),
        columns=columns,
        iota8=np.broadcast_to(np.arange(E, dtype=np.float32), (P, E)),
    )


def kernel(**inputs):
    import numpy as np
    import concourse.bacc as bacc
    from concourse.bass_utils import run_bass_kernel_spmd

    laid = _lay_out(np, {k: np.asarray(v) for k, v in inputs.items()})
    nc = bacc.Bacc("TRN2", target_bir_lowering=False, num_devices=1)
    arrays, handles = {}, {}
    for name, a in laid.items():
        a = np.ascontiguousarray(a)
        arrays["in_" + name] = a
        handles[name] = nc.dram_tensor("in_" + name, a.shape, mybir.dt.from_np(a.dtype), kind="ExternalInput").ap()
    out = nc.dram_tensor("out_0", (P, NB, 2 * L), F32, kind="ExternalOutput").ap()
    program(nc, out=out, **handles)
    got = run_bass_kernel_spmd(nc, [arrays], core_ids=[0]).results[0]["out_0"]
    return np.ascontiguousarray(got.reshape(P, NB, 2, L).transpose(1, 3, 2, 0).reshape(NB, L, D))
```

```python
from contextlib import ExitStack

import concourse.bass as bass
from concourse import mybir

F32 = mybir.dt.float32
BF16 = mybir.dt.bfloat16
U32 = mybir.dt.uint32
ACT = mybir.ActivationFunctionType
ALU = mybir.AluOpType
AX = mybir.AxisListType

P = 128
NB = 4
L = 256
D = 256
HALVES = D // P
NS = 16
GROUPS = NS // 2
DR = 8
TAPS = 4
E = 8
FE = 176
FS = 704
T0 = -(-(E * FE + FS) // P)
T1 = E * FE // P
NH = 32
HD = D // NH
STACK = 9 * HD
SCALE = 1.0 / float(HD) ** 0.5
EPS = 1e-5
TWO_PI_HI = 6.28125
TWO_PI_LO = 0.0019353071795864769
ROUND = 12582912.0
CHAIN = dict(DVE_A=28, ACT_A=26, POOL_A=7, DVE_B=42, ACT_B=9, POOL_B=0)


def program(nc, x_t, x_rows, ctx_t, pos, gates, in_proj, conv_w, conv_b, bc_proj, dt_lo_proj, dt_proj,
            dt_b, a_log, d_skip, gu0, down0, route0, gu1, down1, route1, wq, wq_swap, wk, wk_swap, wv,
            wout, bout, sel_state, sel0, sel1, ident, columns, iota8, out):
    ctx = ExitStack()
    with ctx:
        def sb(name, shape, dt=F32):
            return ctx.enter_context(nc.sbuf_tensor(name, shape, dt))

        def sem(name):
            return ctx.enter_context(nc.semaphore(name))

        bank = [ctx.enter_context(nc.psum_tensor(f"bank{i}", [P, 512], F32)) for i in range(8)]

        w_in = sb("w_in", [P, D])
        w_conv = sb("w_conv", [P, HALVES, TAPS])
        b_conv = sb("b_conv", [P, HALVES])
        w_bc = sb("w_bc", [P, HALVES, 96])
        w_dtlo = sb("w_dtlo", [P, HALVES, DR])
        w_dt = sb("w_dt", [DR, D])
        b_dt = sb("b_dt", [P, HALVES])
        a_col = sb("a_col", [P, HALVES, NS])
        d_col = sb("d_col", [P, HALVES])
        gate_raw = sb("gate_raw", [P, 4])
        gate = sb("gate", [P, 4])
        half_gate = sb("half_gate", [P, 4])
        w_gu0 = sb("w_gu0", [P, T0, 2, 2, P])
        w_down0 = sb("w_down0", [P, T0, D])
        w_gu1 = w_gu0[:, 0:T1, :, :, :]
        w_down1 = w_down0[:, 0:T1, :]
        w_route0 = sb("w_route0", [P, HALVES, E + 1])
        w_route1 = sb("w_route1", [P, HALVES, E])
        w_q = sb("w_q", [P, HALVES, D])
        w_qs = sb("w_qs", [P, HALVES, D])
        w_k = sb("w_k", [P, D])
        w_ks = sb("w_ks", [P, D])
        w_v = sb("w_v", [P, D])
        w_out = sb("w_out", [P, HALVES, D])
        b_out = sb("b_out", [P, HALVES])
        region4 = sb("region4", [P, 2048])
        pick_state = region4[0:96, :].bitcast(BF16).rearrange("p (n c) -> p n c", n=2 * NS)
        pick0 = sb("pick0", [96, T0, P], BF16)
        pick1 = sb("pick1", [96, T1, P], BF16)
        ident_b = sb("ident_b", [P, P], BF16)
        col = sb("col", [P, 8])
        iota = sb("iota", [P, E])
        mean_w = sb("mean_w", [P, P])
        ones_pad = sb("ones_pad", [P, 4, 32])

        xres = sb("xres", [P, NB, 2 * L])
        ctx_all = sb("ctx_all", [P, NB, L])
        region3 = sb("region3", [P, 6144])
        delta = region3[:, 0:2048].rearrange("p (b e l) -> p b e l", b=NB, e=2)
        du = region3[:, 2048:4096].rearrange("p (b n) -> p b n", b=NB)
        ygate = region3[:, 4096:6144].rearrange("p (b n) -> p b n", b=NB)
        p_exp = region3[:, 0:4096].rearrange("p (r j k l) -> p r j k l", r=2, j=4, k=2)
        v_pad = region3[:, 4096:6144].rearrange("p (k h c) -> p k h c", k=2, h=NH)
        bc3 = sb("bc3", [96, NB * L], BF16)
        cos_t = sb("cos_t", [P, NB, L])
        sin_t = sb("sin_t", [P, NB, L])

        region = sb("region", [P, 9248])
        xpad = region[:, 0:HALVES * NB * (L + 3)].rearrange("p (e b l) -> p e b l", e=HALVES, b=NB)
        tmp = region[:, 2080:4128].rearrange("p (b n) -> p b n", b=NB)
        tmp2 = region[:, 4128:6176].rearrange("p (b n) -> p b n", b=NB)
        u_all = region[:, 6176:8224].rearrange("p (b n) -> p b n", b=NB)
        bc_rest = region[0:96, 8224:9248]
        q_stack = region[0:96, 0:NH * L // 2].bitcast(BF16).rearrange("p (h l) -> p h l", h=NH)
        k_stack = region[0:96, NH * L // 2:NH * L].bitcast(BF16).rearrange("p (h l) -> p h l", h=NH)
        da = region[:, 0:2048].rearrange("p (r j e l) -> p r j e l", r=2, j=2, e=2)
        dbu = region[:, 4128:5152]
        states = region[:, 5152:6176]
        rt1, rt2 = region[:, 8192:8704], region[:, 8704:9216]
        region2 = sb("region2", [P, 3072])
        x_nat = region2[:, 0:2048].rearrange("p (b e l) -> p b e l", b=NB, e=2)
        dt_lo = region2[0:DR, 2048:3072]
        hc = region2[:, 0:2048].rearrange("p (r j n) -> p r j n", r=2, j=2)
        acc = region2[:, 2048:2560]
        qk = region2[:, 0:1024]
        parts = region2[:, 1024:2560].bitcast(BF16).rearrange("p (i n) -> p i n", i=3)
        step = sb("step", [P, 2, L])
        stats = sb("stats", [P, 8, 6])
        mv = sb("mv", [P, 8, 2])
        z_scale = sb("z_scale", [P, 8])
        z_bias = sb("z_bias", [P, 8])

        dev = sb("dev", [P, 512])
        sq = sb("sq", [P, 512])
        rstd = sb("rstd", [P, L])
        xn = sb("xn", [P, HALVES, L])
        at_dev, at_sq = region4[:, 0:512], region4[:, 512:1024]
        at_xn = region4[:, 1024:1536].rearrange("p (e l) -> p e l", e=HALVES)
        at_rstd = region4[:, 1536:1792]
        logit = sb("logit", [P, 2, 16])
        top = sb("top", [P, 2, E])
        top_i = sb("top_i", [P, 2, E], U32)
        top_f = sb("top_f", [P, 2, E])
        filler = sb("filler", [P, 1])
        gap = sb("gap", [P, 2, 1])
        egap = sb("egap", [P, 2, 1])
        sg = sb("sg", [P, 2, 1])
        w12 = sb("w12", [P, 2, 2])
        cm = sb("cm", [P, 2, 32])
        cm_b = sb("cm_b", [P, 2, E])
        cm3 = sb("cm3", [P, 2, 3, 32], BF16)
        cmt = sb("cmt", [96, L], BF16)
        th = sb("th", [P, 2, 512])
        h1 = sb("h1", [P, 3, 512])
        cbs = sb("cbs", [P, 2, 512])
        hh = sb("hh", [P, 3, 2, L])
        ctx_b = sb("ctx_b", [P, L])
        mx = sb("mx", [P, 2, NH])
        mrest = sb("mrest", [P, 2, NH])
        mp = sb("mp", [P, 2, 3, NH], BF16)
        mt = sb("mt", [96, L], BF16)
        attn = step
        scratch = nc.dram_tensor("scratch", (3, 2, D, L), BF16, kind="Internal").ap()

        ld_const, ld_front, ld_x, ld_m0, ld_m1, ld_at = (
            sem(n) for n in ("ld_const", "ld_front", "ld_x", "ld_m0", "ld_m1", "ld_at"))
        dve_front, act_front, pool_front = sem("dve_front"), sem("act_front"), sem("pool_front")
        dve_0, act_0, pool_0 = sem("dve_0"), sem("act_0"), sem("pool_0")
        dve_a, act_a, pool_a = sem("dve_a"), sem("act_a"), sem("pool_a")
        dve_z, act_z, pool_z = sem("dve_z"), sem("act_z"), sem("pool_z")
        dve_b, act_b, pool_b = sem("dve_b"), sem("act_b"), sem("pool_b")
        dve_y, act_y = sem("dve_y"), sem("act_y")
        memset_done, xin_ready, xin_copied, conv_ready, u_ready = (
            sem(n) for n in ("memset_done", "xin_ready", "xin_copied", "conv_ready", "u_ready"))
        bc_proj_ready, dtlo_ready, dtlo_copied, dt_ready = (
            sem(n) for n in ("bc_proj_ready", "dtlo_ready", "dtlo_copied", "dt_ready"))
        soft_in, w_ready, ln_ready, zstat_ready, zrstd_ready, zbias_ready, ygate_raw = (
            sem(n) for n in ("soft_in", "w_ready", "ln_ready", "zstat_ready", "zrstd_ready", "zbias_ready",
                             "ygate_raw"))
        a_exp, front_dve, front_pool, ang_ready, gate_ready, bc3_ready = (
            sem(n) for n in ("a_exp", "front_dve", "front_pool", "ang_ready", "gate_ready",
                             "bc3_ready"))
        step_ready, da_ready, bc_ready, dbu_done, scan_done, hc_ready, hc_used, acc_used = (
            sem(n) for n in ("step_ready", "da_ready", "bc_ready", "dbu_done", "scan_done", "hc_ready", "hc_used",
                             "acc_used"))
        x_ready = {k: sem(f"x_ready_{k}") for k in ("m0", "at", "m1", "out")}
        norm = {k: {n: sem(f"{n}_{k}") for n in ("mean_ready", "dev_ready", "sq_ready", "var_ready",
                                                 "rstd_ready", "xn_ready")} for k in ("m0", "at", "m1")}
        moe = {k: {n: sem(f"{n}_{k}") for n in (
            "logits_ready", "gap_ready", "egap_ready", "cm_ready", "cmt_ready", "cmt_copied", "gu_ready",
            "tanh_ready", "h1_ready", "cb_ready", "cb_copied", "h_ready", "h_used")}
            for k in ("m0", "m1")}
        (ctx_copied, qk_ready, v_ready, v_copied, rope_read, parts_ready, parts_stored, stacks_ready,
         s1_ready, max_done, mp_ready, mt_ready, mt_copied, rows_ready, s2_ready, exp_done, pv_done,
         attn_ready, o_ready, vpad_zero, stacks_used) = (sem(n) for n in (
            "ctx_copied", "qk_ready", "v_ready", "v_copied", "rope_read", "parts_ready", "parts_stored",
            "stacks_ready", "s1_ready", "max_done", "mp_ready", "mt_ready", "mt_copied", "rows_ready",
            "s2_ready", "exp_done", "pv_done", "attn_ready", "o_ready", "vpad_zero", "stacks_used"))
        stored = sem("stored")
        block = ctx.enter_context(nc.Block())

        N_CONST = 2

        def wait(e, s, value):
            if isinstance(value, int):
                if value > 0:
                    e.wait_ge(s, value)
                return
            e.wait_ge(s, value)
            e.wait_ge(ld_const, 16 * N_CONST)

        class Chain:

            def __init__(self, e, s, base=0):
                self.e, self.s, self.base, self.n, self.marks = e, s, base, 0, []

            def then(self, ins, s=None, value=None):
                if s is None:
                    self.n += 1
                    s, value = self.s, self.base + self.n
                self.marks.append((s, value))
                ins.then_inc(s, 1)

            def behind(self, lag=0):
                if len(self.marks) > lag:
                    wait(self.e, *self.marks[-1 - lag])

            def close(self, per=None):
                assert per is None or self.n == per, (self.n, per)
                self.behind()

        MOE = {
            "m0": dict(T=T0, gu=w_gu0, down=w_down0, route=w_route0, nr=E + 1, pick=pick0, gate=2,
                       second=range(0, 99, 2), nxt="at"),
            "m1": dict(T=T1, gu=w_gu1, down=w_down1, route=w_route1, nr=E, pick=pick1, gate=3,
                       second=(1,), nxt="out"),
        }
        MOE["m0 last"] = dict(MOE["m0"], second=(1,))
        for m in MOE.values():
            m["NP"] = -(-m["T"] // 2)
            m["banks"] = [(2, 3) if p in m["second"] else (4, 5) for p in range(m["NP"])]
        moe["m0 last"], norm["m0 last"], x_ready["m0 last"] = moe["m0"], norm["m0"], x_ready["m0"]
        NORM = {k: (dev, sq, rstd, xn) for k in MOE}
        NORM["at"] = (at_dev, at_sq, at_rstd, at_xn)

        def bank_before(k, p):
            banks = MOE[k]["banks"]
            return max((q for q in range(p) if banks[q] == banks[p]), default=None)

        STEPS = {"m0 last": {"stacks": (1, 2, 3), "head5": (4,), "head12": (5,), "head19": (6,), "head26": (7,),
                             "rows": (8, 9), "group0": (10,)},
                 "m1": {"stacks": (1, 2), "head8": (3,), "head16": (4,), "head22": (5,),
                        "rows": (6,), "group0": (7,)}}
        PIECES = {"m0 last": {h: (st, n) for st in (4, 5, 6, 7)
                              for n, h in enumerate((7 * st - 26, 7 * st - 24, 7 * st - 22))},
                  "m1": {3: (3, 0), 5: (3, 1), 7: (3, 2), 11: (4, 0), 13: (4, 1), 15: (4, 2), 18: (5, 0),
                         21: (5, 2)}}
        FRONT = {"group0": 0, "group1": 1, "group3": 2, "group5": 3}
        FRONT_BANKS = {True: (bank[2], bank[0], bank[1]), False: (bank[6], bank[4], bank[5])}
        CB, Y = bank[6], bank[7]

        @block.sync
        def _(sp):
            sp.dma_start(w_in[:, :], in_proj).then_inc(ld_front, 16)
            sp.dma_start(ctx_all[:, :, :], ctx_t).then_inc(ld_front, 16)
            sp.dma_start(w_conv[:, :, :], conv_w).then_inc(ld_front, 16)
            sp.dma_start(b_conv[:, :], conv_b).then_inc(ld_front, 16)
            sp.dma_start(w_bc[:, :, :], bc_proj).then_inc(ld_front, 16)
            sp.dma_start(w_dtlo[:, :, :], dt_lo_proj).then_inc(ld_front, 16)
            sp.dma_start(w_dt[:, :], dt_proj).then_inc(ld_front, 16)
            sp.dma_start(b_dt[:, :], dt_b).then_inc(ld_front, 16)
            sp.dma_start(a_col[:, :, :], a_log).then_inc(ld_front, 16)
            sp.dma_start(d_col[:, :], d_skip).then_inc(ld_front, 16)
            sp.dma_start(xres[:, :, :], x_t).then_inc(ld_x, 16)
            sp.dma_start(pick_state, sel_state).then_inc(ld_x, 16)
            sp.dma_start(ident_b[:, :], ident).then_inc(ld_m0, 16)
            sp.dma_start(w_gu0[:, :, :, :, :], gu0).then_inc(ld_m0, 16)
            sp.dma_start(w_route0[:, :, :], route0).then_inc(ld_m0, 16)
            sp.dma_start(pick0[:, :, :], sel0).then_inc(ld_m0, 16)
            sp.dma_start(w_down0[:, :, :], down0).then_inc(ld_m0, 16)
            sp.dma_start(iota[:, :], iota8).then_inc(ld_m0, 16)
            for to, of in ((w_q[:, :, :], wq), (w_qs[:, :, :], wq_swap), (w_k[:, :], wk),
                           (w_ks[:, :], wk_swap), (w_v[:, :], wv), (w_out[:, :, :], wout),
                           (b_out[:, :], bout)):
                sp.dma_start(to, of).then_inc(ld_at, 16)

            def store(b):
                wait(sp, parts_ready, b + 1)
                sp.dma_start(scratch.rearrange("i s (t p) l -> p i s t l", p=P),
                             parts[:, :, :].rearrange("p i (s t l) -> p i s t l", s=2, t=2)
                             ).then_inc(parts_stored, 16)
                wait(sp, parts_stored, 16 * b + 16)

            def stack(b):
                for j in range(3):
                    for i in range(3):
                        r = j * 24 + i * 8
                        sp.dma_start(q_stack[r:r + 8, :, :],
                                     scratch[i, 0].rearrange("(h d) l -> d h l", d=HD)
                                     ).then_inc(stacks_ready, 16)
                        sp.dma_start(k_stack[r:r + 8, :, :],
                                     scratch[j, 1].rearrange("(h d) l -> d h l", d=HD)
                                     ).then_inc(stacks_ready, 16)
                wait(sp, mt_copied, b + 1)
                for s in range(3):
                    sp.dma_start(q_stack[STACK + s:STACK + s + 1, :, :], mt[32 * s:32 * s + 32, :]
                                 ).then_inc(rows_ready, 16)

            sp.wait_ge(vpad_zero, 2)
            store(0)
            stack(0)
            sp.wait_ge(x_ready["at"], NB)
            for to, of in ((w_gu1, gu1), (w_down1, down1),
                           (w_route1[:, :, :], route1), (pick1[:, :, :], sel1)):
                sp.dma_start(to, of).then_inc(ld_m1, 16)
            with sp.Fori(0, NB - 1) as i:
                store(i + 1)
                wait(sp, stacks_used, i + 1)
                stack(i + 1)
                wait(sp, x_ready["out"], i + 1)
                sp.dma_start(out[:, i, :], xres[:, i, :]).then_inc(stored, 16)
            sp.wait_ge(x_ready["out"], NB)
            sp.dma_start(out[:, NB - 1, :], xres[:, NB - 1, :]).then_inc(stored, 16)
            sp.wait_ge(stored, 16 * NB)

        @block.gpsimd
        def _(pool):
            pool.memset(region[:, 0:HALVES * NB * (L + 3)].rearrange("p (g l) -> p g l", l=L + 3)[:, :, 0:3],
                        0.0).then_inc(memset_done, 1)
            pool.memset(mean_w[:, :], 1.0 / D).then_inc(memset_done, 1)
            pool.memset(ones_pad[:, :, :], 0.0).then_inc(memset_done, 1)
            pool.memset(cm[:, :, :], 0.0).then_inc(memset_done, 1)
            pool.wait_ge(memset_done, 4)
            for r in range(4):
                pool.memset(ones_pad[:, r, r * HD:(r + 1) * HD], 1.0).then_inc(memset_done, 1)
            ch = Chain(pool, pool_front)
            pool.wait_ge(ld_const, 16 * N_CONST)
            ang, turns = cos_t[:, :, :], sin_t[:, :, :]
            ch.then(pool.tensor_scalar(ang, ang, col[:, 2:3], None, ALU.mult))
            ch.behind()
            ch.then(pool.tensor_scalar(turns, ang, 1.0 / (TWO_PI_HI + TWO_PI_LO), ROUND, ALU.mult, ALU.add))
            ch.behind()
            ch.then(pool.tensor_scalar(turns, turns, ROUND, None, ALU.subtract))
            t3 = h1[:, 0:2, :].rearrange("p a n -> p (a n)").rearrange("p (b l) -> p b l", b=NB)
            for part in (TWO_PI_HI, TWO_PI_LO):
                ch.behind()
                ch.then(pool.tensor_scalar(t3, turns, part, None, ALU.mult))
                ch.behind()
                ch.then(pool.tensor_tensor(ang, ang, t3, ALU.subtract))
            ch.behind()
            ch.then(pool.tensor_copy(t3, ang), ang_ready, 1)
            pool.wait_ge(ygate_raw, 8)
            pool.wait_ge(gate_ready, 1)
            ch.behind()
            ch.then(pool.tensor_scalar(ygate[:, :, :], ygate[:, :, :], gate[:, 0:1], None, ALU.mult))
            pool.wait_ge(u_ready, 2)
            pool.wait_ge(ld_x, 32)
            pool.wait_ge(front_dve, 1)
            for e in range(2):
                ch.behind()
                ch.then(pool.tensor_scalar(tmp[:, :, e * L:(e + 1) * L], u_all[:, :, e * L:(e + 1) * L],
                                           d_col[:, e:e + 1], None, ALU.mult))
            ch.behind()
            ch.then(pool.tensor_tensor(tmp, tmp, ygate[:, :, :], ALU.mult))
            ch.behind()
            ch.then(pool.tensor_tensor(xres[:, :, :], xres[:, :, :], tmp, ALU.add), front_pool, 1)

            def mixer_group(ch, b, g):
                if g == 0:
                    wait(pool, acc_used, b)
                wait(pool, hc_ready, GROUPS * b + g + 1)
                ch.behind()
                if g == 0:
                    ch.then(pool.tensor_tensor(acc, hc[:, g % 2, 0, :], hc[:, g % 2, 1, :], ALU.add)
                            , hc_used, GROUPS * b + g + 1)
                else:
                    ch.then(pool.tensor_tensor(acc, acc, hc[:, g % 2, 0, :], ALU.add))
                    ch.behind()
                    ch.then(pool.tensor_tensor(acc, acc, hc[:, g % 2, 1, :], ALU.add), hc_used, GROUPS * b + g + 1)

            def expert_pair(ch, k, b, p):
                m, s = MOE[k], moe[k]
                n = min(2, m["T"] - 2 * p) * L
                wait(pool, s["h1_ready"], m["NP"] * b + p + 1)
                wait(pool, s["cb_copied"], m["NP"] * b + p + 1)
                if p >= 3:
                    wait(pool, s["h_used"], m["NP"] * b + p - 2)
                ch.behind(2)
                ch.then(pool.tensor_tensor(hh[:, p % 3, 0:n // L, :].rearrange("p a l -> p (a l)"),
                                           h1[:, p % 3, 0:n], cbs[:, p % 2, 0:n], ALU.mult)
                        , s["h_ready"], m["NP"] * b + p + 1)

            ch.close()
            ch = Chain(pool, pool_0)
            for g in range(GROUPS):
                mixer_group(ch, 0, g)
            ch.close()
            with pool.Fori(0, NB - 1) as i:
                ch = Chain(pool, pool_a, i * CHAIN["POOL_A"])
                for slot in range(12):
                    if slot < GROUPS:
                        mixer_group(ch, i + 1, slot)
                    if slot >= 3:
                        expert_pair(ch, "m0", i, slot - 3)
                ch.close(CHAIN["POOL_A"])
            pool.wait_ge(x_ready["m0"], NB)
            pool.memset(v_pad, 0.0).then_inc(vpad_zero, 1)
            pool.wait_ge(vpad_zero, 1)
            pool.memset(k_stack[64:96, :, :], 1.0).then_inc(vpad_zero, 1)
            pool.wait_ge(vpad_zero, 2)
            ch = Chain(pool, pool_z)
            for p in range(MOE["m0"]["NP"]):
                expert_pair(ch, "m0 last", NB - 1, p)
            ch.close()
            with pool.Fori(0, NB) as b:
                ch = Chain(pool, pool_b, b * CHAIN["POOL_B"])
                for p in range(MOE["m1"]["NP"]):
                    expert_pair(ch, "m1", b, p)
                ch.close(CHAIN["POOL_B"])

        @block.scalar
        def _(act):
            act.dma_start(col[:, :], columns).then_inc(ld_const, 16)
            act.dma_start(cos_t[:, :, :], pos).then_inc(ld_const, 16)
            act.dma_start(x_nat, x_rows).then_inc(ld_front, 16)
            act.dma_start(gate_raw[:, :], gates).then_inc(ld_front, 16)
            ch = Chain(act, act_front)
            act.wait_ge(ld_const, 32)
            for e in range(2):
                for q in range(2):
                    n = 2 * e + q
                    act.wait_ge(xin_ready, n + 1)
                    ch.then(act.activation(xpad[:, e, 2 * q:2 * q + 2, 3:3 + L],
                                           bank[n][:, :].rearrange("p (b l) -> p b l", b=2),
                                           ACT.Copy), xin_copied, n + 1)
            act.wait_ge(zstat_ready, 1)
            act.wait_ge(ld_front, 16 * 12)
            ch.then(act.activation(z_scale[:, :], mv[:, :, 1], ACT.Ln, bias=col[:, 0:1]))
            ch.behind()
            ch.then(act.activation(z_scale[:, :], z_scale[:, :], ACT.Exp, scale=-0.5), zrstd_ready, 1)
            ch.then(act.activation(a_col[:, :, :], a_col[:, :, :], ACT.Exp), a_exp, 1)
            for e in range(2):
                act.wait_ge(conv_ready, e + 1)
                ch.then(act.activation(u_all[:, :, e * L:(e + 1) * L], tmp[:, :, e * L:(e + 1) * L], ACT.Silu,
                                       bias=b_conv[:, e:e + 1]), u_ready, e + 1)
            act.wait_ge(zbias_ready, 1)
            for n in range(8):
                b, e = n // 2, n % 2
                ch.then(act.activation(ygate[:, b, e * L:(e + 1) * L], x_nat[:, b, e, :], ACT.Silu,
                                       bias=z_bias[:, n:n + 1], scale=z_scale[:, n:n + 1])
                        , ygate_raw, n + 1)
            ch.then(act.activation(gate[:, :], gate_raw[:, :], ACT.Tanh), gate_ready, 1)
            act.wait_ge(ang_ready, 1)
            t3 = h1[:, 0:2, :].rearrange("p a n -> p (a n)").rearrange("p (b l) -> p b l", b=NB)
            ch.then(act.activation(sin_t[:, :, :], t3, ACT.Sin, scale=col[:, 3:4]))
            ch.then(act.activation(cos_t[:, :, :], t3, ACT.Abs))
            ch.behind()
            ch.then(act.activation(cos_t[:, :, :], cos_t[:, :, :], ACT.Sin, bias=col[:, 1:2], scale=-1.0))
            act.wait_ge(dtlo_ready, 1)
            for q in range(2):
                ch.then(act.activation(dt_lo[:, 512 * q:512 * q + 512], bank[4 + q][0:DR, :], ACT.Copy)
                        , dtlo_copied, q + 1)
            for e in range(2):
                for q in range(2):
                    n = 2 * e + q
                    act.wait_ge(dt_ready, n + 1)
                    ch.behind()
                    ch.then(act.activation(delta[:, 2 * q:2 * q + 2, e, :],
                                           bank[n][:, :].rearrange("p (b l) -> p b l", b=2), ACT.Identity,
                                           bias=b_dt[:, e:e + 1]))
            dl = delta[:, :, :, :].rearrange("p b e l -> p (b e l)")
            t1 = tmp.rearrange("p b n -> p (b n)")
            t2 = tmp2.rearrange("p b n -> p (b n)")
            ch.behind()
            ch.then(act.activation(t2, dl, ACT.Abs))
            ch.behind()
            ch.then(act.activation(t2, t2, ACT.Exp, scale=-1.0), soft_in, 1)
            act.wait_ge(w_ready, 1)
            ch.then(act.activation(t1, xpad_flat(region), ACT.Ln), ln_ready, 1)

            def mixer_decay(ch, b, g):
                wait(act, scan_done, GROUPS * b + g - 1)
                if g == 0:
                    wait(act, step_ready, b + 1)
                for j in range(2):
                    for e in range(2):
                        n = 2 * g + j
                        ins = act.activation(da[:, g % 2, j, e, 1:L], step[:, e, 1:L], ACT.Exp,
                                             scale=a_col[:, e, n:n + 1])
                        ch.then(ins, *((da_ready, GROUPS * b + g + 1) if j and e else ()))

            def norm_square(ch, k, b):
                dev, sq, _, _ = NORM[k]
                wait(act, norm[k]["dev_ready"], b + 1)
                ch.behind()
                ch.then(act.activation(sq[:, :], dev[:, :], ACT.Square), norm[k]["sq_ready"], b + 1)

            def norm_rstd(ch, pairs):
                for k, b, at in pairs:
                    wait(act, norm[k]["var_ready"], b + 1)
                    ch.then(act.activation(NORM[k][2][:, :], at[:, L:2 * L], ACT.Ln, bias=col[:, 0:1]))
                for k, b, at in pairs:
                    rstd = NORM[k][2]
                    ch.behind(len(pairs) - 1)
                    ch.then(act.activation(rstd[:, :], rstd[:, :], ACT.Exp, scale=-0.5)
                            , norm[k]["rstd_ready"], b + 1)

            def route_exp(ch, k, b):
                wait(act, moe[k]["gap_ready"], b + 1)
                if MOE[k]["nr"] > E:
                    ch.then(act.activation(sg[:, :, :], logit[:, :, E:E + 1], ACT.Tanh, scale=0.5))
                ch.then(act.activation(egap[:, :, :], gap[:, :, :], ACT.Exp)
                        , moe[k]["egap_ready"], b + 1)

            def route_copy(ch, k, b):
                wait(act, moe[k]["cmt_ready"], b + 1)
                ch.then(act.activation(cmt[:, :], CB[0:96, L:2 * L], ACT.Copy)
                        , moe[k]["cmt_copied"], b + 1)

            def expert_tanh(ch, k, b, p):
                m, s = MOE[k], moe[k]
                n = min(2, m["T"] - 2 * p) * L
                wait(act, s["gu_ready"], m["NP"] * b + p + 1)
                if p >= 2:
                    wait(act, s["h1_ready"], m["NP"] * b + p - 1)
                ch.behind(1)
                ch.then(act.activation(th[:, p % 2, 0:n], bank[m["banks"][p][0]][:, 0:n],
                                       ACT.Tanh, scale=0.5), s["tanh_ready"], m["NP"] * b + p + 1)

            def expert_weight(ch, k, b, p):
                m, s = MOE[k], moe[k]
                n = min(2, m["T"] - 2 * p) * L
                wait(act, s["cb_ready"], m["NP"] * b + p + 1)
                if p >= 2:
                    wait(act, s["h_ready"], m["NP"] * b + p - 1)
                ch.behind(1)
                ch.then(act.activation(cbs[:, p % 2, 0:n], CB[:, 0:n], ACT.Copy), s["cb_copied"], m["NP"] * b + p + 1)

            act.wait_ge(front_dve, 1)
            ch.close()
            ch = Chain(act, act_0)
            for g in range(GROUPS):
                mixer_decay(ch, 0, g)

            def turn_a(ch, i, mixer):
                for slot in range(12):
                    if mixer and slot == 0:
                        mixer_decay(ch, i + 1, 0)
                    if mixer and slot + 1 < GROUPS:
                        mixer_decay(ch, i + 1, slot + 1)
                    if slot == 0:
                        norm_square(ch, "m0", i)
                    elif slot == 1:
                        norm_rstd(ch, [("m0", i, CB)])
                    elif slot == 2:
                        route_exp(ch, "m0", i)
                    elif slot == 3:
                        route_copy(ch, "m0", i)
                    if 2 <= slot < 11:
                        expert_tanh(ch, "m0", i, slot - 2)
                    if slot >= 3:
                        expert_weight(ch, "m0", i, slot - 3)

            ch.close()
            with act.Fori(0, NB - 1) as i:
                ch = Chain(act, act_a, i * CHAIN["ACT_A"])
                turn_a(ch, i, True)
                ch.close(CHAIN["ACT_A"])

            def expert_step(ch, k, b, stage_no):
                if stage_no < MOE[k]["NP"]:
                    expert_tanh(ch, k, b, stage_no)
                if stage_no == 1:
                    route_copy(ch, k, b)
                if 1 <= stage_no <= MOE[k]["NP"]:
                    expert_weight(ch, k, b, stage_no - 1)

            def front_step(ch, b, n, first):
                if n == 0:
                    wait(act, v_copied, b)
                    ch.then(act.activation(ctx_b[:, :], ctx_all[:, b, :], ACT.Copy), ctx_copied, b + 1)
                    norm_square(ch, "at", b)
                elif n == 1:
                    norm_rstd(ch, [("at", b, FRONT_BANKS[first][0])])

            def turn_b(ch, k, bm, ba, first=False, ahead=True):
                def experts(stage):
                    for stage_no in STEPS[k].get(stage, ()):
                        expert_step(ch, k, bm, stage_no)

                if first:
                    for n in range(2):
                        front_step(ch, 0, n, True)
                norm_square(ch, k, bm)
                norm_rstd(ch, [(k, bm, CB)])
                route_exp(ch, k, bm)
                expert_step(ch, k, bm, 0)
                wait(act, v_ready, ba + 1)
                for r in range(4):
                    for t in range(2):
                        ins = act.activation(
                            v_pad[:, t, :, :].rearrange("p (g r) c -> p g r c", r=4)[:, :, r, r * HD:(r + 1) * HD],
                            bank[1][:, t * L:(t + 1) * L].rearrange("p (g r d) -> p g r d", g=NH // 4,
                                                                    r=4)[:, :, r, :], ACT.Copy)
                        ch.then(ins, *((v_copied, ba + 1) if r == 3 and t == 1 else ()))
                experts("stacks")
                for h in range(NH):
                    experts(f"head{h}")
                wait(act, mt_ready, ba + 1)
                ch.then(act.activation(mt[:, :], bank[2][0:96, 0:L], ACT.Copy), mt_copied, ba + 1)
                experts("rows")
                for g in range(8):
                    for s in range(4):
                        n = 4 * g + s
                        wait(act, s2_ready, NH * ba + n + 1)
                        if s == 0 and g >= 2:
                            wait(act, pv_done, 8 * ba + g - 1)
                        ch.behind(2)
                        ch.then(act.activation(p_exp[:, g % 2, s, :, :],
                                               bank[n % 2][:, :].rearrange("p (k l) -> p k l", k=2), ACT.Exp,
                                               scale=SCALE), exp_done, NH * ba + n + 1)
                    experts(f"group{g}")
                    if ahead and f"group{g}" in FRONT:
                        front_step(ch, ba + 1, FRONT[f"group{g}"], False)

            ch.close()
            act.wait_ge(vpad_zero, 2)
            ch = Chain(act, act_z)
            turn_b(ch, "m0 last", NB - 1, 0, first=True)
            ch.close()
            with act.Fori(0, NB - 2) as i:
                ch = Chain(act, act_b, i * CHAIN["ACT_B"])
                turn_b(ch, "m1", i, i + 1)
                ch.close(CHAIN["ACT_B"])
            ch = Chain(act, act_y)
            turn_b(ch, "m1", NB - 2, NB - 1, ahead=False)
            norm_square(ch, "m1", NB - 1)
            norm_rstd(ch, [("m1", NB - 1, CB)])
            route_exp(ch, "m1", NB - 1)
            for stage_no in range(MOE["m1"]["NP"] + 1):
                expert_step(ch, "m1", NB - 1, stage_no)

        @block.vector
        def _(dve):
            ch = Chain(dve, dve_front)
            dve.wait_ge(ld_front, 16 * 12)
            for n in range(8):
                ch.then(dve.bn_stats(stats[:, n, :], x_nat[:, n // 2, n % 2, :]))
            ch.behind()
            for n in range(8):
                ch.then(dve.bn_aggr(mv[:, n, :], stats[:, n, :]), *((zstat_ready, 1) if n == 7 else ()))
            for e in range(2):
                dve.wait_ge(xin_copied, 2 * e + 2)
                dve.wait_ge(memset_done, 8)
                dst = tmp[:, :, e * L:(e + 1) * L]
                for k in range(TAPS):
                    src = xpad[:, e, :, k:k + L]
                    ch.behind()
                    if k == 0:
                        ch.then(dve.tensor_scalar(dst, src, w_conv[:, e, k:k + 1], None, ALU.mult))
                    else:
                        ins = dve.scalar_tensor_tensor(dst, src, w_conv[:, e, k:k + 1], dst, ALU.mult, ALU.add)
                        ch.then(ins, *((conv_ready, e + 1) if k == TAPS - 1 else ()))
            dve.wait_ge(zrstd_ready, 1)
            ch.behind()
            ch.then(dve.scalar_tensor_tensor(z_bias[:, :], mv[:, :, 0], -1.0, z_scale[:, :],
                                             ALU.mult, ALU.mult), zbias_ready, 1)
            dve.wait_ge(a_exp, 1)
            ch.then(dve.tensor_scalar(a_col[:, :, :], a_col[:, :, :], -1.0, None, ALU.mult))
            dve.wait_ge(bc_proj_ready, 1)
            for q in range(2):
                cols = slice(512 * q, 512 * q + 512)
                src, rest, to = bank[6 + q], bc_rest[:, cols], bc3[:, cols]
                ch.behind()
                ch.then(dve.tensor_copy(to, src[0:96, :]))
                ch.behind()
                ch.then(dve.tensor_tensor(rest, src[0:96, :], to, ALU.subtract))
                ch.behind()
                for strip in ((32, 64), (64, 96)):
                    ch.then(dve.tensor_copy(bc3[strip[0]:strip[1], cols], bc_rest[strip[0]:strip[1], cols]))
                ch.behind()
                ch.then(dve.tensor_tensor(bc_rest[64:96, cols], bc_rest[64:96, cols], bc3[64:96, cols],
                                          ALU.subtract))
                ch.behind()
                ch.then(dve.tensor_copy(bc3[64:96, cols], bc_rest[64:96, cols]), bc3_ready, q + 1)
            dve.wait_ge(gate_ready, 1)
            ch.then(dve.tensor_scalar(half_gate[:, :], gate[:, :], 0.5, None, ALU.mult))
            dl = delta[:, :, :, :].rearrange("p b e l -> p (b e l)")
            t1 = tmp.rearrange("p b n -> p (b n)")
            t2 = tmp2.rearrange("p b n -> p (b n)")
            w1 = xpad_flat(region)
            dve.wait_ge(soft_in, 1)
            dve.wait_ge(u_ready, 2)
            ch.behind()
            ch.then(dve.tensor_scalar(w1, t2, 1.0, None, ALU.add), w_ready, 1)
            ch.behind()
            ch.then(dve.scalar_tensor_tensor(t2, w1, 1.0, t2, ALU.subtract, ALU.subtract))
            dve.wait_ge(ln_ready, 1)
            ch.behind()
            ch.then(dve.scalar_tensor_tensor(dl, dl, 0.0, t1, ALU.max, ALU.add))
            ch.behind()
            ch.then(dve.tensor_tensor(dl, dl, t2, ALU.subtract))
            ch.behind()
            ch.then(dve.tensor_tensor(du[:, :, :], delta[:, :, :, :].rearrange("p b e l -> p b (e l)"),
                                      u_all, ALU.mult))
            dve.wait_ge(ygate_raw, 8)
            dve.wait_ge(dt_ready, 4)
            ch.then(dve.memset(da[:, :, :, :, 0:1].rearrange("p r j e l -> p (r j e) l"), 0.0)
                    , front_dve, 1)

            def mixer_step(ch, b):
                ch.behind()
                ch.then(dve.tensor_scalar(step[:, :, :].rearrange("p e l -> p (e l)"),
                                          delta[:, b, :, :].rearrange("p e l -> p (e l)"), 1.0, None,
                                          ALU.mult), step_ready, b + 1)

            def mixer_group(ch, b, g):
                wait(dve, bc_ready, GROUPS * b + g + 1)
                ch.behind(1)
                ch.then(dve.tensor_tensor(
                    dbu.rearrange("p (j e l) -> p j e l", j=2, e=2),
                    du[:, b, :].rearrange("p (e l) -> p e l", e=2).unsqueeze(1).broadcast_to([P, 2, 2, L]),
                    bank[0][:, :].rearrange("p (j l) -> p j l", j=2).unsqueeze(2).broadcast_to([P, 2, 2, L]),
                    ALU.mult), dbu_done, GROUPS * b + g + 1)
                wait(dve, da_ready, GROUPS * b + g + 1)
                ch.behind()
                ch.then(dve.tensor_tensor_scan(
                    states, da[:, g % 2, :, :, :].rearrange("p j e l -> p (j e l)"), dbu, 0.0,
                    ALU.mult, ALU.add), scan_done, GROUPS * b + g + 1)
                wait(dve, hc_used, GROUPS * b + g - 1)
                ch.behind()
                ch.then(dve.tensor_tensor(
                    hc[:, g % 2, :, :].rearrange("p j (e l) -> p j e l", e=2),
                    states.rearrange("p (j e l) -> p j e l", j=2, e=2),
                    bank[1][:, :].rearrange("p (j l) -> p j l", j=2).unsqueeze(2).broadcast_to([P, 2, 2, L]),
                    ALU.mult), hc_ready, GROUPS * b + g + 1)

            def mixer_end(ch, b):
                wait(dve, hc_used, GROUPS * b + GROUPS)
                ch.behind()
                ch.then(dve.tensor_tensor(dev[:, :], acc, ygate[:, b, :], ALU.mult), acc_used, b + 1)
                ch.behind()
                ch.then(dve.tensor_tensor(xres[:, b, :], xres[:, b, :], dev[:, :], ALU.add)
                        , x_ready["m0"], b + 1)

            def norm_dev(ch, k, b, at):
                dev = NORM[k][0]
                wait(dve, norm[k]["mean_ready"], b + 1)
                ch.behind()
                ch.then(dve.tensor_tensor(
                    dev[:, :].rearrange("p (e l) -> p e l", e=2),
                    xres[:, b, :].rearrange("p (e l) -> p e l", e=2),
                    at[:, 0:L].unsqueeze(1).broadcast_to([P, 2, L]), ALU.subtract)
                , norm[k]["dev_ready"], b + 1)

            def norm_scale(ch, k, b):
                dev, _, rstd, xn = NORM[k]
                wait(dve, norm[k]["rstd_ready"], b + 1)
                ch.behind()
                ch.then(dve.tensor_tensor(
                    xn[:, :, :], dev[:, :].rearrange("p (e l) -> p e l", e=2),
                    rstd[:, :].unsqueeze(1).broadcast_to([P, 2, L]), ALU.mult)
                , norm[k]["xn_ready"], b + 1)

            def route_top(ch, k, b):
                nr = MOE[k]["nr"]
                wait(dve, moe[k]["logits_ready"], b + 1)
                ch.behind()
                ch.then(dve.tensor_copy(logit[:, :, 0:nr],
                                        CB[:, 0:32].rearrange("p (t n) -> p t n", t=2)[:, :, 0:nr]))
                ch.behind()
                ch.then(dve.memset(filler[:, :], 0.0))
                for t in range(2):
                    ch.then(dve.max(top[:, t, :], logit[:, t, 0:E]))
                ch.behind()
                ch.then(dve.tensor_tensor(gap[:, :, :], top[:, :, 1:2], top[:, :, 0:1], ALU.subtract)
                        , moe[k]["gap_ready"], b + 1)
                for t in range(2):
                    ch.then(dve.max_index(top_i[:, t, :], top[:, t, :], logit[:, t, 0:E]))
                ch.behind()
                ch.then(dve.tensor_copy(top_f[:, :, :], top_i[:, :, :]))

            def route_weights(ch, k, b):
                wait(dve, moe[k]["egap_ready"], b + 1)
                ch.behind()
                ch.then(dve.tensor_scalar(w12[:, :, 0:1], egap[:, :, :], 1.0, None, ALU.add))
                ch.behind()
                ch.then(dve.reciprocal(w12[:, :, 0:1], w12[:, :, 0:1]))
                ch.behind()
                ch.then(dve.tensor_tensor(w12[:, :, 1:2], egap[:, :, :], w12[:, :, 0:1], ALU.mult))
                ch.behind()
                for t in range(2):
                    ch.then(dve.tensor_scalar(cm[:, t, 0:E], iota[:, :], top_f[:, t, 0:1], w12[:, t, 0:1],
                                              ALU.is_equal, ALU.mult))
                for t in range(2):
                    ch.then(dve.tensor_scalar(cm_b[:, t, :], iota[:, :], top_f[:, t, 1:2], w12[:, t, 1:2],
                                              ALU.is_equal, ALU.mult))
                ch.behind()
                ch.then(dve.tensor_tensor(cm[:, :, 0:E], cm[:, :, 0:E], cm_b[:, :, :], ALU.add))
                if MOE[k]["nr"] > E:
                    ch.then(dve.tensor_scalar(cm[:, :, E:E + 1], sg[:, :, :], 0.5, 0.5, ALU.mult, ALU.add))
                ch.behind()
                ch.then(dve.tensor_copy(cm3[:, :, 0, :], cm[:, :, :]))
                ch.behind()
                ch.then(dve.tensor_tensor(cm[:, :, :], cm[:, :, :], cm3[:, :, 0, :], ALU.subtract))
                ch.behind()
                ch.then(dve.tensor_copy(cm3[:, :, 1, :], cm[:, :, :]))
                ch.behind()
                ch.then(dve.tensor_tensor(cm3[:, :, 2, :], cm[:, :, :], cm3[:, :, 1, :], ALU.subtract)
                        , moe[k]["cm_ready"], b + 1)

            def expert_pair(ch, k, b, p):
                m, s = MOE[k], moe[k]
                n = min(2, m["T"] - 2 * p) * L
                gb, ub = m["banks"][p]
                wait(dve, s["tanh_ready"], m["NP"] * b + p + 1)
                ch.behind(1)
                ch.then(dve.scalar_tensor_tensor(th[:, p % 2, 0:n], th[:, p % 2, 0:n], 1.0,
                                                 bank[gb][:, 0:n], ALU.add, ALU.mult))
                if p >= 3:
                    wait(dve, s["h_ready"], m["NP"] * b + p - 2)
                ch.behind()
                ch.then(dve.tensor_tensor(h1[:, p % 3, 0:n], th[:, p % 2, 0:n], bank[ub][:, 0:n], ALU.mult)
                        , s["h1_ready"], m["NP"] * b + p + 1)

            def expert_end(ch, k, b):
                m = MOE[k]
                wait(dve, moe[k]["h_used"], m["NP"] * b + m["NP"])
                ch.behind()
                ch.then(dve.scalar_tensor_tensor(xres[:, b, :], Y[:, :], half_gate[:, m["gate"]:m["gate"] + 1],
                                                 xres[:, b, :], ALU.mult, ALU.add)
                        , x_ready[m["nxt"]], b + 1)

            ch.close()
            ch = Chain(dve, dve_0)
            mixer_step(ch, 0)
            for g in range(GROUPS):
                mixer_group(ch, 0, g)
            dve.wait_ge(front_pool, 1)
            mixer_end(ch, 0)
            dve.wait_ge(ld_m0, 16 * 6)

            def turn_a(ch, i, mixer):
                if mixer:
                    mixer_step(ch, i + 1)
                for slot in range(12):
                    if mixer and slot < GROUPS:
                        mixer_group(ch, i + 1, slot)
                    if slot == 0:
                        norm_dev(ch, "m0", i, CB)
                    elif slot == 1:
                        norm_scale(ch, "m0", i)
                    elif slot == 2:
                        route_top(ch, "m0", i)
                    elif slot == 3:
                        route_weights(ch, "m0", i)
                    if 2 <= slot < 11:
                        expert_pair(ch, "m0", i, slot - 2)
                if mixer:
                    mixer_end(ch, i + 1)
                expert_end(ch, "m0", i)

            ch.close()
            with dve.Fori(0, NB - 1) as i:
                ch = Chain(dve, dve_a, i * CHAIN["DVE_A"])
                turn_a(ch, i, True)
                ch.close(CHAIN["DVE_A"])

            def expert_step(ch, k, b, stage_no):
                if stage_no < MOE[k]["NP"]:
                    expert_pair(ch, k, b, stage_no)

            def front_step(ch, b, n, first):
                norm_bank, plain, swapped = FRONT_BANKS[first]
                if n == 0:
                    norm_dev(ch, "at", b, norm_bank)
                elif n == 1:
                    norm_scale(ch, "at", b)
                else:
                    s = n - 2
                    half = slice(512 * s, 512 * s + 512)
                    wait(dve, qk_ready, 2 * b + s + 1)
                    for src, to, table in ((plain, rt1, cos_t), (swapped, rt2, sin_t)):
                        ch.behind()
                        ins = dve.tensor_tensor(
                            to[:, :].rearrange("p (m l) -> p m l", m=2),
                            src[:, :].rearrange("p (m l) -> p m l", m=2),
                            table[:, b, :].unsqueeze(1).broadcast_to([P, 2, L]), ALU.mult)
                        ch.then(ins, *((rope_read, 2 * b + s + 1) if to is rt2 else ()))
                    ch.behind()
                    ch.then(dve.tensor_tensor(qk[:, half], rt1[:, :], rt2[:, :], ALU.add))
                    ch.behind()
                    ch.then(dve.tensor_copy(parts[:, 0, half], qk[:, half]))
                    ch.behind()
                    ch.then(dve.tensor_tensor(qk[:, half], qk[:, half], parts[:, 0, half], ALU.subtract))
                    ch.behind()
                    ch.then(dve.tensor_copy(parts[:, 1, half], qk[:, half]))
                    ch.behind()
                    ins = dve.tensor_tensor(parts[:, 2, half], qk[:, half], parts[:, 1, half], ALU.subtract)
                    ch.then(ins, *((parts_ready, b + 1) if s else ()))

            def softmax_divide(ch, b, half):
                wait(dve, pv_done, 8 * b + 4 * half + 4)
                ch.behind()
                ch.then(dve.reciprocal(rt1[:, 0:L], bank[2 + half][:, L:2 * L]))
                ch.behind()
                ch.then(dve.tensor_tensor(attn[:, half, :], bank[2 + half][:, 0:L], rt1[:, 0:L], ALU.mult)
                        , attn_ready, 2 * b + half + 1)

            def turn_b(ch, k, bm, ba, first=False, ahead=True):
                def experts(stage):
                    for stage_no in STEPS[k].get(stage, ()):
                        expert_step(ch, k, bm, stage_no)

                if first:
                    front_step(ch, 0, 0, True)
                    norm_dev(ch, k, bm, CB)
                    front_step(ch, 0, 1, True)
                    norm_scale(ch, k, bm)
                    front_step(ch, 0, 2, True)
                    route_top(ch, k, bm)
                    front_step(ch, 0, 3, True)
                else:
                    norm_dev(ch, k, bm, CB)
                    norm_scale(ch, k, bm)
                    route_top(ch, k, bm)
                route_weights(ch, k, bm)
                expert_step(ch, k, bm, 0)
                experts("stacks")
                for h in range(NH):
                    wait(dve, s1_ready, NH * ba + h + 1)
                    ch.behind(1)
                    ch.then(dve.tensor_reduce(mx[:, :, h],
                                              bank[h % 4][:, :].rearrange("p (t k) -> p t k", t=2),
                                              AX.X, ALU.max), max_done, NH * ba + h + 1)
                    experts(f"head{h}")
                ch.behind()
                ch.then(dve.tensor_scalar(mp[:, :, 0, :], mx[:, :, :], -1.0, None, ALU.mult))
                ch.behind()
                ch.then(dve.scalar_tensor_tensor(mrest[:, :, :], mx[:, :, :], -1.0, mp[:, :, 0, :],
                                                 ALU.mult, ALU.subtract))
                ch.behind()
                ch.then(dve.tensor_copy(mp[:, :, 1, :], mrest[:, :, :]))
                ch.behind()
                ch.then(dve.tensor_tensor(mp[:, :, 2, :], mrest[:, :, :], mp[:, :, 1, :], ALU.subtract)
                        , mp_ready, ba + 1)
                experts("rows")
                for g in range(8):
                    experts(f"group{g}")
                    if g == 0:
                        expert_end(ch, k, bm)
                    if ahead and f"group{g}" in FRONT:
                        front_step(ch, ba + 1, FRONT[f"group{g}"], False)
                    if g == 4:
                        softmax_divide(ch, ba, 0)
                softmax_divide(ch, ba, 1)
                wait(dve, o_ready, ba + 1)
                ch.behind()
                for e in range(2):
                    ch.then(dve.tensor_scalar(rt2[:, e * L:(e + 1) * L], bank[0][:, e * L:(e + 1) * L],
                                              b_out[:, e:e + 1], gate[:, 1:2], ALU.add, ALU.mult))
                ch.behind()
                ch.then(dve.tensor_tensor(xres[:, ba, :], xres[:, ba, :], rt2[:, :], ALU.add)
                        , x_ready["m1"], ba + 1)

            ch = Chain(dve, dve_z)
            turn_b(ch, "m0 last", NB - 1, 0, first=True)
            ch.close()
            with dve.Fori(0, NB - 2) as i:
                ch = Chain(dve, dve_b, i * CHAIN["DVE_B"])
                turn_b(ch, "m1", i, i + 1)
                ch.close(CHAIN["DVE_B"])
            ch = Chain(dve, dve_y)
            turn_b(ch, "m1", NB - 2, NB - 1, ahead=False)
            norm_dev(ch, "m1", NB - 1, CB)
            norm_scale(ch, "m1", NB - 1)
            route_top(ch, "m1", NB - 1)
            route_weights(ch, "m1", NB - 1)
            for stage_no in range(MOE["m1"]["NP"]):
                expert_step(ch, "m1", NB - 1, stage_no)
            expert_end(ch, "m1", NB - 1)

        @block.tensor
        def _(pe):
            pe.wait_ge(ld_front, 16 * 12)
            for e in range(2):
                for q in range(2):
                    pe.matmul(bank[2 * e + q][:, :], w_in[:, e * P:(e + 1) * P], ctx_all[:, 2 * q:2 * q + 2, :],
                              start=True, stop=True).then_inc(xin_ready, 1)
            pe.wait_ge(u_ready, 2)
            for q in range(2):
                for e in range(2):
                    last = pe.matmul(bank[4 + q][0:DR, :], w_dtlo[:, e, :],
                                     u_all[:, 2 * q:2 * q + 2, e * L:(e + 1) * L], start=(e == 0), stop=(e == 1))
            last.then_inc(dtlo_ready, 1)
            for q in range(2):
                for e in range(2):
                    last = pe.matmul(bank[6 + q][0:96, :], w_bc[:, e, :],
                                     u_all[:, 2 * q:2 * q + 2, e * L:(e + 1) * L], start=(e == 0), stop=(e == 1))
            last.then_inc(bc_proj_ready, 1)
            pe.wait_ge(dtlo_copied, 2)
            for e in range(2):
                for q in range(2):
                    pe.matmul(bank[2 * e + q][:, :], w_dt[:, e * P:(e + 1) * P], dt_lo[:, 512 * q:512 * q + 512],
                              start=True, stop=True).then_inc(dt_ready, 1)

            def mixer_spread(b, g):
                for which, (to, free) in enumerate(((bank[0], dbu_done), (bank[1], hc_ready))):
                    wait(pe, free, GROUPS * b + g)
                    for j in range(2):
                        last = pe.matmul(to[:, j * L:(j + 1) * L], pick_state[:, which * NS + 2 * g + j, :],
                                         bc3[:, bass.ds(b * L, L)], start=True, stop=True)
                last.then_inc(bc_ready, 1)

            def norm_mean(k, b, to):
                wait(pe, x_ready[k], b + 1)
                for e in range(2):
                    last = pe.matmul(to[:, 0:L], mean_w[:, :], xres[:, b, e * L:(e + 1) * L],
                                     start=(e == 0), stop=(e == 1))
                last.then_inc(norm[k]["mean_ready"], 1)

            def norm_var(k, b, to):
                sq = NORM[k][1]
                wait(pe, norm[k]["sq_ready"], b + 1)
                for e in range(2):
                    last = pe.matmul(to[:, L:2 * L], mean_w[:, :], sq[:, e * L:(e + 1) * L],
                                     start=(e == 0), stop=(e == 1))
                last.then_inc(norm[k]["var_ready"], 1)

            def route(k, b):
                m = MOE[k]
                wait(pe, norm[k]["xn_ready"], b + 1)
                for t in range(2):
                    for e in range(2):
                        last = pe.matmul(CB[:, 16 * t:16 * t + m["nr"]], xn[:, e, t * P:(t + 1) * P],
                                         m["route"][:, e, 0:m["nr"]], start=(e == 0), stop=(e == 1))
                last.then_inc(moe[k]["logits_ready"], 1)

            def route_turn(k, b):
                wait(pe, moe[k]["cm_ready"], b + 1)
                for t in range(2):
                    last = pe.matmul(CB[0:96, L + t * P:L + (t + 1) * P],
                                     cm3[:, t, :, :].rearrange("p s c -> p (s c)"), ident_b[:, :],
                                     start=True, stop=True)
                last.then_inc(moe[k]["cmt_ready"], 1)

            def expert_up(k, b, p, only=None):
                m, s = MOE[k], moe[k]
                banks = m["banks"][p]
                before = bank_before(k, p)
                n = min(2, m["T"] - 2 * p)
                if before is not None and not only:
                    wait(pe, s["h1_ready"], m["NP"] * b + before + 1)
                for j in range(n) if only is None else (only,):
                    for which in range(2):
                        for e in range(2):
                            last = pe.matmul(bank[banks[which]][:, j * L:(j + 1) * L],
                                             m["gu"][:, 2 * p + j, e, which, :], xn[:, e, :],
                                             start=(e == 0), stop=(e == 1))
                if only in (None, n - 1):
                    last.then_inc(s["gu_ready"], 1)

            def expert_weight(k, b, p):
                m, s = MOE[k], moe[k]
                if p == 0:
                    wait(pe, s["cmt_copied"], b + 1)
                else:
                    wait(pe, s["cb_copied"], m["NP"] * b + p)
                for j in range(min(2, m["T"] - 2 * p)):
                    last = pe.matmul(CB[:, j * L:(j + 1) * L], m["pick"][:, 2 * p + j, :], cmt[:, :],
                                     start=True, stop=True)
                last.then_inc(s["cb_ready"], 1)

            def expert_down(k, b, p):
                m, s = MOE[k], moe[k]
                wait(pe, s["h_ready"], m["NP"] * b + p + 1)
                for j in range(min(2, m["T"] - 2 * p)):
                    t = 2 * p + j
                    for e in range(2):
                        last = pe.matmul(Y[:, e * L:(e + 1) * L], m["down"][:, t, e * P:(e + 1) * P],
                                         hh[:, p % 3, j, :], start=(t == 0 and e == 0),
                                         stop=(t == m["T"] - 1), skip_group_check=True)
                last.then_inc(s["h_used"], 1)

            def turn_a(i, mixer):
                for slot in range(13):
                    if mixer and slot < GROUPS:
                        mixer_spread(i + 1, slot)
                    if slot == 0:
                        norm_mean("m0", i, CB)
                    elif slot == 1:
                        norm_var("m0", i, CB)
                    elif slot == 2:
                        route("m0", i)
                    elif slot == 3:
                        route_turn("m0", i)
                    if 2 <= slot < 11:
                        expert_up("m0", i, slot - 2)
                    if 3 <= slot < 12:
                        expert_weight("m0", i, slot - 3)
                    if slot >= 4:
                        expert_down("m0", i, slot - 4)

            pe.wait_ge(bc3_ready, 2)
            pe.wait_ge(ld_x, 32)
            pe.wait_ge(front_dve, 1)
            for g in range(GROUPS):
                mixer_spread(0, g)
            pe.wait_ge(memset_done, 8)
            pe.wait_ge(ld_m0, 16 * 6)
            with pe.Fori(0, NB - 1) as i:
                turn_a(i, True)

            def expert_step(k, b, stage_no, piece=None):
                NP = MOE[k]["NP"]
                if stage_no < NP and piece != 2:
                    expert_up(k, b, stage_no, piece)
                if piece in (0, 1):
                    return
                if stage_no == 1:
                    route_turn(k, b)
                if 1 <= stage_no <= NP:
                    expert_weight(k, b, stage_no - 1)
                if stage_no >= 2:
                    expert_down(k, b, stage_no - 2)

            def front_step(b, n, first):
                norm_bank, plain, swapped = FRONT_BANKS[first]
                if n == 0:
                    norm_mean("at", b, norm_bank)
                elif n == 1:
                    norm_var("at", b, norm_bank)
                elif n == 2:
                    wait(pe, norm["at"]["xn_ready"], b + 1)
                    for to, w in ((plain, w_q), (swapped, w_qs)):
                        for m in range(2):
                            for e in range(2):
                                last = pe.matmul(to[:, m * L:(m + 1) * L], w[:, e, m * P:(m + 1) * P],
                                                 at_xn[:, e, :], start=(e == 0), stop=(e == 1))
                    last.then_inc(qk_ready, 1)
                else:
                    wait(pe, ctx_copied, b + 1)
                    wait(pe, rope_read, 2 * b + 1)
                    for to, w in ((plain, w_k), (swapped, w_ks)):
                        for m in range(2):
                            last = pe.matmul(to[:, m * L:(m + 1) * L], w[:, m * P:(m + 1) * P], ctx_b[:, :],
                                             start=True, stop=True)
                    last.then_inc(qk_ready, 1)

            def values_product(b):
                if not isinstance(b, int) or b > 0:
                    wait(pe, exp_done, NH * b)
                for t in range(2):
                    last = pe.matmul(bank[1][:, t * L:(t + 1) * L], ctx_b[:, t * P:(t + 1) * P], w_v[:, :],
                                     start=True, stop=True)
                last.then_inc(v_ready, 1)

            def turn_b(k, bm, ba, first=False, ahead=True):
                def experts(stage):
                    for stage_no in STEPS[k].get(stage, ()):
                        expert_step(k, bm, stage_no)

                if first:
                    front_step(0, 0, True)
                    norm_mean(k, bm, CB)
                    front_step(0, 1, True)
                    norm_var(k, bm, CB)
                    front_step(0, 2, True)
                    route(k, bm)
                    front_step(0, 3, True)
                    wait(pe, rope_read, 2)
                    values_product(0)
                else:
                    norm_mean(k, bm, CB)
                    norm_var(k, bm, CB)
                    route(k, bm)
                expert_step(k, bm, 0)
                experts("stacks")
                wait(pe, stacks_ready, 16 * 18 * (ba + 1))
                wait(pe, v_copied, ba + 1)
                for h in range(NH):
                    if h == 2:
                        wait(pe, moe[k]["h1_ready"], MOE[k]["NP"] * bm + 2)
                    if h >= 4:
                        wait(pe, max_done, NH * ba + h - 3)
                    for t in range(2):
                        last = pe.matmul(bank[h % 4][:, t * L:(t + 1) * L],
                                         q_stack[0:STACK, h, t * P:(t + 1) * P],
                                         k_stack[0:STACK, h, :], start=True, stop=True)
                    last.then_inc(s1_ready, 1)
                    if h in PIECES[k]:
                        expert_step(k, bm, *PIECES[k][h])
                wait(pe, mp_ready, ba + 1)
                for t in range(2):
                    last = pe.matmul(bank[2][0:96, t * P:(t + 1) * P], mp[:, t, :, :].rearrange("p s h -> p (s h)"),
                                     ident_b[:, :], start=True, stop=True)
                last.then_inc(mt_ready, 1)
                experts("rows")
                wait(pe, rows_ready, 48 * (ba + 1))

                def values(g, piece):
                    half, r, kt, part = g // 4, g % 4, piece // 2, piece % 2
                    if piece == 0:
                        wait(pe, exp_done, NH * ba + 4 * g + 4)
                    for s in range(4):
                        w = ones_pad[:, r, :] if part else v_pad[:, kt, 16 * half + 4 * s + r, :]
                        last = pe.matmul(bank[2 + half][32 * s:32 * s + 32, part * L:(part + 1) * L],
                                         w, p_exp[:, g % 2, s, kt, :], start=(r == 0 and piece == 0),
                                         stop=(r == 3 and kt == 1), skip_group_check=True)
                        if g == 6 and piece == 3 and s == 0:
                            last.then_inc(stacks_used, 1)
                    if piece == 3:
                        last.then_inc(pv_done, 1)

                for g in range(8):
                    half, r = g // 4, g % 4
                    for s in range(4):
                        n, h = 4 * g + s, 16 * half + 4 * s + r
                        if n >= 2:
                            wait(pe, exp_done, NH * ba + n - 1)
                        for kt in range(2):
                            last = pe.matmul(bank[n % 2][:, kt * L:(kt + 1) * L],
                                             k_stack[0:STACK + 3, h, kt * P:(kt + 1) * P],
                                             q_stack[0:STACK + 3, h, :], start=True, stop=True)
                        last.then_inc(s2_ready, 1)
                        if g >= 1:
                            values(g - 1, s)
                    experts(f"group{g}")
                    if ahead and f"group{g}" in FRONT:
                        front_step(ba + 1, FRONT[f"group{g}"], False)
                for piece in range(4):
                    values(7, piece)
                if ahead:
                    values_product(ba + 1)
                for e in range(2):
                    wait(pe, attn_ready, 2 * ba + e + 1)
                    for m in range(2):
                        last = pe.matmul(bank[0][:, m * L:(m + 1) * L], w_out[:, e, m * P:(m + 1) * P],
                                         attn[:, e, :], start=(e == 0 and m == 0), stop=(e == 1),
                                         skip_group_check=True)
                last.then_inc(o_ready, 1)

            pe.wait_ge(ld_at, 16 * 7)
            turn_b("m0 last", NB - 1, 0, first=True)
            pe.wait_ge(ld_m1, 16 * 4)
            with pe.Fori(0, NB - 2) as i:
                turn_b("m1", i, i + 1)
            turn_b("m1", NB - 2, NB - 1, ahead=False)
            norm_mean("m1", NB - 1, CB)
            norm_var("m1", NB - 1, CB)
            route("m1", NB - 1)
            for stage_no in range(MOE["m1"]["NP"] + 2):
                expert_step("m1", NB - 1, stage_no)


def xpad_flat(region):
    return region[:, 0:2048]




def _lay_out(np, i):
    bf = np.dtype("bfloat16")

    def halves(a):
        return a.reshape(2, P, -1).transpose(1, 0, 2)

    def feature_rows(blocks, tiles):
        rows = np.concatenate(blocks, 0)
        full = np.zeros((tiles * P, rows.shape[1]), rows.dtype)
        full[:rows.shape[0]] = rows
        return full

    def gate_up(gate, up, tiles):
        both = np.stack([feature_rows(gate, tiles), feature_rows(up, tiles)])
        return both.reshape(2, tiles, P, 2, P).transpose(4, 1, 3, 0, 2)

    def down(blocks, tiles):
        return feature_rows(blocks, tiles).reshape(tiles, P, D).transpose(1, 0, 2)

    def expert_pick(tiles, shared):
        pick = np.zeros((96, tiles, P), bf)
        for f in range(tiles * P):
            j = f // FE if f < E * FE else E
            for s in range(3):
                pick[32 * s + j, f // P, f % P] = 1
        return pick

    x, c = i["x"], i["ctx_1024"]
    w_x = i["L0_xattn_x_proj_w"]
    gu = i["L0_ffn_gate_up_proj"]
    g1, u1 = i["L1_ffn_gate_proj"], i["L1_ffn_up_proj"]
    swap = np.arange(D) ^ 1
    wkv = i["L1_xattn_Wkv"]
    sel_state = np.zeros((96, 2 * NS, P), bf)
    for j in range(2 * NS):
        sel_state[[j, 32 + j, 64 + j], j, :] = 1
    row = np.arange(P)
    columns = np.zeros((P, 8), np.float32)
    columns[:, 0] = EPS
    columns[:, 1] = np.pi / 2
    columns[:, 2] = np.where(row // 2 % 2 == 0, 1.0, 0.01)
    columns[:, 3] = np.where(row % 2 == 0, -1.0, 1.0)
    return dict(
        x_t=x.transpose(2, 0, 1).reshape(2, P, NB, L).transpose(1, 2, 0, 3).reshape(P, NB, 2 * L),
        x_rows=x.reshape(NB, 2, P, D).transpose(2, 0, 1, 3),
        ctx_t=c.transpose(2, 0, 1),
        pos=i["fside_BxSx2_0"].transpose(2, 0, 1)[row % HD // 4],
        gates=np.broadcast_to(np.concatenate([i["g_xattn"], i["g_ffn"]]), (P, 4)),
        in_proj=i["L0_xattn_in_proj_w"].T,
        conv_w=halves(i["L0_xattn_conv_w"]),
        conv_b=i["L0_xattn_conv_b"].reshape(2, P).T,
        bc_proj=halves(np.tile(w_x[DR:].T, (1, 3))),
        dt_lo_proj=halves(w_x[:DR].T),
        dt_proj=i["L0_xattn_dt_proj_w"].T,
        dt_b=i["L0_xattn_dt_proj_b"].reshape(2, P).T,
        a_log=halves(i["L0_xattn_A_log"]),
        d_skip=i["L0_xattn_D"].reshape(2, P).T,
        gu0=gate_up([gu[:, :FE].reshape(-1, D), i["L0_ffn_sh_gate_w"]],
                    [gu[:, FE:].reshape(-1, D), i["L0_ffn_sh_up_w"]], T0),
        down0=down([i["L0_ffn_down_proj"].transpose(0, 2, 1).reshape(-1, D), i["L0_ffn_sh_down_w"].T], T0),
        route0=halves(np.concatenate([i["L0_ffn_router_weight"], i["L0_ffn_shared_gate_w"]]).T),
        gu1=gate_up([g1.reshape(-1, D)], [u1.reshape(-1, D)], T1),
        down1=down([i["L1_ffn_down_proj"].transpose(0, 2, 1).reshape(-1, D)], T1),
        route1=halves(i["L1_ffn_gate_w"].T),
        wq=halves(i["L1_xattn_Wq"]),
        wq_swap=halves(i["L1_xattn_Wq"][:, swap]),
        wk=wkv[:, :D],
        wk_swap=wkv[:, swap],
        wv=wkv[:, D:],
        wout=halves(i["L1_xattn_Wout"]),
        bout=i["L1_xattn_bout"].reshape(2, P).T,
        sel_state=sel_state,
        sel0=expert_pick(T0, True),
        sel1=expert_pick(T1, False),
        ident=np.eye(P, dtype=bf),
        columns=columns,
        iota8=np.broadcast_to(np.arange(E, dtype=np.float32), (P, E)),
    )


def kernel(**inputs):
    import numpy as np
    import concourse.bacc as bacc
    from concourse.bass_utils import run_bass_kernel_spmd

    laid = _lay_out(np, {k: np.asarray(v) for k, v in inputs.items()})
    nc = bacc.Bacc("TRN2", target_bir_lowering=False, num_devices=1)
    arrays, handles = {}, {}
    for name, a in laid.items():
        a = np.ascontiguousarray(a)
        arrays["in_" + name] = a
        handles[name] = nc.dram_tensor("in_" + name, a.shape, mybir.dt.from_np(a.dtype), kind="ExternalInput").ap()
    out = nc.dram_tensor("out_0", (P, NB, 2 * L), F32, kind="ExternalOutput").ap()
    program(nc, out=out, **handles)
    got = run_bass_kernel_spmd(nc, [arrays], core_ids=[0]).results[0]["out_0"]
    return np.ascontiguousarray(got.reshape(P, NB, 2, L).transpose(1, 3, 2, 0).reshape(NB, L, D))
```

```python
from contextlib import ExitStack

import concourse.bass as bass
from concourse import mybir

F32 = mybir.dt.float32
BF16 = mybir.dt.bfloat16
U32 = mybir.dt.uint32
ACT = mybir.ActivationFunctionType
ALU = mybir.AluOpType
AX = mybir.AxisListType

P = 128
NB = 4
L = 256
D = 256
HALVES = D // P
NS = 16
GROUPS = NS // 2
DR = 8
TAPS = 4
E = 8
FE = 176
FS = 704
T0 = -(-(E * FE + FS) // P)
T1 = E * FE // P
NH = 32
HD = D // NH
STACK = 9 * HD
SCALE = 1.0 / float(HD) ** 0.5
EPS = 1e-5
TWO_PI_HI = 6.28125
TWO_PI_LO = 0.0019353071795864769
ROUND = 12582912.0
CHAIN = dict(DVE_A=22, ACT_A=27, POOL_A=13, DVE_B=44, ACT_B=9, POOL_B=0)


def program(nc, x_t, x_rows, ctx_t, pos, gates, in_proj, conv_w, conv_b, x_proj, dt_proj,
            dt_b, a_log, d_skip, gu0, down0, route0, gu1, down1, route1, wq, wk, wv,
            wout, bout, sel_state, sel0, sel1, ident, columns, iota8, out):
    ctx = ExitStack()
    with ctx:
        def sb(name, shape, dt=F32):
            return ctx.enter_context(nc.sbuf_tensor(name, shape, dt))

        def sem(name):
            return ctx.enter_context(nc.semaphore(name))

        bank = [ctx.enter_context(nc.psum_tensor(f"bank{i}", [P, 512], F32)) for i in range(8)]

        w_in = sb("w_in", [P, D])
        w_conv = sb("w_conv", [P, HALVES, TAPS])
        b_conv = sb("b_conv", [P, HALVES])
        w_x = sb("w_x", [P, HALVES, 96 + DR])
        w_dt = sb("w_dt", [P, D])[96:96 + DR, :]
        b_dt = sb("b_dt", [P, HALVES])
        a_col = sb("a_col", [P, HALVES, NS])
        d_col = sb("d_col", [P, HALVES])
        gate_raw = sb("gate_raw", [P, 4])
        gate = sb("gate", [P, 4])
        half_gate = sb("half_gate", [P, 4])
        gated_b = sb("gated_b", [P, HALVES])
        w_gu0 = sb("w_gu0", [P, T0, 2, 2, P])
        w_down0 = sb("w_down0", [P, T0, D])
        w_gu1 = w_gu0[:, 0:T1, :, :, :]
        w_down1 = w_down0[:, 0:T1, :]
        w_route0 = sb("w_route0", [P, HALVES, E + 1])
        w_route1 = sb("w_route1", [P, HALVES, E])
        w_q = sb("w_q", [P, HALVES, D])
        w_k = sb("w_k", [P, D])
        w_v = sb("w_v", [P, D])
        w_out = sb("w_out", [P, HALVES, D])
        b_out = sb("b_out", [P, HALVES])
        region4 = sb("region4", [P, 2048])
        pick_state = region4[0:96, :].bitcast(BF16).rearrange("p (n c) -> p n c", n=2 * NS)
        pick0 = sb("pick0", [96, T0, P], BF16)
        pick1 = sb("pick1", [96, T1, P], BF16)
        ident_b = sb("ident_b", [P, P], BF16)
        col = sb("col", [P, 8])
        iota = sb("iota", [P, E])
        mean_w = sb("mean_w", [P, P])
        ones_pad = sb("ones_pad", [P, 4, 32])

        xres = sb("xres", [P, NB, 2 * L])
        ctx_all = sb("ctx_all", [P, NB, L])
        region3 = sb("region3", [P, 6144])
        delta = region3[:, 0:2048].rearrange("p (b e l) -> p b e l", b=NB, e=2)
        du = region3[:, 2048:4096].rearrange("p (b n) -> p b n", b=NB)
        ygate = region3[:, 4096:6144].rearrange("p (b n) -> p b n", b=NB)
        p_exp = region3[:, 0:4096].rearrange("p (r j k l) -> p r j k l", r=2, j=4, k=2)
        v_pad = region3[:, 4096:6144].rearrange("p (k h c) -> p k h c", k=2, h=NH)
        delta_flat = region3[:, 0:2048]
        bc3 = sb("bc3", [96, NB * L], BF16)
        cos_t = sb("cos_t", [P, NB, L])
        sin_t = sb("sin_t", [P, NB, L])

        region = sb("region", [P, 9248])
        xpad = region[:, 0:HALVES * NB * (L + 3)].rearrange("p (e b l) -> p e b l", e=HALVES, b=NB)
        tmp = region[:, 2080:4128].rearrange("p (b n) -> p b n", b=NB)
        tmp_flat = region[:, 2080:4128]
        soft_t = (region[:, 4128:5152], region[:, 8224:9248])
        u_all = region[:, 6176:8224].rearrange("p (b n) -> p b n", b=NB)
        bc_rest = region[0:96, 8224:9248]
        q_stack = region[0:96, 0:NH * L // 2].bitcast(BF16).rearrange("p (h l) -> p h l", h=NH)
        k_stack = region[0:96, NH * L // 2:NH * L].bitcast(BF16).rearrange("p (h l) -> p h l", h=NH)
        da = region[:, 0:2048].rearrange("p (r j e l) -> p r j e l", r=2, j=2, e=2)
        dbu = region[:, 4128:5152]
        states = region[:, 5152:6176]
        rt1, rt2 = region[:, 8192:8704], region[:, 8704:9216]
        region2 = sb("region2", [P, 3072])
        dt_lo = region2[96:96 + DR, 2048:3072]
        hc = region2[:, 0:2048].rearrange("p (r j n) -> p r j n", r=2, j=2)
        acc = region2[:, 2048:2560]
        qk = region2[:, 0:1024]
        parts = region2[:, 1024:2560].bitcast(BF16).rearrange("p (i n) -> p i n", i=3)
        step = sb("step", [P, 2, L])
        stats = sb("stats", [P, 8, 6])
        mv = sb("mv", [P, 8, 2])
        z_scale = sb("z_scale", [P, 8])
        z_bias = sb("z_bias", [P, 8])

        dev = sb("dev", [P, 512])
        sq = sb("sq", [P, 512])
        rstd = sb("rstd", [P, L])
        xn = sb("xn", [P, HALVES, L])
        at_dev, at_sq = region4[:, 0:512], region4[:, 512:1024]
        at_xn = region4[:, 1024:1536].rearrange("p (e l) -> p e l", e=HALVES)
        at_rstd = region4[:, 1536:1792]
        logit = sb("logit", [P, 2, 16])
        top = sb("top", [P, 2, E])
        top_i = sb("top_i", [P, 2, E], U32)
        top_f = sb("top_f", [P, 2, E])
        filler = sb("filler", [P, 1])
        gap = sb("gap", [P, 2, 1])
        egap = sb("egap", [P, 2, 1])
        sg = sb("sg", [P, 2, 1])
        w12 = sb("w12", [P, 2, 2])
        cm = sb("cm", [P, 2, 32])
        chosen = sb("chosen", [P, 2, 2, E])
        zero = sb("zero", [P, 2, 32])
        cm_b = sb("cm_b", [P, 2, E])
        cm3 = sb("cm3", [P, 2, 3, 32], BF16)
        cmt = sb("cmt", [96, L], BF16)
        region5 = sb("region5", [P, 5120])
        x_nat = region5[:, 0:2048].rearrange("p (b e l) -> p b e l", b=NB, e=2)
        angles = region5[:, 2048:3072].rearrange("p (b l) -> p b l", b=NB)
        soft_w = region5[:, 3072:5120].rearrange("p (q n) -> p q n", q=2)
        th = region5[:, 0:1024].rearrange("p (r n) -> p r n", r=2)
        cbs = region5[:, 1024:2048].rearrange("p (r n) -> p r n", r=2)
        h1 = region5[:, 2048:3584].rearrange("p (r n) -> p r n", r=3)
        hh = region5[:, 3584:5120].rearrange("p (r j l) -> p r j l", r=3, j=2)
        ctx_b = sb("ctx_b", [P, L])
        mx = sb("mx", [P, 2, NH])
        mrest = sb("mrest", [P, 2, NH])
        mp = sb("mp", [P, 2, 3, NH], BF16)
        mt = sb("mt", [96, L], BF16)
        attn = step
        scratch = nc.dram_tensor("scratch", (3, 2, D, L), BF16, kind="Internal").ap()

        ld_in, ld_conv, ld_rows = sem("ld_in"), sem("ld_conv"), sem("ld_rows")
        ld_const, ld_front, ld_x, ld_m0, ld_m1, ld_at = (
            sem(n) for n in ("ld_const", "ld_front", "ld_x", "ld_m0", "ld_m1", "ld_at"))
        dve_front, act_front, pool_front = sem("dve_front"), sem("act_front"), sem("pool_front")
        dve_0, act_0, pool_0 = sem("dve_0"), sem("act_0"), sem("pool_0")
        dve_a, act_a, pool_a = sem("dve_a"), sem("act_a"), sem("pool_a")
        dve_z, act_z, pool_z = sem("dve_z"), sem("act_z"), sem("pool_z")
        dve_b, act_b, pool_b = sem("dve_b"), sem("act_b"), sem("pool_b")
        dve_y, act_y = sem("dve_y"), sem("act_y")
        memset_done, xin_ready, xin_copied, conv_ready, u_ready = (
            sem(n) for n in ("memset_done", "xin_ready", "xin_copied", "conv_ready", "u_ready"))
        x_proj_ready, dtlo_copied, dt_ready = (
            sem(n) for n in ("x_proj_ready", "dtlo_copied", "dt_ready"))
        w_ready, ln_ready, zstat_ready, zrstd_ready, zbias_ready, ygate_raw = (
            sem(n) for n in ("w_ready", "ln_ready", "zstat_ready", "zrstd_ready", "zbias_ready",
                             "ygate_raw"))
        a_exp, front_dve, ang_ready, gate_ready, bc3_ready = (
            sem(n) for n in ("a_exp", "front_dve", "ang_ready", "gate_ready",
                             "bc3_ready"))
        step_ready, da_ready, b_ready, c_ready, dbu_done, scan_done, hc_ready, hc_used, acc_used = (
            sem(n) for n in ("step_ready", "da_ready", "b_ready", "c_ready", "dbu_done", "scan_done", "hc_ready", "hc_used",
                             "acc_used"))
        x_ready = {k: sem(f"x_ready_{k}") for k in ("m0", "at", "m1", "out")}
        norm = {k: {n: sem(f"{n}_{k}") for n in ("mean_ready", "dev_ready", "sq_ready", "var_ready",
                                                 "rstd_ready", "xn_ready")} for k in ("m0", "at", "m1")}
        moe = {k: {n: sem(f"{n}_{k}") for n in (
            "logits_ready", "gap_ready", "egap_ready", "w12_ready", "cm_ready", "cmt_ready", "cmt_copied", "gu_ready",
            "tanh_ready", "h1_ready", "cb_ready", "cb_copied", "h_ready", "h_used")}
            for k in ("m0", "m1")}
        (ctx_copied, qk_ready, v_ready, v_copied, rope_read, parts_ready, parts_stored,
         s1_ready, max_done, mp_ready, mt_ready, mt_copied, rows_ready, s2_ready, exp_done, pv_done,
         attn_ready, o_ready, vpad_zero) = (sem(n) for n in (
            "ctx_copied", "qk_ready", "v_ready", "v_copied", "rope_read", "parts_ready", "parts_stored",
            "s1_ready", "max_done", "mp_ready", "mt_ready", "mt_copied", "rows_ready",
            "s2_ready", "exp_done", "pv_done", "attn_ready", "o_ready", "vpad_zero"))
        stacks_ready = [sem(f"stacks_ready_{half}") for half in range(2)]
        stacks_used = [sem(f"stacks_used_{half}") for half in range(2)]
        stored = sem("stored")
        block = ctx.enter_context(nc.Block())

        N_CONST, N_FRONT = 3, 6

        def wait(e, s, value):
            if isinstance(value, int):
                if value > 0:
                    e.wait_ge(s, value)
                return
            e.wait_ge(s, value)
            e.wait_ge(ld_const, 16 * N_CONST)

        class Chain:

            def __init__(self, e, s, base=0):
                self.e, self.s, self.base, self.n, self.marks = e, s, base, 0, []

            def then(self, ins, s=None, value=None):
                if s is None:
                    self.n += 1
                    s, value = self.s, self.base + self.n
                self.marks.append((s, value))
                ins.then_inc(s, 1)

            def behind(self, lag=0):
                if len(self.marks) > lag:
                    wait(self.e, *self.marks[-1 - lag])

            def close(self, per=None):
                assert per is None or self.n == per, (self.n, per)
                self.behind()

        MOE = {
            "m0": dict(T=T0, gu=w_gu0, down=w_down0, route=w_route0, nr=E + 1, pick=pick0, gate=2,
                       second=range(0, 99, 2), nxt="at"),
            "m1": dict(T=T1, gu=w_gu1, down=w_down1, route=w_route1, nr=E, pick=pick1, gate=3,
                       second=(), nxt="out"),
        }
        MOE["m0 last"] = dict(MOE["m0"], second=(1, 3))
        MOE["m1 last"] = dict(MOE["m1"], second=(1, 3, 5))
        for m in MOE.values():
            m["NP"] = -(-m["T"] // 2)
            m["banks"] = [(2, 3) if p in m["second"] else (4, 5) for p in range(m["NP"])]
        for k in ("m0", "m1"):
            moe[k + " last"], norm[k + " last"], x_ready[k + " last"] = moe[k], norm[k], x_ready[k]
        NORM = {k: (dev, sq, rstd, xn) for k in MOE}
        NORM["at"] = (at_dev, at_sq, at_rstd, at_xn)

        def bank_before(k, p):
            banks = MOE[k]["banks"]
            return max((q for q in range(p) if banks[q] == banks[p]), default=None)

        PIECES = {"m0 last": {5: [(6, "up")], 10: [(6, "rest")], 16: [(7, "up")], 22: [(7, "rest")],
                              31: [(8, "up")]},
                  "m1": {11: [(0, "up")], 15: [(1, "up")], 19: [(1, "rest"), (2, "up")],
                         23: [(2, "rest"), (3, "up")], 27: [(3, "rest"), (4, "up")],
                         31: [(4, "rest"), (5, "up")]}}
        NORM_AT = dict(pe_var=3, dve_scale=5, pe_route=7, dve_top=8, dve_weights=10)
        STEPS = {"m0 last": {"stacks": (3, 4, 5), "rows": (8, 9), "group0": (10,)},
                 "m1": {"stacks": (), "rows": (5, 6), "group0": (7,)}}
        for k, pieces in PIECES.items():
            for h, todo in pieces.items():
                if h < NH - 1:
                    STEPS[k][f"head{h}"] = tuple(n for n, what in todo if what == "up")
        FRONT = {"group1": 2, "group2": 3}
        FRONT_BANKS = {True: (bank[1], bank[0], bank[1]), False: (bank[3], bank[4], bank[5])}
        CB, Y = bank[6], bank[7]

        @block.sync
        def _(sp):
            sp.dma_start(w_in[:, :], in_proj).then_inc(ld_in, 16)
            sp.dma_start(w_conv[:, :, :], conv_w).then_inc(ld_conv, 16)
            sp.dma_start(ctx_all[:, :, :], ctx_t).then_inc(ld_in, 16)
            sp.dma_start(b_conv[:, :], conv_b).then_inc(ld_front, 16)
            sp.dma_start(w_x[:, :, :], x_proj).then_inc(ld_front, 16)
            sp.dma_start(w_dt, dt_proj).then_inc(ld_front, 16)
            sp.dma_start(b_dt[:, :], dt_b).then_inc(ld_front, 16)
            sp.dma_start(a_col[:, :, :], a_log).then_inc(ld_front, 16)
            sp.dma_start(d_col[:, :], d_skip).then_inc(ld_front, 16)
            sp.dma_start(x_nat, x_rows).then_inc(ld_rows, 16)
            sp.dma_start(xres[:, :, :], x_t).then_inc(ld_x, 16)
            sp.dma_start(pick_state, sel_state).then_inc(ld_x, 16)
            sp.dma_start(ident_b[:, :], ident).then_inc(ld_m0, 16)
            sp.dma_start(w_gu0[:, :, :, :, :], gu0).then_inc(ld_m0, 16)
            sp.dma_start(w_route0[:, :, :], route0).then_inc(ld_m0, 16)
            sp.dma_start(pick0[:, :, :], sel0).then_inc(ld_m0, 16)
            sp.dma_start(w_down0[:, :, :], down0).then_inc(ld_m0, 16)
            sp.dma_start(iota[:, :], iota8).then_inc(ld_m0, 16)
            for to, of in ((w_q[:, :, :], wq), (w_k[:, :], wk), (w_v[:, :], wv), (w_out[:, :, :], wout),
                           (b_out[:, :], bout)):
                sp.dma_start(to, of).then_inc(ld_at, 16)

            def store(b):
                wait(sp, parts_ready, b + 1)
                sp.dma_start(scratch.rearrange("i s (p t) l -> p i s t l", t=2),
                             parts[:, :, :].rearrange("p i (s t l) -> p i s t l", s=2, t=2)
                             ).then_inc(parts_stored, 16)
                wait(sp, parts_stored, 16 * b + 16)

            def stack(b, used=()):
                for half in range(2):
                    heads = slice(half * NH // 2, (half + 1) * NH // 2)
                    if used:
                        wait(sp, used[half], b)
                    for j in range(3):
                        for i in range(3):
                            r = j * 24 + i * 8
                            sp.dma_start(q_stack[r:r + 8, heads, :],
                                         scratch[i, 0].rearrange("(h d) l -> d h l", d=HD)[:, heads, :]
                                         ).then_inc(stacks_ready[half], 16)
                            sp.dma_start(k_stack[r:r + 8, heads, :],
                                         scratch[j, 1].rearrange("(h d) l -> d h l", d=HD)[:, heads, :]
                                         ).then_inc(stacks_ready[half], 16)
                wait(sp, mt_copied, b + 1)
                for s in range(3):
                    sp.dma_start(q_stack[STACK + s:STACK + s + 1, :, :], mt[32 * s:32 * s + 32, :]
                                 ).then_inc(rows_ready, 16)

            sp.wait_ge(vpad_zero, 2)
            store(0)
            stack(0)
            sp.wait_ge(x_ready["at"], NB)
            for to, of in ((w_gu1, gu1), (w_down1, down1),
                           (w_route1[:, :, :], route1), (pick1[:, :, :], sel1)):
                sp.dma_start(to, of).then_inc(ld_m1, 16)
            with sp.Fori(0, NB - 1) as i:
                store(i + 1)
                stack(i + 1, used=stacks_used)
                wait(sp, x_ready["out"], i + 1)
                sp.dma_start(out[:, i, :], xres[:, i, :]).then_inc(stored, 16)
            sp.wait_ge(x_ready["out"], NB)
            sp.dma_start(out[:, NB - 1, :], xres[:, NB - 1, :]).then_inc(stored, 16)
            sp.wait_ge(stored, 16 * NB)

        @block.gpsimd
        def _(pool):
            pool.memset(region[:, 0:HALVES * NB * (L + 3)].rearrange("p (g l) -> p g l", l=L + 3)[:, :, 0:3],
                        0.0).then_inc(memset_done, 1)
            pool.memset(mean_w[:, :], 1.0 / D).then_inc(memset_done, 1)
            pool.memset(ones_pad[:, :, :], 0.0).then_inc(memset_done, 1)
            pool.memset(cm[:, :, :], 0.0).then_inc(memset_done, 1)
            pool.memset(zero[:, :, :], 0.0).then_inc(memset_done, 1)
            pool.wait_ge(memset_done, 5)
            for r in range(4):
                pool.memset(ones_pad[:, r, r * HD:(r + 1) * HD], 1.0).then_inc(memset_done, 1)
            ch = Chain(pool, pool_front)
            pool.wait_ge(ld_const, 16 * N_CONST)
            ang, turns = cos_t[:, :, :], sin_t[:, :, :]
            ch.then(pool.tensor_scalar(ang, ang, col[:, 2:3], None, ALU.mult))
            ch.behind()
            ch.then(pool.tensor_scalar(turns, ang, 1.0 / (TWO_PI_HI + TWO_PI_LO), ROUND, ALU.mult, ALU.add))
            ch.behind()
            ch.then(pool.tensor_scalar(turns, turns, ROUND, None, ALU.subtract))
            t3 = angles
            for part in (TWO_PI_HI, TWO_PI_LO):
                ch.behind()
                ch.then(pool.tensor_scalar(t3, turns, part, None, ALU.mult))
                ch.behind()
                ch.then(pool.tensor_tensor(ang, ang, t3, ALU.subtract))
            ch.behind()
            ch.then(pool.tensor_copy(t3, ang), ang_ready, 1)
            def mixer_group(ch, b, g):
                if g == 0:
                    wait(pool, acc_used, b)
                wait(pool, hc_ready, GROUPS * b + g + 1)
                ch.behind()
                if g == 0:
                    ch.then(pool.tensor_tensor(acc, hc[:, g % 2, 0, :], hc[:, g % 2, 1, :], ALU.add)
                            , hc_used, GROUPS * b + g + 1)
                else:
                    ch.then(pool.tensor_tensor(acc, acc, hc[:, g % 2, 0, :], ALU.add))
                    ch.behind()
                    ch.then(pool.tensor_tensor(acc, acc, hc[:, g % 2, 1, :], ALU.add), hc_used, GROUPS * b + g + 1)

            def route_place(ch, k, b):
                wait(pool, moe[k]["w12_ready"], b + 1)
                ch.behind()
                for n, to in ((0, cm[:, :, 0:E]), (1, cm_b[:, :, :])):
                    ch.then(pool.tensor_tensor(to, chosen[:, n, :, :], w12[:, :, n:n + 1].broadcast_to([P, 2, E]),
                                               ALU.mult))
                ch.behind()
                ch.then(pool.tensor_tensor(cm[:, :, 0:E], cm[:, :, 0:E], cm_b[:, :, :], ALU.add))
                ch.behind()
                ch.then(pool.tensor_tensor(cm3[:, :, 0, :], cm[:, :, :], zero[:, :, :], ALU.add))
                ch.behind()
                ch.then(pool.tensor_tensor(cm[:, :, :], cm[:, :, :], cm3[:, :, 0, :], ALU.subtract))
                ch.behind()
                ch.then(pool.tensor_tensor(cm3[:, :, 1, :], cm[:, :, :], zero[:, :, :], ALU.add))
                ch.behind()
                ch.then(pool.tensor_tensor(cm3[:, :, 2, :], cm[:, :, :], cm3[:, :, 1, :], ALU.subtract)
                        , moe[k]["cm_ready"], b + 1)

            def expert_pair(ch, k, b, p):
                m, s = MOE[k], moe[k]
                n = min(2, m["T"] - 2 * p) * L
                wait(pool, s["h1_ready"], m["NP"] * b + p + 1)
                wait(pool, s["cb_copied"], m["NP"] * b + p + 1)
                if p >= 3:
                    wait(pool, s["h_used"], m["NP"] * b + p - 2)
                ch.behind(2)
                ch.then(pool.tensor_tensor(hh[:, p % 3, 0:n // L, :].rearrange("p a l -> p (a l)"),
                                           h1[:, p % 3, 0:n], cbs[:, p % 2, 0:n], ALU.mult)
                        , s["h_ready"], m["NP"] * b + p + 1)

            ch.close()
            ch = Chain(pool, pool_0)
            for g in range(GROUPS):
                mixer_group(ch, 0, g)
            ch.close()
            pool.wait_ge(ld_m0, 16 * 6)
            with pool.Fori(0, NB - 1) as i:
                ch = Chain(pool, pool_a, i * CHAIN["POOL_A"])
                route_place(ch, "m0", i)
                for slot in range(MOE["m0"]["NP"] + 1):
                    if slot < GROUPS:
                        mixer_group(ch, i + 1, slot)
                    if slot >= 1:
                        expert_pair(ch, "m0", i, slot - 1)
                ch.close(CHAIN["POOL_A"])
            pool.wait_ge(x_ready["m0"], NB)
            pool.memset(v_pad, 0.0).then_inc(vpad_zero, 1)
            pool.wait_ge(vpad_zero, 1)
            pool.memset(k_stack[64:96, :, :], 1.0).then_inc(vpad_zero, 1)
            pool.wait_ge(vpad_zero, 2)
            ch = Chain(pool, pool_z)
            route_place(ch, "m0 last", NB - 1)
            for p in range(MOE["m0"]["NP"]):
                expert_pair(ch, "m0 last", NB - 1, p)
            ch.close()
            with pool.Fori(0, NB) as b:
                ch = Chain(pool, pool_b, b * CHAIN["POOL_B"])
                for p in range(MOE["m1"]["NP"]):
                    expert_pair(ch, "m1", b, p)
                ch.close(CHAIN["POOL_B"])

        @block.scalar
        def _(act):
            act.dma_start(col[:, :], columns).then_inc(ld_const, 16)
            act.dma_start(gate_raw[:, :], gates).then_inc(ld_const, 16)
            act.dma_start(cos_t[:, :, :], pos).then_inc(ld_const, 16)
            ch = Chain(act, act_front)
            act.wait_ge(ld_const, 16 * N_CONST)
            ch.then(act.activation(gate[:, :], gate_raw[:, :], ACT.Tanh), gate_ready, 1)
            for q in range(2):
                for e in range(2):
                    n = 2 * q + e
                    act.wait_ge(xin_ready, n + 1)
                    ch.then(act.activation(xpad[:, e, 2 * q:2 * q + 2, 3:3 + L],
                                           bank[n][:, :].rearrange("p (b l) -> p b l", b=2), ACT.Copy))
                    act.wait_ge(ld_conv, 16)
                    ch.then(act.activation(tmp[:, 2 * q:2 * q + 2, e * L:(e + 1) * L],
                                           bank[n][:, :].rearrange("p (b l) -> p b l", b=2), ACT.Identity,
                                           scale=w_conv[:, e, TAPS - 1:TAPS]), xin_copied, n + 1)

            def front_u(q):
                for e in range(2):
                    act.wait_ge(conv_ready, 2 * q + e + 1)
                    ch.then(act.activation(u_all[:, 2 * q:2 * q + 2, e * L:(e + 1) * L],
                                           tmp[:, 2 * q:2 * q + 2, e * L:(e + 1) * L], ACT.Silu,
                                           bias=b_conv[:, e:e + 1]), u_ready, 2 * q + e + 1)

            def front_dt_lo(q):
                act.wait_ge(x_proj_ready, q + 1)
                ch.then(act.activation(dt_lo[:, 512 * q:512 * q + 512], bank[6 + q][96:96 + DR, :], ACT.Copy)
                        , dtlo_copied, q + 1)

            def front_soft(q):
                for e in range(2):
                    n = 2 * q + e
                    act.wait_ge(dt_ready, n + 1)
                    ch.then(act.activation(delta[:, 2 * q:2 * q + 2, e, :],
                                           bank[n][:, :].rearrange("p (b l) -> p b l", b=2), ACT.Identity,
                                           bias=b_dt[:, e:e + 1]))
                if q == 1:
                    act.wait_ge(bc3_ready, 2)
                ch.behind()
                ch.then(act.activation(soft_t[q], delta_flat[:, 1024 * q:1024 * q + 1024], ACT.Abs))
                ch.behind()
                ch.then(act.activation(soft_t[q], soft_t[q], ACT.Exp, scale=-1.0))
                ch.behind()
                ch.then(act.activation(soft_w[:, q, :], soft_t[q], ACT.Identity, bias=col[:, 4:5]), w_ready, q + 1)

            def front_ln(q):
                ch.behind()
                ch.then(act.activation(tmp_flat[:, 1024 * q:1024 * q + 1024], soft_w[:, q, :], ACT.Ln)
                        , ln_ready, q + 1)

            act.wait_ge(ld_front, 16 * N_FRONT)
            front_u(0)
            front_dt_lo(0)
            front_u(1)
            front_soft(0)
            ch.then(act.activation(a_col[:, :, :], a_col[:, :, :], ACT.Exp), a_exp, 1)
            front_dt_lo(1)
            front_ln(0)
            act.wait_ge(zstat_ready, 1)
            ch.then(act.activation(z_scale[:, :], mv[:, :, 1], ACT.Ln, bias=col[:, 0:1]))
            front_soft(1)
            ch.then(act.activation(z_scale[:, :], z_scale[:, :], ACT.Exp, scale=-0.5), zrstd_ready, 1)

            def mixer_decay(ch, b, g):
                wait(act, scan_done, GROUPS * b + g - 1)
                if g == 0:
                    wait(act, step_ready, b + 1)
                for j in range(2):
                    for e in range(2):
                        n = 2 * g + j
                        ins = act.activation(da[:, g % 2, j, e, 1:L], step[:, e, 1:L], ACT.Exp,
                                             scale=a_col[:, e, n:n + 1])
                        ch.then(ins, *((da_ready, GROUPS * b + g + 1) if j and e else ()))

            def norm_square(ch, k, b):
                dev, sq, _, _ = NORM[k]
                wait(act, norm[k]["dev_ready"], b + 1)
                ch.behind()
                ch.then(act.activation(sq[:, :], dev[:, :], ACT.Square), norm[k]["sq_ready"], b + 1)

            def norm_rstd(ch, pairs):
                for k, b, at in pairs:
                    wait(act, norm[k]["var_ready"], b + 1)
                    ch.then(act.activation(NORM[k][2][:, :], at[:, L:2 * L], ACT.Ln, bias=col[:, 0:1]))
                for k, b, at in pairs:
                    rstd = NORM[k][2]
                    ch.behind(len(pairs) - 1)
                    ch.then(act.activation(rstd[:, :], rstd[:, :], ACT.Exp, scale=-0.5)
                            , norm[k]["rstd_ready"], b + 1)

            def route_exp(ch, k, b):
                wait(act, moe[k]["gap_ready"], b + 1)
                if MOE[k]["nr"] > E:
                    ch.then(act.activation(sg[:, :, :], logit[:, :, E:E + 1], ACT.Tanh, scale=0.5))
                    ch.behind()
                    ch.then(act.activation(cm[:, :, E:E + 1], sg[:, :, :], ACT.Identity, scale=0.5, bias=col[:, 3:4]))
                ch.then(act.activation(egap[:, :, :], gap[:, :, :], ACT.Exp)
                        , moe[k]["egap_ready"], b + 1)

            def route_copy(ch, k, b):
                wait(act, moe[k]["cmt_ready"], b + 1)
                ch.then(act.activation(cmt[:, :], CB[0:96, L:2 * L], ACT.Copy)
                        , moe[k]["cmt_copied"], b + 1)

            def expert_tanh(ch, k, b, p):
                m, s = MOE[k], moe[k]
                n = min(2, m["T"] - 2 * p) * L
                wait(act, s["gu_ready"], m["NP"] * b + p + 1)
                if p >= 2:
                    wait(act, s["h1_ready"], m["NP"] * b + p - 1)
                ch.behind(1)
                ch.then(act.activation(th[:, p % 2, 0:n], bank[m["banks"][p][0]][:, 0:n],
                                       ACT.Tanh, scale=0.5), s["tanh_ready"], m["NP"] * b + p + 1)

            def expert_weight(ch, k, b, p):
                m, s = MOE[k], moe[k]
                n = min(2, m["T"] - 2 * p) * L
                wait(act, s["cb_ready"], m["NP"] * b + p + 1)
                if p >= 2:
                    wait(act, s["h_ready"], m["NP"] * b + p - 1)
                ch.behind(1)
                ch.then(act.activation(cbs[:, p % 2, 0:n], CB[:, 0:n], ACT.Copy), s["cb_copied"], m["NP"] * b + p + 1)

            def expert_step(ch, k, b, step_no):
                if step_no < MOE[k]["NP"]:
                    expert_tanh(ch, k, b, step_no)
                if step_no == 1:
                    route_copy(ch, k, b)
                if 1 <= step_no <= MOE[k]["NP"]:
                    expert_weight(ch, k, b, step_no - 1)

            act.wait_ge(front_dve, 1)
            ch.close()
            ch = Chain(act, act_0)
            for g in range(GROUPS):
                mixer_decay(ch, 0, g)
                if g == 2:
                    front_ln(1)
                elif g == 5:
                    act.wait_ge(zbias_ready, 1)
                    for n in range(8):
                        b, e = n // 2, n % 2
                        ch.then(act.activation(ygate[:, b, e * L:(e + 1) * L], x_nat[:, b, e, :], ACT.Silu,
                                               bias=z_bias[:, n:n + 1], scale=z_scale[:, n:n + 1])
                                , ygate_raw, n + 1)
                elif g == 6:
                    act.wait_ge(ang_ready, 1)
                    ch.then(act.activation(sin_t[:, :, :], angles, ACT.Sin))
                    ch.then(act.activation(cos_t[:, :, :], angles, ACT.Abs))
                    ch.behind()
                    ch.then(act.activation(cos_t[:, :, :], cos_t[:, :, :], ACT.Sin, bias=col[:, 1:2], scale=-1.0))

            norm_square(ch, "m0", 0)
            norm_rstd(ch, [("m0", 0, bank[0])])

            def turn_a(ch, i):
                NP = MOE["m0"]["NP"]
                mixer_decay(ch, i + 1, 0)
                route_exp(ch, "m0", i)
                for slot in range(NP + 1):
                    if slot + 1 < GROUPS:
                        mixer_decay(ch, i + 1, slot + 1)
                    expert_step(ch, "m0", i, slot)
                    if slot == NP - 1:
                        norm_square(ch, "m0", i + 1)
                    elif slot == NP:
                        norm_rstd(ch, [("m0", i + 1, bank[0])])

            ch.close()
            with act.Fori(0, NB - 1) as i:
                ch = Chain(act, act_a, i * CHAIN["ACT_A"])
                turn_a(ch, i)
                ch.close(CHAIN["ACT_A"])

            def front_step(ch, b, n, first):
                if n == 0:
                    wait(act, v_copied, b)
                    ch.then(act.activation(ctx_b[:, :], ctx_all[:, b, :], ACT.Copy), ctx_copied, b + 1)
                    norm_square(ch, "at", b)
                elif n == 1:
                    norm_rstd(ch, [("at", b, FRONT_BANKS[first][0])])

            def turn_b(ch, k, bm, ba, first=False, ahead=True):
                def experts(stage):
                    for step_no in STEPS[k].get(stage, ()):
                        expert_step(ch, k, bm, step_no)

                if first:
                    route_exp(ch, k, bm)
                    for n in range(2):
                        front_step(ch, 0, n, True)
                        expert_step(ch, k, bm, n)
                    expert_step(ch, k, bm, 2)
                wait(act, v_ready, ba + 1)
                for r in range(4):
                    for t in range(2):
                        ins = act.activation(
                            v_pad[:, t, :, :].rearrange("p (g r) c -> p g r c", r=4)[:, :, r, r * HD:(r + 1) * HD],
                            bank[1][:, t * L:(t + 1) * L].rearrange("p (g r d) -> p g r d", g=NH // 4,
                                                                    r=4)[:, :, r, :], ACT.Copy)
                        ch.then(ins, *((v_copied, ba + 1) if r == 3 and t == 1 else ()))
                if not first:
                    norm_square(ch, k, bm)
                    norm_rstd(ch, [(k, bm, CB)])
                    route_exp(ch, k, bm)
                experts("stacks")
                for h in range(NH):
                    experts(f"head{h}")
                wait(act, mt_ready, ba + 1)
                ch.then(act.activation(mt[:, :], bank[2][0:96, 0:L], ACT.Copy), mt_copied, ba + 1)
                if ahead:
                    front_step(ch, ba + 1, 0, False)
                experts("rows")
                if ahead:
                    front_step(ch, ba + 1, 1, False)
                for g in range(8):
                    for s in range(4):
                        n = 4 * g + s
                        wait(act, s2_ready, NH * ba + n + 1)
                        if s == 0 and g >= 2:
                            wait(act, pv_done, 8 * ba + g - 1)
                        ch.behind(2)
                        ch.then(act.activation(p_exp[:, g % 2, s, :, :],
                                               bank[n % 2][:, :].rearrange("p (k l) -> p k l", k=2), ACT.Exp,
                                               scale=SCALE), exp_done, NH * ba + n + 1)
                    experts(f"group{g}")
                    if ahead and f"group{g}" in FRONT:
                        front_step(ch, ba + 1, FRONT[f"group{g}"], False)

            ch.close()
            act.wait_ge(vpad_zero, 2)
            ch = Chain(act, act_z)
            turn_b(ch, "m0 last", NB - 1, 0, first=True)
            ch.close()
            with act.Fori(0, NB - 2) as i:
                ch = Chain(act, act_b, i * CHAIN["ACT_B"])
                turn_b(ch, "m1", i, i + 1)
                ch.close(CHAIN["ACT_B"])
            ch = Chain(act, act_y)
            turn_b(ch, "m1", NB - 2, NB - 1, ahead=False)
            norm_square(ch, "m1 last", NB - 1)
            norm_rstd(ch, [("m1 last", NB - 1, CB)])
            route_exp(ch, "m1 last", NB - 1)
            for step_no in range(MOE["m1"]["NP"] + 1):
                expert_step(ch, "m1 last", NB - 1, step_no)

        @block.vector
        def _(dve):
            ch = Chain(dve, dve_front)
            def front_conv(q):
                for e in range(2):
                    dve.wait_ge(xin_copied, 2 * q + e + 1)
                    dve.wait_ge(memset_done, 9)
                    dst = tmp[:, 2 * q:2 * q + 2, e * L:(e + 1) * L]
                    for k in range(TAPS - 1):
                        src = xpad[:, e, 2 * q:2 * q + 2, k:k + L]
                        ch.behind()
                        ins = dve.scalar_tensor_tensor(dst, src, w_conv[:, e, k:k + 1], dst, ALU.mult, ALU.add)
                        ch.then(ins, *((conv_ready, 2 * q + e + 1) if k == TAPS - 2 else ()))

            def front_bc(q):
                dve.wait_ge(x_proj_ready, q + 1)
                dve.wait_ge(dtlo_copied, q + 1)
                cols = slice(512 * q, 512 * q + 512)
                src, rest, to = bank[6 + q], bc_rest[:, cols], bc3[:, cols]
                ch.behind()
                ch.then(dve.tensor_copy(to, src[0:96, :]))
                ch.behind()
                ch.then(dve.tensor_tensor(rest, src[0:96, :], to, ALU.subtract))
                ch.behind()
                for strip in ((32, 64), (64, 96)):
                    ch.then(dve.tensor_copy(bc3[strip[0]:strip[1], cols], bc_rest[strip[0]:strip[1], cols]))
                ch.behind()
                ch.then(dve.tensor_tensor(bc_rest[64:96, cols], bc_rest[64:96, cols], bc3[64:96, cols],
                                          ALU.subtract))
                ch.behind()
                ch.then(dve.tensor_copy(bc3[64:96, cols], bc_rest[64:96, cols]), bc3_ready, q + 1)

            def front_log1p(ch, q):
                dve.wait_ge(w_ready, q + 1)
                ch.behind()
                ch.then(dve.scalar_tensor_tensor(soft_t[q], soft_w[:, q, :], 1.0, soft_t[q],
                                                 ALU.subtract, ALU.subtract))

            def front_delta(ch, q):
                dl = delta_flat[:, 1024 * q:1024 * q + 1024]
                dve.wait_ge(ln_ready, q + 1)
                ch.behind()
                ch.then(dve.scalar_tensor_tensor(dl, dl, 0.0, tmp_flat[:, 1024 * q:1024 * q + 1024],
                                                 ALU.max, ALU.add))
                ch.behind()
                ch.then(dve.tensor_tensor(dl, dl, soft_t[q], ALU.subtract))
                ch.behind()
                ch.then(dve.tensor_tensor(du[:, 2 * q:2 * q + 2, :].rearrange("p b n -> p (b n)"), dl,
                                          u_all[:, 2 * q:2 * q + 2, :].rearrange("p b n -> p (b n)"), ALU.mult)
                        , front_dve, q + 1)

            front_conv(0)
            front_conv(1)
            front_bc(0)
            ch.then(dve.memset(da[:, :, :, :, 0:1].rearrange("p r j e l -> p (r j e) l"), 0.0))
            dve.wait_ge(ld_rows, 16)
            for n in range(8):
                ch.then(dve.bn_stats(stats[:, n, :], x_nat[:, n // 2, n % 2, :]))
            ch.behind()
            for n in range(8):
                ch.then(dve.bn_aggr(mv[:, n, :], stats[:, n, :]), *((zstat_ready, 1) if n == 7 else ()))
            front_log1p(ch, 0)
            dve.wait_ge(a_exp, 1)
            ch.then(dve.tensor_scalar(a_col[:, :, :], a_col[:, :, :], -1.0, None, ALU.mult))
            front_bc(1)
            front_delta(ch, 0)

            def mixer_step(ch, b):
                ch.behind()
                ch.then(dve.tensor_scalar(step[:, :, :].rearrange("p e l -> p (e l)"),
                                          delta[:, b, :, :].rearrange("p e l -> p (e l)"), 1.0, None,
                                          ALU.mult), step_ready, b + 1)

            def mixer_group(ch, b, g):
                wait(dve, b_ready, GROUPS * b + g + 1)
                ch.behind(1)
                ch.then(dve.tensor_tensor(
                    dbu.rearrange("p (j e l) -> p j e l", j=2, e=2),
                    du[:, b, :].rearrange("p (e l) -> p e l", e=2).unsqueeze(1).broadcast_to([P, 2, 2, L]),
                    bank[0][:, :].rearrange("p (j l) -> p j l", j=2).unsqueeze(2).broadcast_to([P, 2, 2, L]),
                    ALU.mult), dbu_done, GROUPS * b + g + 1)
                wait(dve, da_ready, GROUPS * b + g + 1)
                ch.behind()
                ch.then(dve.tensor_tensor_scan(
                    states, da[:, g % 2, :, :, :].rearrange("p j e l -> p (j e l)"), dbu, 0.0,
                    ALU.mult, ALU.add), scan_done, GROUPS * b + g + 1)
                wait(dve, hc_used, GROUPS * b + g - 1)
                wait(dve, c_ready, GROUPS * b + g + 1)
                ch.behind()
                ch.then(dve.tensor_tensor(
                    hc[:, g % 2, :, :].rearrange("p j (e l) -> p j e l", e=2),
                    states.rearrange("p (j e l) -> p j e l", j=2, e=2),
                    bank[1][:, :].rearrange("p (j l) -> p j l", j=2).unsqueeze(2).broadcast_to([P, 2, 2, L]),
                    ALU.mult), hc_ready, GROUPS * b + g + 1)

            def mixer_end(ch, b):
                wait(dve, hc_used, GROUPS * b + GROUPS)
                ch.behind()
                for e in range(2):
                    half = slice(e * L, (e + 1) * L)
                    ins = dve.scalar_tensor_tensor(dev[:, half], u_all[:, b, half], d_col[:, e:e + 1],
                                                   acc[:, half], ALU.mult, ALU.add)
                    ch.then(ins, *((acc_used, b + 1) if e else ()))
                ch.behind()
                ch.then(dve.tensor_tensor(dev[:, :], dev[:, :], ygate[:, b, :], ALU.mult))
                ch.behind()
                ch.then(dve.scalar_tensor_tensor(xres[:, b, :], dev[:, :], gate[:, 0:1], xres[:, b, :],
                                                 ALU.mult, ALU.add), x_ready["m0"], b + 1)

            def norm_dev(ch, k, b, at):
                dev = NORM[k][0]
                wait(dve, norm[k]["mean_ready"], b + 1)
                ch.behind()
                ch.then(dve.tensor_tensor(
                    dev[:, :].rearrange("p (e l) -> p e l", e=2),
                    xres[:, b, :].rearrange("p (e l) -> p e l", e=2),
                    at[:, 0:L].unsqueeze(1).broadcast_to([P, 2, L]), ALU.subtract)
                , norm[k]["dev_ready"], b + 1)

            def norm_scale(ch, k, b):
                dev, _, rstd, xn = NORM[k]
                wait(dve, norm[k]["rstd_ready"], b + 1)
                ch.behind()
                ch.then(dve.tensor_tensor(
                    xn[:, :, :], dev[:, :].rearrange("p (e l) -> p e l", e=2),
                    rstd[:, :].unsqueeze(1).broadcast_to([P, 2, L]), ALU.mult)
                , norm[k]["xn_ready"], b + 1)

            def route_top(ch, k, b):
                nr = MOE[k]["nr"]
                wait(dve, moe[k]["logits_ready"], b + 1)
                ch.behind()
                ch.then(dve.tensor_copy(logit[:, :, 0:nr],
                                        CB[:, 0:32].rearrange("p (t n) -> p t n", t=2)[:, :, 0:nr]))
                ch.behind()
                ch.then(dve.memset(filler[:, :], 0.0))
                for t in range(2):
                    ch.then(dve.max(top[:, t, :], logit[:, t, 0:E]))
                ch.behind()
                ch.then(dve.tensor_tensor(gap[:, :, :], top[:, :, 1:2], top[:, :, 0:1], ALU.subtract)
                        , moe[k]["gap_ready"], b + 1)
                for t in range(2):
                    ch.then(dve.max_index(top_i[:, t, :], top[:, t, :], logit[:, t, 0:E]))
                ch.behind()
                ch.then(dve.tensor_copy(top_f[:, :, :], top_i[:, :, :]))
                ch.behind()
                for n in range(2):
                    ch.then(dve.tensor_tensor(chosen[:, n, :, :], iota[:, :].unsqueeze(1).broadcast_to([P, 2, E]),
                                              top_f[:, :, n:n + 1].broadcast_to([P, 2, E]), ALU.is_equal))

            def route_weights(ch, k, b):
                wait(dve, moe[k]["egap_ready"], b + 1)
                ch.behind()
                ch.then(dve.tensor_scalar(w12[:, :, 0:1], egap[:, :, :], 1.0, None, ALU.add))
                ch.behind()
                ch.then(dve.reciprocal(w12[:, :, 0:1], w12[:, :, 0:1]))
                ch.behind()
                ch.then(dve.tensor_tensor(w12[:, :, 1:2], egap[:, :, :], w12[:, :, 0:1], ALU.mult)
                        , *((moe[k]["w12_ready"], b + 1) if MOE[k]["T"] == T0 else ()))
                if MOE[k]["T"] == T0:
                    return
                ch.behind()
                for n, to in ((0, cm[:, :, 0:E]), (1, cm_b[:, :, :])):
                    ch.then(dve.tensor_tensor(to, chosen[:, n, :, :], w12[:, :, n:n + 1].broadcast_to([P, 2, E]),
                                              ALU.mult))
                ch.behind()
                ch.then(dve.tensor_tensor(cm[:, :, 0:E], cm[:, :, 0:E], cm_b[:, :, :], ALU.add))
                ch.behind()
                ch.then(dve.tensor_copy(cm3[:, :, 0, :], cm[:, :, :]))
                ch.behind()
                ch.then(dve.tensor_tensor(cm[:, :, :], cm[:, :, :], cm3[:, :, 0, :], ALU.subtract))
                ch.behind()
                ch.then(dve.tensor_copy(cm3[:, :, 1, :], cm[:, :, :]))
                ch.behind()
                ch.then(dve.tensor_tensor(cm3[:, :, 2, :], cm[:, :, :], cm3[:, :, 1, :], ALU.subtract)
                        , moe[k]["cm_ready"], b + 1)

            def expert_pair(ch, k, b, p):
                m, s = MOE[k], moe[k]
                n = min(2, m["T"] - 2 * p) * L
                gb, ub = m["banks"][p]
                wait(dve, s["tanh_ready"], m["NP"] * b + p + 1)
                ch.behind(1)
                ch.then(dve.scalar_tensor_tensor(th[:, p % 2, 0:n], th[:, p % 2, 0:n], 1.0,
                                                 bank[gb][:, 0:n], ALU.add, ALU.mult))
                if p >= 3:
                    wait(dve, s["h_ready"], m["NP"] * b + p - 2)
                ch.behind()
                ch.then(dve.tensor_tensor(h1[:, p % 3, 0:n], th[:, p % 2, 0:n], bank[ub][:, 0:n], ALU.mult)
                        , s["h1_ready"], m["NP"] * b + p + 1)

            def expert_end(ch, k, b):
                m = MOE[k]
                wait(dve, moe[k]["h_used"], m["NP"] * b + m["NP"])
                ch.behind()
                ch.then(dve.scalar_tensor_tensor(xres[:, b, :], Y[:, :], half_gate[:, m["gate"]:m["gate"] + 1],
                                                 xres[:, b, :], ALU.mult, ALU.add)
                        , x_ready[m["nxt"]], b + 1)

            ch.close()
            ch = Chain(dve, dve_0)
            mixer_step(ch, 0)
            for g in range(GROUPS):
                mixer_group(ch, 0, g)
                if g == 1:
                    front_log1p(ch, 1)
                    dve.wait_ge(zrstd_ready, 1)
                    ch.then(dve.scalar_tensor_tensor(z_bias[:, :], mv[:, :, 0], -1.0, z_scale[:, :],
                                                     ALU.mult, ALU.mult), zbias_ready, 1)
                elif g == 3:
                    front_delta(ch, 1)
            dve.wait_ge(gate_ready, 1)
            ch.then(dve.tensor_scalar(half_gate[:, :], gate[:, :], 0.5, None, ALU.mult))
            dve.wait_ge(ygate_raw, 8)
            dve.wait_ge(ld_x, 32)
            mixer_end(ch, 0)
            dve.wait_ge(ld_m0, 16 * 6)

            def expert_step(ch, k, b, step_no):
                if step_no < MOE[k]["NP"]:
                    expert_pair(ch, k, b, step_no)

            norm_dev(ch, "m0", 0, bank[0])
            norm_scale(ch, "m0", 0)

            def turn_a(ch, i):
                mixer_step(ch, i + 1)
                route_top(ch, "m0", i)
                for slot in range(MOE["m0"]["NP"]):
                    if slot < GROUPS:
                        mixer_group(ch, i + 1, slot)
                    if slot == 0:
                        route_weights(ch, "m0", i)
                    if slot == GROUPS:
                        mixer_end(ch, i + 1)
                    expert_step(ch, "m0", i, slot)
                norm_dev(ch, "m0", i + 1, bank[0])
                norm_scale(ch, "m0", i + 1)
                expert_end(ch, "m0", i)

            ch.close()
            with dve.Fori(0, NB - 1) as i:
                ch = Chain(dve, dve_a, i * CHAIN["DVE_A"])
                turn_a(ch, i)
                ch.close(CHAIN["DVE_A"])

            def front_step(ch, b, n, first):
                norm_bank, *product = FRONT_BANKS[first]
                if n == 0:
                    norm_dev(ch, "at", b, norm_bank)
                elif n == 1:
                    norm_scale(ch, "at", b)
                else:
                    s = n - 2
                    half = slice(512 * s, 512 * s + 512)
                    wait(dve, qk_ready, 2 * b + s + 1)
                    ch.behind()
                    ch.then(dve.tensor_tensor(
                        rt1.rearrange("p (m l) -> p m l", m=2), product[s][:, :].rearrange("p (m l) -> p m l", m=2),
                        cos_t[:, b, :].unsqueeze(1).broadcast_to([P, 2, L]), ALU.mult))
                    ch.then(dve.tensor_tensor(
                        rt2.rearrange("p (m l) -> p m l", m=2), product[s][:, :].rearrange("p (m l) -> p m l", m=2),
                        sin_t[:, b, :].unsqueeze(1).broadcast_to([P, 2, L]), ALU.mult), rope_read, 2 * b + s + 1)
                    ch.behind()
                    ch.then(dve.tensor_tensor(qk[:, 512 * s:512 * s + L], rt1[:, 0:L], rt2[:, L:2 * L],
                                              ALU.subtract))
                    ch.then(dve.tensor_tensor(qk[:, 512 * s + L:512 * s + 512], rt1[:, L:2 * L], rt2[:, 0:L],
                                              ALU.add))
                    ch.behind()
                    ch.then(dve.tensor_copy(parts[:, 0, half], qk[:, half]))
                    ch.behind()
                    ch.then(dve.tensor_tensor(qk[:, half], qk[:, half], parts[:, 0, half], ALU.subtract))
                    ch.behind()
                    ch.then(dve.tensor_copy(parts[:, 1, half], qk[:, half]))
                    ch.behind()
                    ins = dve.tensor_tensor(parts[:, 2, half], qk[:, half], parts[:, 1, half], ALU.subtract)
                    ch.then(ins, *((parts_ready, b + 1) if s else ()))

            def softmax_divide(ch, b, half):
                wait(dve, pv_done, 8 * b + 4 * half + 4)
                ch.behind()
                ch.then(dve.reciprocal(rt1[:, 0:L], bank[2 + half][:, L:2 * L]))
                ch.behind()
                ch.then(dve.tensor_tensor(attn[:, half, :], bank[2 + half][:, 0:L], rt1[:, 0:L], ALU.mult)
                        , attn_ready, 2 * b + half + 1)

            def turn_b(ch, k, bm, ba, first=False, ahead=True):
                def experts(stage):
                    for step_no in STEPS[k].get(stage, ()):
                        expert_step(ch, k, bm, step_no)

                if first:
                    route_top(ch, k, bm)
                    front_step(ch, 0, 0, True)
                    expert_step(ch, k, bm, 0)
                    route_weights(ch, k, bm)
                    front_step(ch, 0, 1, True)
                    expert_step(ch, k, bm, 1)
                    front_step(ch, 0, 2, True)
                    front_step(ch, 0, 3, True)
                    expert_step(ch, k, bm, 2)
                else:
                    norm_dev(ch, k, bm, CB)
                experts("stacks")
                for h in range(NH):
                    wait(dve, s1_ready, NH * ba + h + 1)
                    ch.behind(1)
                    ch.then(dve.tensor_reduce(mx[:, :, h],
                                              bank[h % 4][:, :].rearrange("p (t k) -> p t k", t=2),
                                              AX.X, ALU.max), max_done, NH * ba + h + 1)
                    if not first and h == NORM_AT["dve_scale"]:
                        norm_scale(ch, k, bm)
                    if not first and h == NORM_AT["dve_top"]:
                        route_top(ch, k, bm)
                    if not first and h == NORM_AT["dve_weights"]:
                        route_weights(ch, k, bm)
                    experts(f"head{h}")
                ch.behind()
                ch.then(dve.tensor_scalar(mp[:, :, 0, :], mx[:, :, :], -1.0, None, ALU.mult))
                ch.behind()
                ch.then(dve.scalar_tensor_tensor(mrest[:, :, :], mx[:, :, :], -1.0, mp[:, :, 0, :],
                                                 ALU.mult, ALU.subtract))
                ch.behind()
                ch.then(dve.tensor_copy(mp[:, :, 1, :], mrest[:, :, :]))
                ch.behind()
                ch.then(dve.tensor_tensor(mp[:, :, 2, :], mrest[:, :, :], mp[:, :, 1, :], ALU.subtract)
                        , mp_ready, ba + 1)
                if ahead:
                    front_step(ch, ba + 1, 0, False)
                experts("rows")
                if ahead:
                    front_step(ch, ba + 1, 1, False)
                for g in range(8):
                    experts(f"group{g}")
                    if g == 0:
                        expert_end(ch, k, bm)
                    if ahead and f"group{g}" in FRONT:
                        front_step(ch, ba + 1, FRONT[f"group{g}"], False)
                    if g == 3:
                        softmax_divide(ch, ba, 0)
                    elif g == 5:
                        ch.behind()
                        for e in range(2):
                            ch.then(dve.tensor_scalar(xres[:, ba, e * L:(e + 1) * L], xres[:, ba, e * L:(e + 1) * L],
                                                      gated_b[:, e:e + 1], None, ALU.add))
                softmax_divide(ch, ba, 1)
                wait(dve, o_ready, ba + 1)
                ch.behind()
                ch.then(dve.scalar_tensor_tensor(xres[:, ba, :], bank[0][:, :], gate[:, 1:2], xres[:, ba, :],
                                                 ALU.mult, ALU.add), x_ready["m1"], ba + 1)

            ch = Chain(dve, dve_z)
            dve.wait_ge(ld_at, 16 * 5)
            ch.then(dve.tensor_scalar(gated_b[:, :], b_out[:, :], gate[:, 1:2], None, ALU.mult))
            turn_b(ch, "m0 last", NB - 1, 0, first=True)
            ch.close()
            with dve.Fori(0, NB - 2) as i:
                ch = Chain(dve, dve_b, i * CHAIN["DVE_B"])
                turn_b(ch, "m1", i, i + 1)
                ch.close(CHAIN["DVE_B"])
            ch = Chain(dve, dve_y)
            turn_b(ch, "m1", NB - 2, NB - 1, ahead=False)
            norm_dev(ch, "m1 last", NB - 1, CB)
            norm_scale(ch, "m1 last", NB - 1)
            route_top(ch, "m1 last", NB - 1)
            route_weights(ch, "m1 last", NB - 1)
            for step_no in range(MOE["m1"]["NP"]):
                expert_step(ch, "m1 last", NB - 1, step_no)
            expert_end(ch, "m1 last", NB - 1)

        @block.tensor
        def _(pe):
            pe.wait_ge(ld_in, 32)
            for q in range(2):
                for e in range(2):
                    pe.matmul(bank[2 * q + e][:, :], w_in[:, e * P:(e + 1) * P], ctx_all[:, 2 * q:2 * q + 2, :],
                              start=True, stop=True).then_inc(xin_ready, 1)
            for q in range(2):
                pe.wait_ge(u_ready, 2 * q + 2)
                pe.wait_ge(ld_front, 16 * N_FRONT)
                for e in range(2):
                    last = pe.matmul(bank[6 + q][0:96 + DR, :], w_x[:, e, :],
                                     u_all[:, 2 * q:2 * q + 2, e * L:(e + 1) * L], start=(e == 0), stop=(e == 1))
                last.then_inc(x_proj_ready, 1)
                pe.wait_ge(dtlo_copied, q + 1)
                for e in range(2):
                    pe.matmul(bank[2 * q + e][:, :], w_dt[:, e * P:(e + 1) * P], dt_lo[:, 512 * q:512 * q + 512],
                              start=True, stop=True).then_inc(dt_ready, 1)

            def mixer_spread(b, g):
                for which, (to, free) in enumerate(((bank[0], dbu_done), (bank[1], hc_ready))):
                    wait(pe, free, GROUPS * b + g)
                    for j in range(2):
                        last = pe.matmul(to[:, j * L:(j + 1) * L], pick_state[:, which * NS + 2 * g + j, :],
                                         bc3[:, bass.ds(b * L, L)], start=True, stop=True)
                    last.then_inc(c_ready if which else b_ready, 1)

            def norm_mean(k, b, to):
                wait(pe, x_ready[k], b + 1)
                for e in range(2):
                    last = pe.matmul(to[:, 0:L], mean_w[:, :], xres[:, b, e * L:(e + 1) * L],
                                     start=(e == 0), stop=(e == 1))
                last.then_inc(norm[k]["mean_ready"], 1)

            def norm_var(k, b, to):
                sq = NORM[k][1]
                wait(pe, norm[k]["sq_ready"], b + 1)
                for e in range(2):
                    last = pe.matmul(to[:, L:2 * L], mean_w[:, :], sq[:, e * L:(e + 1) * L],
                                     start=(e == 0), stop=(e == 1))
                last.then_inc(norm[k]["var_ready"], 1)

            def route(k, b):
                m = MOE[k]
                wait(pe, norm[k]["xn_ready"], b + 1)
                for t in range(2):
                    for e in range(2):
                        last = pe.matmul(CB[:, 16 * t:16 * t + m["nr"]], xn[:, e, t * P:(t + 1) * P],
                                         m["route"][:, e, 0:m["nr"]], start=(e == 0), stop=(e == 1))
                last.then_inc(moe[k]["logits_ready"], 1)

            def route_turn(k, b):
                wait(pe, moe[k]["cm_ready"], b + 1)
                for t in range(2):
                    last = pe.matmul(CB[0:96, L + t * P:L + (t + 1) * P],
                                     cm3[:, t, :, :].rearrange("p s c -> p (s c)"), ident_b[:, :],
                                     start=True, stop=True)
                last.then_inc(moe[k]["cmt_ready"], 1)

            def expert_up(k, b, p):
                m, s = MOE[k], moe[k]
                banks = m["banks"][p]
                before = bank_before(k, p)
                if before is not None:
                    wait(pe, s["h1_ready"], m["NP"] * b + before + 1)
                for j in range(min(2, m["T"] - 2 * p)):
                    for which in range(2):
                        for e in range(2):
                            last = pe.matmul(bank[banks[which]][:, j * L:(j + 1) * L],
                                             m["gu"][:, 2 * p + j, e, which, :], xn[:, e, :],
                                             start=(e == 0), stop=(e == 1))
                last.then_inc(s["gu_ready"], 1)

            def expert_weight(k, b, p):
                m, s = MOE[k], moe[k]
                if p == 0:
                    wait(pe, s["cmt_copied"], b + 1)
                else:
                    wait(pe, s["cb_copied"], m["NP"] * b + p)
                for j in range(min(2, m["T"] - 2 * p)):
                    last = pe.matmul(CB[:, j * L:(j + 1) * L], m["pick"][:, 2 * p + j, :], cmt[:, :],
                                     start=True, stop=True)
                last.then_inc(s["cb_ready"], 1)

            def expert_down(k, b, p):
                m, s = MOE[k], moe[k]
                wait(pe, s["h_ready"], m["NP"] * b + p + 1)
                for j in range(min(2, m["T"] - 2 * p)):
                    t = 2 * p + j
                    for e in range(2):
                        last = pe.matmul(Y[:, e * L:(e + 1) * L], m["down"][:, t, e * P:(e + 1) * P],
                                         hh[:, p % 3, j, :], start=(t == 0 and e == 0),
                                         stop=(t == m["T"] - 1), skip_group_check=True)
                last.then_inc(s["h_used"], 1)

            def expert_step(k, b, step_no, what=None):
                NP = MOE[k]["NP"]
                if step_no < NP and what != "rest":
                    expert_up(k, b, step_no)
                if what == "up":
                    return
                if step_no == 1:
                    route_turn(k, b)
                if 1 <= step_no <= NP:
                    expert_weight(k, b, step_no - 1)
                if step_no >= 2:
                    expert_down(k, b, step_no - 2)

            def turn_a(i):
                NP = MOE["m0"]["NP"]
                mixer_spread(i + 1, 0)
                expert_up("m0", i, 0)
                for slot in range(NP + 2):
                    if slot + 1 < NP:
                        expert_up("m0", i, slot + 1)
                    if slot + 1 < GROUPS:
                        mixer_spread(i + 1, slot + 1)
                    if slot == 1:
                        route_turn("m0", i)
                    if 1 <= slot <= NP:
                        expert_weight("m0", i, slot - 1)
                    if slot >= 2:
                        expert_down("m0", i, slot - 2)
                    if slot == NP - 1:
                        norm_mean("m0", i + 1, bank[0])
                    elif slot == NP:
                        norm_var("m0", i + 1, bank[0])
                route("m0", i + 1)

            pe.wait_ge(bc3_ready, 1)
            pe.wait_ge(w_ready, 1)
            pe.wait_ge(ld_x, 32)
            for g in range(GROUPS):
                mixer_spread(0, g)
            pe.wait_ge(bc3_ready, 2)
            pe.wait_ge(memset_done, 9)
            pe.wait_ge(ld_m0, 16 * 6)
            norm_mean("m0", 0, bank[0])
            norm_var("m0", 0, bank[0])
            route("m0", 0)
            with pe.Fori(0, NB - 1) as i:
                turn_a(i)

            def front_step(b, n, first):
                norm_bank, for_q, for_k = FRONT_BANKS[first]
                if n == 0:
                    norm_mean("at", b, norm_bank)
                elif n == 1:
                    norm_var("at", b, norm_bank)
                elif n == 2:
                    wait(pe, norm["at"]["xn_ready"], b + 1)
                    for m in range(2):
                        for e in range(2):
                            last = pe.matmul(for_q[:, m * L:(m + 1) * L], w_q[:, e, m * P:(m + 1) * P],
                                             at_xn[:, e, :], start=(e == 0), stop=(e == 1))
                    last.then_inc(qk_ready, 1)
                else:
                    wait(pe, ctx_copied, b + 1)
                    for m in range(2):
                        last = pe.matmul(for_k[:, m * L:(m + 1) * L], w_k[:, m * P:(m + 1) * P], ctx_b[:, :],
                                         start=True, stop=True)
                    last.then_inc(qk_ready, 1)

            def values_product(b):
                if not isinstance(b, int) or b > 0:
                    wait(pe, exp_done, NH * b)
                for t in range(2):
                    last = pe.matmul(bank[1][:, t * L:(t + 1) * L], ctx_b[:, t * P:(t + 1) * P], w_v[:, :],
                                     start=True, stop=True)
                last.then_inc(v_ready, 1)

            def turn_b(k, bm, ba, first=False, ahead=True):
                def experts(stage):
                    for step_no in STEPS[k].get(stage, ()):
                        expert_step(k, bm, step_no)

                if first:
                    front_step(0, 0, True)
                    expert_step(k, bm, 0)
                    front_step(0, 1, True)
                    expert_step(k, bm, 1)
                    front_step(0, 2, True)
                    front_step(0, 3, True)
                    expert_step(k, bm, 2)
                    wait(pe, rope_read, 2)
                    values_product(0)
                else:
                    norm_mean(k, bm, CB)
                experts("stacks")
                wait(pe, v_copied, ba + 1)
                for h in range(NH):
                    if h % (NH // 2) == 0:
                        wait(pe, stacks_ready[h // (NH // 2)], 16 * 18 * (ba + 1))
                    if h == 2 and first:
                        wait(pe, moe[k]["h1_ready"], MOE[k]["NP"] * bm + 4)
                    if h >= 4:
                        wait(pe, max_done, NH * ba + h - 3)
                    for t in range(2):
                        last = pe.matmul(bank[h % 4][:, t * L:(t + 1) * L],
                                         q_stack[0:STACK, h, t * P:(t + 1) * P],
                                         k_stack[0:STACK, h, :], start=True, stop=True)
                    last.then_inc(s1_ready, 1)
                    if not first and h == NORM_AT["pe_var"]:
                        norm_var(k, bm, CB)
                    if not first and h == NORM_AT["pe_route"]:
                        route(k, bm)
                    for n, what in PIECES[k].get(h, ()):
                        expert_step(k, bm, n, what)
                wait(pe, mp_ready, ba + 1)
                for t in range(2):
                    last = pe.matmul(bank[2][0:96, t * P:(t + 1) * P], mp[:, t, :, :].rearrange("p s h -> p (s h)"),
                                     ident_b[:, :], start=True, stop=True)
                last.then_inc(mt_ready, 1)
                for n, step_no in enumerate(STEPS[k]["rows"]):
                    if ahead:
                        front_step(ba + 1, n, False)
                    expert_step(k, bm, step_no, "rest")
                wait(pe, rows_ready, 48 * (ba + 1))

                def values(g, piece):
                    half, r, kt, part = g // 4, g % 4, piece // 2, piece % 2
                    if piece == 0:
                        wait(pe, exp_done, NH * ba + 4 * g + 4)
                    for s in range(4):
                        w = ones_pad[:, r, :] if part else v_pad[:, kt, 16 * half + 4 * s + r, :]
                        last = pe.matmul(bank[2 + half][32 * s:32 * s + 32, part * L:(part + 1) * L],
                                         w, p_exp[:, g % 2, s, kt, :], start=(r == 0 and piece == 0),
                                         stop=(r == 3 and kt == 1), skip_group_check=True)
                        if g in (2, 6) and piece == 3 and s == 0:
                            last.then_inc(stacks_used[g // 4], 1)
                    if piece == 3:
                        last.then_inc(pv_done, 1)

                for g in range(8):
                    half, r = g // 4, g % 4
                    for s in range(4):
                        n, h = 4 * g + s, 16 * half + 4 * s + r
                        if n >= 2:
                            wait(pe, exp_done, NH * ba + n - 1)
                        for kt in range(2):
                            last = pe.matmul(bank[n % 2][:, kt * L:(kt + 1) * L],
                                             k_stack[0:STACK + 3, h, kt * P:(kt + 1) * P],
                                             q_stack[0:STACK + 3, h, :], start=True, stop=True)
                        last.then_inc(s2_ready, 1)
                        if g >= 1:
                            values(g - 1, s)
                    experts(f"group{g}")
                    if ahead and f"group{g}" in FRONT:
                        front_step(ba + 1, FRONT[f"group{g}"], False)
                for piece in range(4):
                    values(7, piece)
                if ahead:
                    values_product(ba + 1)
                for e in range(2):
                    wait(pe, attn_ready, 2 * ba + e + 1)
                    for m in range(2):
                        last = pe.matmul(bank[0][:, m * L:(m + 1) * L], w_out[:, e, m * P:(m + 1) * P],
                                         attn[:, e, :], start=(e == 0 and m == 0), stop=(e == 1),
                                         skip_group_check=True)
                last.then_inc(o_ready, 1)

            pe.wait_ge(ld_at, 16 * 5)
            turn_b("m0 last", NB - 1, 0, first=True)
            pe.wait_ge(ld_m1, 16 * 4)
            with pe.Fori(0, NB - 2) as i:
                turn_b("m1", i, i + 1)
            turn_b("m1", NB - 2, NB - 1, ahead=False)
            norm_mean("m1 last", NB - 1, CB)
            norm_var("m1 last", NB - 1, CB)
            wait(pe, norm["m1 last"]["xn_ready"], NB)
            for step_no in range(MOE["m1"]["NP"] + 2):
                if step_no == 1:
                    route("m1 last", NB - 1)
                expert_step("m1 last", NB - 1, step_no)


def _lay_out(np, i):
    bf = np.dtype("bfloat16")

    def halves(a):
        return a.reshape(2, P, -1).transpose(1, 0, 2)

    def feature_rows(blocks, tiles):
        rows = np.concatenate(blocks, 0)
        full = np.zeros((tiles * P, rows.shape[1]), rows.dtype)
        full[:rows.shape[0]] = rows
        return full

    def gate_up(gate, up, tiles):
        both = np.stack([feature_rows(gate, tiles), feature_rows(up, tiles)])
        return both.reshape(2, tiles, P, 2, P).transpose(4, 1, 3, 0, 2)

    def down(blocks, tiles):
        return feature_rows(blocks, tiles).reshape(tiles, P, D).transpose(1, 0, 2)

    def expert_pick(tiles, shared):
        pick = np.zeros((96, tiles, P), bf)
        for f in range(tiles * P):
            j = f // FE if f < E * FE else E
            for s in range(3):
                pick[32 * s + j, f // P, f % P] = 1
        return pick

    x, c = i["x"], i["ctx_1024"]
    w_x = i["L0_xattn_x_proj_w"]
    gu = i["L0_ffn_gate_up_proj"]
    g1, u1 = i["L1_ffn_gate_proj"], i["L1_ffn_up_proj"]
    turned = np.arange(D).reshape(P, 2).T.reshape(-1)
    wkv = i["L1_xattn_Wkv"]
    sel_state = np.zeros((96, 2 * NS, P), bf)
    for j in range(2 * NS):
        sel_state[[j, 32 + j, 64 + j], j, :] = 1
    row = np.arange(P)
    columns = np.zeros((P, 8), np.float32)
    columns[:, 0] = EPS
    columns[:, 1] = np.pi / 2
    columns[:, 2] = np.where(row % 2 == 0, 1.0, 0.01)
    columns[:, 3] = 0.5
    columns[:, 4] = 1.0
    return dict(
        x_t=x.transpose(2, 0, 1).reshape(2, P, NB, L).transpose(1, 2, 0, 3).reshape(P, NB, 2 * L),
        x_rows=x.reshape(NB, 2, P, D).transpose(2, 0, 1, 3),
        ctx_t=c.transpose(2, 0, 1),
        pos=i["fside_BxSx2_0"].transpose(2, 0, 1)[row % 4 // 2],
        gates=np.broadcast_to(np.concatenate([i["g_xattn"], i["g_ffn"]]), (P, 4)),
        in_proj=i["L0_xattn_in_proj_w"].T,
        conv_w=halves(i["L0_xattn_conv_w"]),
        conv_b=i["L0_xattn_conv_b"].reshape(2, P).T,
        x_proj=halves(np.concatenate([w_x[DR:]] * 3 + [w_x[:DR]]).T),
        dt_proj=i["L0_xattn_dt_proj_w"].T,
        dt_b=i["L0_xattn_dt_proj_b"].reshape(2, P).T,
        a_log=halves(i["L0_xattn_A_log"]),
        d_skip=i["L0_xattn_D"].reshape(2, P).T,
        gu0=gate_up([gu[:, :FE].reshape(-1, D), i["L0_ffn_sh_gate_w"]],
                    [gu[:, FE:].reshape(-1, D), i["L0_ffn_sh_up_w"]], T0),
        down0=down([i["L0_ffn_down_proj"].transpose(0, 2, 1).reshape(-1, D), i["L0_ffn_sh_down_w"].T], T0),
        route0=halves(np.concatenate([i["L0_ffn_router_weight"], i["L0_ffn_shared_gate_w"]]).T),
        gu1=gate_up([g1.reshape(-1, D)], [u1.reshape(-1, D)], T1),
        down1=down([i["L1_ffn_down_proj"].transpose(0, 2, 1).reshape(-1, D)], T1),
        route1=halves(i["L1_ffn_gate_w"].T),
        wq=halves(i["L1_xattn_Wq"][:, turned]),
        wk=wkv[:, turned],
        wv=wkv[:, D:],
        wout=halves(i["L1_xattn_Wout"]),
        bout=i["L1_xattn_bout"].reshape(2, P).T,
        sel_state=sel_state,
        sel0=expert_pick(T0, True),
        sel1=expert_pick(T1, False),
        ident=np.eye(P, dtype=bf),
        columns=columns,
        iota8=np.broadcast_to(np.arange(E, dtype=np.float32), (P, E)),
    )


def kernel(**inputs):
    import numpy as np
    import concourse.bacc as bacc
    from concourse.bass_utils import run_bass_kernel_spmd

    laid = _lay_out(np, {k: np.asarray(v) for k, v in inputs.items()})
    nc = bacc.Bacc("TRN2", target_bir_lowering=False, num_devices=1)
    arrays, handles = {}, {}
    for name, a in laid.items():
        a = np.ascontiguousarray(a)
        arrays["in_" + name] = a
        handles[name] = nc.dram_tensor("in_" + name, a.shape, mybir.dt.from_np(a.dtype), kind="ExternalInput").ap()
    out = nc.dram_tensor("out_0", (P, NB, 2 * L), F32, kind="ExternalOutput").ap()
    program(nc, out=out, **handles)
    got = run_bass_kernel_spmd(nc, [arrays], core_ids=[0]).results[0]["out_0"]
    return np.ascontiguousarray(got.reshape(P, NB, 2, L).transpose(1, 3, 2, 0).reshape(NB, L, D))
```
